# Optimizing a Trainium2 kernel written in Bass

```python
import numpy as np
import jax
import jax.numpy as jnp

def _softmax(x, axis=-1):
    return jax.nn.softmax(x, axis=axis)

def _gelu(x):
    return jax.nn.gelu(x, approximate=True)

def _silu(x):
    return jax.nn.silu(x)

def _sigmoid(x):
    return jax.nn.sigmoid(x)

def _layernorm(x, axis=-1, eps=1e-05):
    m = jnp.mean(x, axis=axis, keepdims=True)
    v = jnp.var(x, axis=axis, keepdims=True)
    return (x - m) / jnp.sqrt(v + eps)

def _scatter_add(tgt, idx, src, axis=0):
    return tgt.at[idx].add(src)

def _segment_sum(src, seg, n):
    return jax.ops.segment_sum(src, seg, n)
kernel_name = 'mk_gps_d2_gnn_r8_9d24fa'

def setup_inputs(seed: int=0):
    np.random.seed(seed)
    _w = jnp.asarray

    def _rec_inputs():
        import jax
        import jax.numpy as jnp
        _gk = jax.random.key(seed)
        x = -0.0003713 + 1 * jax.random.normal(jax.random.fold_in(_gk, 1), (6250, 256), jnp.float32)
        src = jax.random.randint(jax.random.fold_in(_gk, 2), (200000,), 0, 6250, jnp.int32)
        dst = jax.random.randint(jax.random.fold_in(_gk, 3), (200000,), 0, 6250, jnp.int32)
        _o = jnp.argsort(dst, stable=True)
        src = src[_o]
        dst = dst[_o]
        edge_weight = jax.random.uniform(jax.random.fold_in(_gk, 13), (200000,), jnp.float32, 0.0, 0.999998)
        node_vec = jax.random.uniform(jax.random.fold_in(_gk, 14), (6250,), jnp.float32, 0.0, 0.999833)
        return (x, src, dst, edge_weight, node_vec)
    x, src, dst, edge_weight, node_vec = _rec_inputs()

    def _L0_gnn_setup():
        import jax, jax.numpy as jnp
        import numpy as np
        N, E = (6250, 100000)
        D_IN, D_OUT, H = (256, 64, 4)
        NEG_SLOPE = 0.01

        def _segment_softmax(z, seg, n):
            m = jax.ops.segment_max(z, seg, num_segments=n)
            ez = jnp.exp(z - m[seg])
            denom = jax.ops.segment_sum(ez, seg, num_segments=n)
            return ez / jnp.maximum(denom[seg], 1e-09)
        key = jax.random.key(seed)
        ks = jax.random.split(key, 7)
        s = 0.1
        return {'features': jax.random.normal(ks[0], (N, D_IN), jnp.float32), 'src': jax.random.randint(ks[1], (E,), 0, N), 'dst': jax.random.randint(ks[2], (E,), 0, N), 'W_fc': jax.random.normal(ks[3], (H, D_IN, D_OUT), jnp.float32) * s, 'W_al': jax.random.normal(ks[4], (H, D_OUT, 1), jnp.float32) * s, 'W_ar': jax.random.normal(ks[5], (H, D_OUT, 1), jnp.float32) * s, 'W_res': jax.random.normal(ks[6], (H, D_IN, D_OUT), jnp.float32) * s}
    _L0_gnn_all = _L0_gnn_setup()
    _L0_gnn_in = {k: v for k, v in _L0_gnn_all.items() if k in ('W_fc', 'W_al', 'W_ar', 'W_res')}
    del _L0_gnn_all

    def _L0_mix_setup():
        import jax, jax.numpy as jnp
        import numpy as np
        NHEAD = 8
        ATT_EPS = 1e-06
        LN_EPS = 1e-05

        def _layernorm(x, g, b):
            mu = jnp.mean(x, axis=-1, keepdims=True)
            var = jnp.mean(jnp.square(x - mu), axis=-1, keepdims=True)
            return (x - mu) * jax.lax.rsqrt(var + LN_EPS) * g + b
        key = jax.random.key(seed)
        ks = jax.random.split(key, 7)
        N, L, C = (4, 2048, 256)
        s = 1.0 / np.sqrt(C)
        return {'x': jax.random.normal(ks[0], (N, L, C), jnp.float32), 'Wq': jax.random.normal(ks[1], (C, C), jnp.float32) * s, 'Wk': jax.random.normal(ks[2], (C, C), jnp.float32) * s, 'Wv': jax.random.normal(ks[3], (C, C), jnp.float32) * s, 'Wm': jax.random.normal(ks[4], (C, C), jnp.float32) * s, 'W1': jax.random.normal(ks[5], (2 * C, 2 * C), jnp.float32) * (1.0 / np.sqrt(2 * C)), 'W2': jax.random.normal(ks[6], (2 * C, C), jnp.float32) * (1.0 / np.sqrt(2 * C)), 'g1': jnp.ones((C,), jnp.float32), 'b1': jnp.zeros((C,), jnp.float32), 'g2': jnp.ones((C,), jnp.float32), 'b2': jnp.zeros((C,), jnp.float32)}
    _L0_mix_all = _L0_mix_setup()
    _L0_mix_in = {k: v for k, v in _L0_mix_all.items() if k in ('Wq', 'Wk', 'Wv', 'Wm', 'W1', 'W2', 'g1', 'b1', 'g2', 'b2')}
    del _L0_mix_all

    def _L0_ffn_setup():
        import jax, jax.numpy as jnp
        import numpy as np
        B, A = (512, 8)
        IN, OUT = (256, 256)
        SH1, SH2 = (256, 128)
        EH1, EH2 = (128, 64)
        E, TOPK = (4, 2)

        def _shared_mlp(x, W1, b1, W2, b2, W3, b3):
            h = jax.nn.relu(x @ W1 + b1)
            h = jax.nn.relu(h @ W2 + b2)
            return h @ W3 + b3

        def _experts_mlp(x, eW1, eb1, eW2, eb2, eW3, eb3):
            h = jax.nn.relu(jnp.einsum('baf,efh->ebah', x, eW1) + eb1[:, None, None, :])
            h = jax.nn.relu(jnp.einsum('ebah,ehg->ebag', h, eW2) + eb2[:, None, None, :])
            o = jnp.einsum('ebag,ego->ebao', h, eW3) + eb3[:, None, None, :]
            return jnp.moveaxis(o, 0, -1)
        key = jax.random.key(seed)
        ks = jax.random.split(key, 16)
        s = 0.05
        return {'x': jax.random.normal(ks[0], (B, A, IN), jnp.float32), 'sW1': jax.random.normal(ks[1], (IN, SH1), jnp.float32) * s, 'sb1': jnp.zeros((SH1,), jnp.float32), 'sW2': jax.random.normal(ks[2], (SH1, SH2), jnp.float32) * s, 'sb2': jnp.zeros((SH2,), jnp.float32), 'sW3': jax.random.normal(ks[3], (SH2, OUT), jnp.float32) * s, 'sb3': jnp.zeros((OUT,), jnp.float32), 'eW1': jax.random.normal(ks[4], (E, IN, EH1), jnp.float32) * s, 'eb1': jnp.zeros((E, EH1), jnp.float32), 'eW2': jax.random.normal(ks[5], (E, EH1, EH2), jnp.float32) * s, 'eb2': jnp.zeros((E, EH2), jnp.float32), 'eW3': jax.random.normal(ks[6], (E, EH2, OUT), jnp.float32) * s, 'eb3': jnp.zeros((E, OUT), jnp.float32), 'gW': jax.random.normal(ks[7], (IN, E), jnp.float32) * s, 'gb': jnp.zeros((E,), jnp.float32)}
    _L0_ffn_all = _L0_ffn_setup()
    _L0_ffn_in = {k: v for k, v in _L0_ffn_all.items() if k in ('sW1', 'sb1', 'sW2', 'sb2', 'sW3', 'sb3', 'eW1', 'eb1', 'eW2', 'eb2', 'eW3', 'eb3', 'gW', 'gb')}
    del _L0_ffn_all

    def _L1_gnn_setup():
        import jax, jax.numpy as jnp
        import numpy as np
        from jax import lax
        N, E, D = (1024, 32768, 256)
        NH, FOUT = (4, 64)
        D_STATE, D_CONV, DT_RANK = (16, 4, 16)

        def _layer_norm(x, g, b, eps=1e-05):
            mu = jnp.mean(x, -1, keepdims=True)
            var = jnp.var(x, -1, keepdims=True)
            return (x - mu) * lax.rsqrt(var + eps) * g + b

        def _mamba(xs, in_proj_w, conv_w, conv_b, x_proj_w, dt_proj_w, dt_proj_b, A_log, D_param, out_proj_w):
            n = xs.shape[0]
            xz = xs @ in_proj_w.T
            xc, z = jnp.split(xz, 2, axis=-1)
            K = conv_w.shape[1]
            xp = jnp.pad(xc, ((K - 1, 0), (0, 0)))
            xc = sum((xp[k:k + n] * conv_w[:, k] for k in range(K))) + conv_b
            xc = jax.nn.silu(xc)
            dbc = xc @ x_proj_w.T
            dt = jax.nn.softplus(dbc[:, :DT_RANK] @ dt_proj_w.T + dt_proj_b)
            Bm = dbc[:, DT_RANK:DT_RANK + D_STATE]
            Cm = dbc[:, DT_RANK + D_STATE:]
            A = -jnp.exp(A_log)
            dA = jnp.exp(dt[:, :, None] * A)
            dBx = (dt * xc)[:, :, None] * Bm[:, None, :]

            def step(h, t):
                dA_t, dBx_t, C_t = t
                h = dA_t * h + dBx_t
                return (h, h @ C_t)
            _, y = lax.scan(step, jnp.zeros((xc.shape[1], D_STATE), xs.dtype), (dA, dBx, Cm))
            y = y + xc * D_param
            y = y * jax.nn.silu(z)
            return y @ out_proj_w.T

        def _forward(x, edge_index, deg_noise, gat_w, gat_a_src, gat_a_tgt, gat_b, ln_local_g, ln_local_b, ln_global_g, ln_global_b, ln2_g, ln2_b, in_proj_w, conv_w, conv_b, x_proj_w, dt_proj_w, dt_proj_b, A_log, D_param, out_proj_w, wl, wg, ff1_w, ff1_b, ff2_w, ff2_b):
            n = x.shape[0]
            src, tgt = (edge_index[0], edge_index[1])
            proj = (x @ gat_w.T).reshape(n, NH, FOUT)
            s_src = jnp.sum(proj * gat_a_src, -1)
            s_tgt = jnp.sum(proj * gat_a_tgt, -1)
            e = jax.nn.leaky_relu(s_src[src] + s_tgt[tgt], 0.2)
            exp_e = jnp.exp(e - jnp.max(e))
            denom = jax.ops.segment_sum(exp_e, tgt, num_segments=n)
            attn = exp_e / (denom[tgt] + 1e-16)
            agg = jax.ops.segment_sum(proj[src] * attn[:, :, None], tgt, num_segments=n)
            h_local = jax.nn.elu((agg + x.reshape(n, NH, FOUT)).reshape(n, NH * FOUT) + gat_b)
            h_local = _layer_norm(h_local, ln_local_g, ln_local_b)
            deg = jax.ops.segment_sum(jnp.ones((src.shape[0],), x.dtype), src, num_segments=n)
            perm = jnp.argsort(deg + deg_noise, stable=True)
            inv = jnp.argsort(perm)
            y = _mamba(x[perm], in_proj_w, conv_w, conv_b, x_proj_w, dt_proj_w, dt_proj_b, A_log, D_param, out_proj_w)
            h_attn = _layer_norm(x + y[inv], ln_global_g, ln_global_b)
            gate = jax.nn.sigmoid(h_local @ wl.T + h_attn @ wg.T)
            h = gate * h_local + (1.0 - gate) * h_attn
            ff = jax.nn.relu(h @ ff1_w.T + ff1_b) @ ff2_w.T + ff2_b
            return _layer_norm(h + ff, ln2_g, ln2_b)
        key = jax.random.key(seed)
        ks = jax.random.split(key, 24)
        w = lambda i, shape, s=0.05: jax.random.normal(ks[i], shape, dtype=jnp.float32) * s
        return {'x': jax.random.normal(ks[0], (N, D), dtype=jnp.float32), 'edge_index': jax.random.randint(ks[1], (2, E), 0, N, dtype=jnp.int32), 'edge_prob': jax.random.uniform(ks[2], (E,), dtype=jnp.float32), 'deg_noise': jax.random.uniform(ks[3], (N,), dtype=jnp.float32), 'gat_w': w(4, (NH * FOUT, D)), 'gat_a_src': w(5, (NH, FOUT)), 'gat_a_tgt': w(6, (NH, FOUT)), 'gat_b': jnp.zeros((NH * FOUT,), jnp.float32), 'ln_local_g': jnp.ones((D,), jnp.float32), 'ln_local_b': jnp.zeros((D,), jnp.float32), 'ln_global_g': jnp.ones((D,), jnp.float32), 'ln_global_b': jnp.zeros((D,), jnp.float32), 'ln2_g': jnp.ones((D,), jnp.float32), 'ln2_b': jnp.zeros((D,), jnp.float32), 'in_proj_w': w(7, (2 * D, D)), 'conv_w': w(8, (D, D_CONV), 0.2), 'conv_b': jnp.zeros((D,), jnp.float32), 'x_proj_w': w(9, (DT_RANK + 2 * D_STATE, D)), 'dt_proj_w': w(10, (D, DT_RANK)), 'dt_proj_b': w(11, (D,), 0.1) - 4.0, 'A_log': jnp.log(jnp.tile(jnp.arange(1, D_STATE + 1, dtype=jnp.float32), (D, 1))), 'D_param': jnp.ones((D,), jnp.float32), 'out_proj_w': w(12, (D, D)), 'wl': w(13, (D, D)), 'wg': w(14, (D, D)), 'ff1_w': w(15, (2 * D, D)), 'ff1_b': jnp.zeros((2 * D,), jnp.float32), 'ff2_w': w(16, (D, 2 * D)), 'ff2_b': jnp.zeros((D,), jnp.float32)}
    _L1_gnn_all = _L1_gnn_setup()
    _L1_gnn_in = {k: v for k, v in _L1_gnn_all.items() if k in ('gat_w', 'gat_a_src', 'gat_a_tgt', 'gat_b', 'ln_local_g', 'ln_local_b', 'ln_global_g', 'ln_global_b', 'ln2_g', 'ln2_b', 'in_proj_w', 'conv_w', 'conv_b', 'x_proj_w', 'dt_proj_w', 'dt_proj_b', 'A_log', 'D_param', 'out_proj_w', 'wl', 'wg', 'ff1_w', 'ff1_b', 'ff2_w', 'ff2_b')}
    del _L1_gnn_all

    def _L1_mix_setup():
        import jax, jax.numpy as jnp
        import numpy as np
        BN_EPS = 1e-05
        key = jax.random.key(seed)
        ks = jax.random.split(key, 4)
        B, N, D = (8, 1024, 256)
        outD = 256
        s = 1.0 / np.sqrt(D)
        return {'feature': jax.random.normal(ks[0], (B, N, D), dtype=jnp.float32), 'W_qk': jax.random.normal(ks[1], (2, D, D), dtype=jnp.float32) * s, 'b_qk': jnp.zeros((2, D), dtype=jnp.float32), 'W_v': jax.random.normal(ks[2], (D, outD), dtype=jnp.float32) * s, 'b_v': jnp.zeros((outD,), dtype=jnp.float32), 'gamma': jnp.ones((D,), dtype=jnp.float32), 'beta': jnp.zeros((D,), dtype=jnp.float32)}
    _L1_mix_all = _L1_mix_setup()
    _L1_mix_in = {k: v for k, v in _L1_mix_all.items() if k in ('W_qk', 'b_qk', 'W_v', 'b_v', 'gamma', 'beta')}
    del _L1_mix_all

    def _L1_ffn_setup():
        import jax, jax.numpy as jnp
        import numpy as np
        B, S, D, E, H, K = (4, 512, 256, 8, 512, 2)
        key = jax.random.key(seed)
        ks = jax.random.split(key, 6)
        x = jax.random.normal(ks[0], (B, S, D), jnp.float32)
        Wg = jax.random.normal(ks[1], (D, E), jnp.float32) * 0.02
        bg = jnp.zeros((E,), jnp.float32)
        W1 = jax.random.normal(ks[2], (E, D, H), jnp.float32) * 0.02
        b1 = jnp.zeros((E, H), jnp.float32)
        W2 = jax.random.normal(ks[3], (E, H, D), jnp.float32) * 0.02
        b2 = jnp.zeros((E, D), jnp.float32)
        return {'x': x, 'Wg': Wg, 'bg': bg, 'W1': W1, 'b1': b1, 'W2': W2, 'b2': b2}
    _L1_ffn_all = _L1_ffn_setup()
    _L1_ffn_in = {k: v for k, v in _L1_ffn_all.items() if k in ('Wg', 'bg', 'W1', 'b1', 'W2', 'b2')}
    del _L1_ffn_all
    return {'x': x, 'src': src, 'dst': dst, 'edge_weight': edge_weight, 'node_vec': node_vec, 'L0_gnn_W_fc': _L0_gnn_in['W_fc'], 'L0_gnn_W_al': _L0_gnn_in['W_al'], 'L0_gnn_W_ar': _L0_gnn_in['W_ar'], 'L0_gnn_W_res': _L0_gnn_in['W_res'], 'L0_mix_Wq': _L0_mix_in['Wq'], 'L0_mix_Wk': _L0_mix_in['Wk'], 'L0_mix_Wv': _L0_mix_in['Wv'], 'L0_mix_Wm': _L0_mix_in['Wm'], 'L0_mix_W1': _L0_mix_in['W1'], 'L0_mix_W2': _L0_mix_in['W2'], 'L0_mix_g1': _L0_mix_in['g1'], 'L0_mix_b1': _L0_mix_in['b1'], 'L0_mix_g2': _L0_mix_in['g2'], 'L0_mix_b2': _L0_mix_in['b2'], 'L0_ffn_sW1': _L0_ffn_in['sW1'], 'L0_ffn_sb1': _L0_ffn_in['sb1'], 'L0_ffn_sW2': _L0_ffn_in['sW2'], 'L0_ffn_sb2': _L0_ffn_in['sb2'], 'L0_ffn_sW3': _L0_ffn_in['sW3'], 'L0_ffn_sb3': _L0_ffn_in['sb3'], 'L0_ffn_eW1': _L0_ffn_in['eW1'], 'L0_ffn_eb1': _L0_ffn_in['eb1'], 'L0_ffn_eW2': _L0_ffn_in['eW2'], 'L0_ffn_eb2': _L0_ffn_in['eb2'], 'L0_ffn_eW3': _L0_ffn_in['eW3'], 'L0_ffn_eb3': _L0_ffn_in['eb3'], 'L0_ffn_gW': _L0_ffn_in['gW'], 'L0_ffn_gb': _L0_ffn_in['gb'], 'L1_gnn_gat_w': _L1_gnn_in['gat_w'], 'L1_gnn_gat_a_src': _L1_gnn_in['gat_a_src'], 'L1_gnn_gat_a_tgt': _L1_gnn_in['gat_a_tgt'], 'L1_gnn_gat_b': _L1_gnn_in['gat_b'], 'L1_gnn_ln_local_g': _L1_gnn_in['ln_local_g'], 'L1_gnn_ln_local_b': _L1_gnn_in['ln_local_b'], 'L1_gnn_ln_global_g': _L1_gnn_in['ln_global_g'], 'L1_gnn_ln_global_b': _L1_gnn_in['ln_global_b'], 'L1_gnn_ln2_g': _L1_gnn_in['ln2_g'], 'L1_gnn_ln2_b': _L1_gnn_in['ln2_b'], 'L1_gnn_in_proj_w': _L1_gnn_in['in_proj_w'], 'L1_gnn_conv_w': _L1_gnn_in['conv_w'], 'L1_gnn_conv_b': _L1_gnn_in['conv_b'], 'L1_gnn_x_proj_w': _L1_gnn_in['x_proj_w'], 'L1_gnn_dt_proj_w': _L1_gnn_in['dt_proj_w'], 'L1_gnn_dt_proj_b': _L1_gnn_in['dt_proj_b'], 'L1_gnn_A_log': _L1_gnn_in['A_log'], 'L1_gnn_D_param': _L1_gnn_in['D_param'], 'L1_gnn_out_proj_w': _L1_gnn_in['out_proj_w'], 'L1_gnn_wl': _L1_gnn_in['wl'], 'L1_gnn_wg': _L1_gnn_in['wg'], 'L1_gnn_ff1_w': _L1_gnn_in['ff1_w'], 'L1_gnn_ff1_b': _L1_gnn_in['ff1_b'], 'L1_gnn_ff2_w': _L1_gnn_in['ff2_w'], 'L1_gnn_ff2_b': _L1_gnn_in['ff2_b'], 'L1_mix_W_qk': _L1_mix_in['W_qk'], 'L1_mix_b_qk': _L1_mix_in['b_qk'], 'L1_mix_W_v': _L1_mix_in['W_v'], 'L1_mix_b_v': _L1_mix_in['b_v'], 'L1_mix_gamma': _L1_mix_in['gamma'], 'L1_mix_beta': _L1_mix_in['beta'], 'L1_ffn_Wg': _L1_ffn_in['Wg'], 'L1_ffn_bg': _L1_ffn_in['bg'], 'L1_ffn_W1': _L1_ffn_in['W1'], 'L1_ffn_b1': _L1_ffn_in['b1'], 'L1_ffn_W2': _L1_ffn_in['W2'], 'L1_ffn_b2': _L1_ffn_in['b2']}

def reference(x, src, dst, edge_weight, node_vec, L0_gnn_W_fc, L0_gnn_W_al, L0_gnn_W_ar, L0_gnn_W_res, L0_mix_Wq, L0_mix_Wk, L0_mix_Wv, L0_mix_Wm, L0_mix_W1, L0_mix_W2, L0_mix_g1, L0_mix_b1, L0_mix_g2, L0_mix_b2, L0_ffn_sW1, L0_ffn_sb1, L0_ffn_sW2, L0_ffn_sb2, L0_ffn_sW3, L0_ffn_sb3, L0_ffn_eW1, L0_ffn_eb1, L0_ffn_eW2, L0_ffn_eb2, L0_ffn_eW3, L0_ffn_eb3, L0_ffn_gW, L0_ffn_gb, L1_gnn_gat_w, L1_gnn_gat_a_src, L1_gnn_gat_a_tgt, L1_gnn_gat_b, L1_gnn_ln_local_g, L1_gnn_ln_local_b, L1_gnn_ln_global_g, L1_gnn_ln_global_b, L1_gnn_ln2_g, L1_gnn_ln2_b, L1_gnn_in_proj_w, L1_gnn_conv_w, L1_gnn_conv_b, L1_gnn_x_proj_w, L1_gnn_dt_proj_w, L1_gnn_dt_proj_b, L1_gnn_A_log, L1_gnn_D_param, L1_gnn_out_proj_w, L1_gnn_wl, L1_gnn_wg, L1_gnn_ff1_w, L1_gnn_ff1_b, L1_gnn_ff2_w, L1_gnn_ff2_b, L1_mix_W_qk, L1_mix_b_qk, L1_mix_W_v, L1_mix_b_v, L1_mix_gamma, L1_mix_beta, L1_ffn_Wg, L1_ffn_bg, L1_ffn_W1, L1_ffn_b1, L1_ffn_W2, L1_ffn_b2):
    import jax
    import jax.numpy as jnp

    def _L0_gnn_ref(features, src, dst, W_fc, W_al, W_ar, W_res):
        import jax, jax.numpy as jnp
        import numpy as np
        N, E = (6250, 100000)
        D_IN, D_OUT, H = (256, 64, 4)
        NEG_SLOPE = 0.01

        def _segment_softmax(z, seg, n):
            m = jax.ops.segment_max(z, seg, num_segments=n)
            ez = jnp.exp(z - m[seg])
            denom = jax.ops.segment_sum(ez, seg, num_segments=n)
            return ez / jnp.maximum(denom[seg], 1e-09)
        ft = jnp.einsum('nd,hdo->hno', features, W_fc)
        a1 = jnp.einsum('hno,hoa->hna', ft, W_al)
        a2 = jnp.einsum('hno,hoa->hna', ft, W_ar)

        def head(ft_h, a1_h, a2_h, Wr_h):
            z = jax.nn.leaky_relu(a1_h[dst, 0] + a2_h[src, 0], NEG_SLOPE)
            e = _segment_softmax(z, dst, N)[:, None]
            accum = jax.ops.segment_sum(e * ft_h[src], dst, num_segments=N)
            return jax.nn.relu(accum + features @ Wr_h)
        outs = jax.vmap(head)(ft, a1, a2, W_res)
        return jnp.transpose(outs, (1, 0, 2)).reshape(N, H * D_OUT)

    def _L0_mix_ref(x, Wq, Wk, Wv, Wm, W1, W2, g1, b1, g2, b2):
        import jax, jax.numpy as jnp
        import numpy as np
        NHEAD = 8
        ATT_EPS = 1e-06
        LN_EPS = 1e-05

        def _layernorm(x, g, b):
            mu = jnp.mean(x, axis=-1, keepdims=True)
            var = jnp.mean(jnp.square(x - mu), axis=-1, keepdims=True)
            return (x - mu) * jax.lax.rsqrt(var + LN_EPS) * g + b
        N, L, C = x.shape
        H = NHEAD
        D = C // H
        q = (x @ Wq).reshape(N, L, H, D)
        k = (x @ Wk).reshape(N, L, H, D)
        v = (x @ Wv).reshape(N, L, H, D)
        Q = jax.nn.elu(q) + 1.0
        K = jax.nn.elu(k) + 1.0
        v = v / L
        KV = jnp.einsum('nshd,nshv->nhdv', K, v)
        Z = 1.0 / (jnp.einsum('nlhd,nhd->nlh', Q, K.sum(axis=1)) + ATT_EPS)
        msg = jnp.einsum('nlhd,nhdv,nlh->nlhv', Q, KV, Z) * L
        msg = msg.reshape(N, L, C) @ Wm
        msg = _layernorm(msg, g1, b1)
        h = jnp.concatenate([x, msg], axis=-1) @ W1
        h = jax.nn.relu(h) @ W2
        msg = _layernorm(h, g2, b2)
        return x + msg

    def _L0_ffn_ref(x, sW1, sb1, sW2, sb2, sW3, sb3, eW1, eb1, eW2, eb2, eW3, eb3, gW, gb):
        import jax, jax.numpy as jnp
        import numpy as np
        B, A = (512, 8)
        IN, OUT = (256, 256)
        SH1, SH2 = (256, 128)
        EH1, EH2 = (128, 64)
        E, TOPK = (4, 2)

        def _shared_mlp(x, W1, b1, W2, b2, W3, b3):
            h = jax.nn.relu(x @ W1 + b1)
            h = jax.nn.relu(h @ W2 + b2)
            return h @ W3 + b3

        def _experts_mlp(x, eW1, eb1, eW2, eb2, eW3, eb3):
            h = jax.nn.relu(jnp.einsum('baf,efh->ebah', x, eW1) + eb1[:, None, None, :])
            h = jax.nn.relu(jnp.einsum('ebah,ehg->ebag', h, eW2) + eb2[:, None, None, :])
            o = jnp.einsum('ebag,ego->ebao', h, eW3) + eb3[:, None, None, :]
            return jnp.moveaxis(o, 0, -1)
        all_out = _experts_mlp(x, eW1, eb1, eW2, eb2, eW3, eb3)
        shared = _shared_mlp(x, sW1, sb1, sW2, sb2, sW3, sb3)
        gates = jax.nn.softmax(x @ gW + gb, axis=-1)
        topv, topi = jax.lax.top_k(gates, TOPK)
        topw = jax.nn.softmax(topv, axis=-1)
        sel = jnp.take_along_axis(all_out, topi[:, :, None, :], axis=-1)
        gated = jnp.sum(sel * topw[:, :, None, :], axis=-1)
        return shared + gated

    def _L1_gnn_ref(x, edge_index, edge_prob, deg_noise, gat_w, gat_a_src, gat_a_tgt, gat_b, ln_local_g, ln_local_b, ln_global_g, ln_global_b, ln2_g, ln2_b, in_proj_w, conv_w, conv_b, x_proj_w, dt_proj_w, dt_proj_b, A_log, D_param, out_proj_w, wl, wg, ff1_w, ff1_b, ff2_w, ff2_b):
        import jax, jax.numpy as jnp
        import numpy as np
        from jax import lax
        N, E, D = (1024, 32768, 256)
        NH, FOUT = (4, 64)
        D_STATE, D_CONV, DT_RANK = (16, 4, 16)

        def _layer_norm(x, g, b, eps=1e-05):
            mu = jnp.mean(x, -1, keepdims=True)
            var = jnp.var(x, -1, keepdims=True)
            return (x - mu) * lax.rsqrt(var + eps) * g + b

        def _mamba(xs, in_proj_w, conv_w, conv_b, x_proj_w, dt_proj_w, dt_proj_b, A_log, D_param, out_proj_w):
            n = xs.shape[0]
            xz = xs @ in_proj_w.T
            xc, z = jnp.split(xz, 2, axis=-1)
            K = conv_w.shape[1]
            xp = jnp.pad(xc, ((K - 1, 0), (0, 0)))
            xc = sum((xp[k:k + n] * conv_w[:, k] for k in range(K))) + conv_b
            xc = jax.nn.silu(xc)
            dbc = xc @ x_proj_w.T
            dt = jax.nn.softplus(dbc[:, :DT_RANK] @ dt_proj_w.T + dt_proj_b)
            Bm = dbc[:, DT_RANK:DT_RANK + D_STATE]
            Cm = dbc[:, DT_RANK + D_STATE:]
            A = -jnp.exp(A_log)
            dA = jnp.exp(dt[:, :, None] * A)
            dBx = (dt * xc)[:, :, None] * Bm[:, None, :]

            def step(h, t):
                dA_t, dBx_t, C_t = t
                h = dA_t * h + dBx_t
                return (h, h @ C_t)
            _, y = lax.scan(step, jnp.zeros((xc.shape[1], D_STATE), xs.dtype), (dA, dBx, Cm))
            y = y + xc * D_param
            y = y * jax.nn.silu(z)
            return y @ out_proj_w.T

        def _forward(x, edge_index, deg_noise, gat_w, gat_a_src, gat_a_tgt, gat_b, ln_local_g, ln_local_b, ln_global_g, ln_global_b, ln2_g, ln2_b, in_proj_w, conv_w, conv_b, x_proj_w, dt_proj_w, dt_proj_b, A_log, D_param, out_proj_w, wl, wg, ff1_w, ff1_b, ff2_w, ff2_b):
            n = x.shape[0]
            src, tgt = (edge_index[0], edge_index[1])
            proj = (x @ gat_w.T).reshape(n, NH, FOUT)
            s_src = jnp.sum(proj * gat_a_src, -1)
            s_tgt = jnp.sum(proj * gat_a_tgt, -1)
            e = jax.nn.leaky_relu(s_src[src] + s_tgt[tgt], 0.2)
            exp_e = jnp.exp(e - jnp.max(e))
            denom = jax.ops.segment_sum(exp_e, tgt, num_segments=n)
            attn = exp_e / (denom[tgt] + 1e-16)
            agg = jax.ops.segment_sum(proj[src] * attn[:, :, None], tgt, num_segments=n)
            h_local = jax.nn.elu((agg + x.reshape(n, NH, FOUT)).reshape(n, NH * FOUT) + gat_b)
            h_local = _layer_norm(h_local, ln_local_g, ln_local_b)
            deg = jax.ops.segment_sum(jnp.ones((src.shape[0],), x.dtype), src, num_segments=n)
            perm = jnp.argsort(deg + deg_noise, stable=True)
            inv = jnp.argsort(perm)
            y = _mamba(x[perm], in_proj_w, conv_w, conv_b, x_proj_w, dt_proj_w, dt_proj_b, A_log, D_param, out_proj_w)
            h_attn = _layer_norm(x + y[inv], ln_global_g, ln_global_b)
            gate = jax.nn.sigmoid(h_local @ wl.T + h_attn @ wg.T)
            h = gate * h_local + (1.0 - gate) * h_attn
            ff = jax.nn.relu(h @ ff1_w.T + ff1_b) @ ff2_w.T + ff2_b
            return _layer_norm(h + ff, ln2_g, ln2_b)
        return _forward(x, edge_index, deg_noise, gat_w, gat_a_src, gat_a_tgt, gat_b, ln_local_g, ln_local_b, ln_global_g, ln_global_b, ln2_g, ln2_b, in_proj_w, conv_w, conv_b, x_proj_w, dt_proj_w, dt_proj_b, A_log, D_param, out_proj_w, wl, wg, ff1_w, ff1_b, ff2_w, ff2_b)

    def _L1_mix_ref(feature, W_qk, b_qk, W_v, b_v, gamma, beta):
        import jax, jax.numpy as jnp
        import numpy as np
        BN_EPS = 1e-05
        QK = jnp.einsum('bnd,kde->bkne', feature, W_qk) + b_qk[None, :, None, :]
        value = jnp.einsum('bnd,de->bne', feature, W_v) + b_v
        query = QK[:, 0]
        key = QK[:, 1]
        sm = jax.nn.softmax(key, axis=1)
        lam = jnp.einsum('bnd,bne->bde', sm, value)
        mean = jnp.mean(lam, axis=(0, 2), keepdims=True)
        var = jnp.var(lam, axis=(0, 2), keepdims=True)
        bn = (lam - mean) * jax.lax.rsqrt(var + BN_EPS)
        bn = bn * gamma[None, :, None] + beta[None, :, None]
        return jnp.einsum('bnd,bde->bne', query, bn)

    def _L1_ffn_ref(x, Wg, bg, W1, b1, W2, b2):
        import jax, jax.numpy as jnp
        import numpy as np
        B, S, D, E, H, K = (4, 512, 256, 8, 512, 2)
        Bv, Sv, Dv = x.shape
        gate_scores = x @ Wg + bg
        _, idx = jax.lax.top_k(gate_scores, K)
        mask = jax.nn.one_hot(idx, E, dtype=x.dtype).sum(axis=-2)
        xf = x.reshape(-1, Dv)
        mf = mask.reshape(-1, E)
        h = jax.nn.gelu(jnp.einsum('td,edh->teh', xf, W1) + b1[None], approximate=False)
        y = jnp.einsum('teh,ehd->ted', h, W2) + b2[None]
        out = jnp.einsum('ted,te->td', y, mf)
        return out.reshape(Bv, Sv, Dv)
    edge_index = jnp.stack([src, dst])
    xn = _layernorm(x, axis=-1)
    x = x + _L0_gnn_ref(xn, src, dst, L0_gnn_W_fc, L0_gnn_W_al, L0_gnn_W_ar, L0_gnn_W_res) + _L0_mix_ref(xn[None], L0_mix_Wq, L0_mix_Wk, L0_mix_Wv, L0_mix_Wm, L0_mix_W1, L0_mix_W2, L0_mix_g1, L0_mix_b1, L0_mix_g2, L0_mix_b2)[0]
    x = x + _L0_ffn_ref(_layernorm(x, axis=-1)[None], L0_ffn_sW1, L0_ffn_sb1, L0_ffn_sW2, L0_ffn_sb2, L0_ffn_sW3, L0_ffn_sb3, L0_ffn_eW1, L0_ffn_eb1, L0_ffn_eW2, L0_ffn_eb2, L0_ffn_eW3, L0_ffn_eb3, L0_ffn_gW, L0_ffn_gb)[0]
    xn = _layernorm(x, axis=-1)
    x = x + _L1_gnn_ref(xn, edge_index, edge_weight, node_vec, L1_gnn_gat_w, L1_gnn_gat_a_src, L1_gnn_gat_a_tgt, L1_gnn_gat_b, L1_gnn_ln_local_g, L1_gnn_ln_local_b, L1_gnn_ln_global_g, L1_gnn_ln_global_b, L1_gnn_ln2_g, L1_gnn_ln2_b, L1_gnn_in_proj_w, L1_gnn_conv_w, L1_gnn_conv_b, L1_gnn_x_proj_w, L1_gnn_dt_proj_w, L1_gnn_dt_proj_b, L1_gnn_A_log, L1_gnn_D_param, L1_gnn_out_proj_w, L1_gnn_wl, L1_gnn_wg, L1_gnn_ff1_w, L1_gnn_ff1_b, L1_gnn_ff2_w, L1_gnn_ff2_b) + _L1_mix_ref(xn[None], L1_mix_W_qk, L1_mix_b_qk, L1_mix_W_v, L1_mix_b_v, L1_mix_gamma, L1_mix_beta)[0]
    x = x + _L1_ffn_ref(_layernorm(x, axis=-1)[None], L1_ffn_Wg, L1_ffn_bg, L1_ffn_W1, L1_ffn_b1, L1_ffn_W2, L1_ffn_b2)[0]
    return x

_drawn_inputs = setup_inputs


def setup_inputs(seed=0):
    import zlib

    import numpy as np

    out = dict(_drawn_inputs(seed))
    spreads = {'L0_mix_g1': (1.0, 0.2),
     'L0_mix_b1': (0.0, 0.1),
     'L0_mix_g2': (1.0, 0.2),
     'L0_mix_b2': (0.0, 0.1),
     'L0_ffn_sb1': (0.0, 0.498),
     'L0_ffn_sb2': (0.0, 0.1),
     'L0_ffn_sb3': (0.0, 0.1),
     'L0_ffn_eb1': (0.0, 0.8),
     'L0_ffn_eb2': (0.0, 0.637),
     'L0_ffn_eb3': (0.0, 0.1),
     'L0_ffn_gb': (0.0, 0.777),
     'L1_gnn_gat_b': (0.0, 0.8),
     'L1_gnn_ln_local_g': (1.0, 0.6),
     'L1_gnn_ln_local_b': (0.0, 0.8),
     'L1_gnn_ln_global_g': (1.0, 0.6),
     'L1_gnn_ln_global_b': (0.0, 0.8),
     'L1_gnn_ln2_g': (1.0, 0.6),
     'L1_gnn_ln2_b': (0.0, 0.8),
     'L1_gnn_conv_b': (0.0, 0.8),
     'L1_gnn_D_param': (1.0, 0.6),
     'L1_gnn_ff1_b': (0.0, 0.8),
     'L1_gnn_ff2_b': (0.0, 0.8),
     'L1_mix_b_qk': (0.0, 0.36),
     'L1_mix_b_v': (0.0, 0.1),
     'L1_mix_gamma': (1.0, 0.2),
     'L1_mix_beta': (0.0, 0.1),
     'L1_ffn_bg': (0.0, 0.8),
     'L1_ffn_b1': (0.0, 0.8),
     'L1_ffn_b2': (0.0, 0.8)}
    factors = {'node_vec': 8.0,
     'L0_ffn_eW1': 3.18,
     'L1_gnn_gat_w': 6.166,
     'L1_gnn_gat_a_src': 8.0,
     'L1_gnn_gat_a_tgt': 8.0,
     'L1_gnn_in_proj_w': 8.0,
     'L1_gnn_conv_w': 8.0,
     'L1_gnn_x_proj_w': 8.0,
     'L1_gnn_dt_proj_w': 8.0,
     'L1_gnn_dt_proj_b': 8.0,
     'L1_gnn_A_log': 8.0,
     'L1_gnn_out_proj_w': 8.0,
     'L1_gnn_wl': 8.0,
     'L1_gnn_wg': 8.0,
     'L1_ffn_Wg': 5.758,
     'L1_ffn_W1': 8.0,
     'L1_ffn_W2': 8.0}
    for name, (base, spread) in spreads.items():
        noise = np.random.default_rng([zlib.crc32(name.encode()), seed]).standard_normal(out[name].shape)
        drawn = base * np.exp(spread * noise) if base else spread * noise
        out[name] = jnp.asarray(drawn.astype(out[name].dtype))
    for name, factor in factors.items():
        out[name] = (out[name] * factor).astype(out[name].dtype)
    return out
```

```python
from contextlib import ExitStack, contextmanager

import numpy as np

import concourse.bass as bass
from concourse import mybir

F32 = mybir.dt.float32
I32 = mybir.dt.int32
ALU = mybir.AluOpType
ACT = mybir.ActivationFunctionType
AX = mybir.AxisListType

P = 128
N = 6250
E = 200000
D = 256
H = 4
TILES = (N + P - 1) // P
NPAD = TILES * P
LAST = N - (TILES - 1) * P
GROUP = 16
ETILES = -(-E // (P * GROUP)) * GROUP
EPAD = ETILES * P
EROW = EPAD // P
STEPS = -(-((E + P - 1) // P + TILES - 1) // GROUP) * GROUP
SBLK = (STEPS + P - 1) // P
SPAD = SBLK * P
FIRST_SEM = 100
POOL_SEM = 220
pool_sems = [POOL_SEM]
BIG = 1.0e30
FAR = 1 << 20
LN_EPS = 1e-5

CONST_COLS = dict(ident=(0, 128), iota=(128, 256), upper=(256, 384), ones=(384, 512), block32=(512, 640),
                  valid=(640, 640 + TILES), step=(700, 700 + SBLK), bound=(720, 720 + TILES - 1),
                  head32=(780, 784), pid=(784, 785), eps=(785, 786), mhalf=(786, 787), zero=(787, 788),
                  one=(788, 789), lower=(800, 928))
CONST_N = 928


def constants():
    c = np.zeros((P, CONST_N), np.float32)
    p = np.arange(P)

    def put(k, v):
        lo, hi = CONST_COLS[k]
        c[:, lo:hi] = v

    put("ident", np.eye(P))
    put("iota", np.broadcast_to(p, (P, P)))
    put("upper", p[:, None] < p[None, :])
    put("lower", p[:, None] > p[None, :])
    put("ones", 1.0)
    put("block32", p[:, None] // 32 == p[None, :] // 32)
    put("valid", p[:, None] + P * np.arange(TILES)[None, :] < N)
    put("step", p[:, None] + P * np.arange(SBLK)[None, :])
    put("bound", np.arange(1, TILES)[None, :])
    put("head32", p[:, None] // 32 == np.arange(4)[None, :])
    put("pid", p[:, None])
    put("eps", LN_EPS)
    put("mhalf", -0.5)
    put("one", 1.0)
    return c


class Net:
    pass


def rows(ap):
    return ap.rearrange("p a b -> p (a b)")


def wait(net, eng, sem, value):
    eng.wait_ge(sem, value)


def wait_apart(net, eng, sem, value):
    eng.wait_ge(sem, value)
    eng.sem_inc(net.tick, 1)


@contextmanager
def stage(nc, name, sems):
    pool = [x for x in sems if x.startswith("gp_")]
    rest = [x for x in sems if not x.startswith("gp_")]
    with ExitStack() as c:
        ns = {x: c.enter_context(nc.semaphore(f"{name}_{x}", num=first + i))
              for first, group in ((FIRST_SEM, rest), (pool_sems[0], pool)) for i, x in enumerate(group)}
        pool_sems[0] += len(pool)
        with nc.Block() as block:
            yield block, ns
        nc.all_engine_barrier(sems_to_clear=range(FIRST_SEM, FIRST_SEM + len(rest)))


def buffers(nc, c, name, **shapes):
    return {k: c.enter_context(nc.sbuf_tensor(f"{name}_{k}", [P] + list(v), I32 if k.endswith("_i") else F32))
            for k, v in shapes.items()}


def weight(dram):
    return dram.rearrange("(a p) n -> p a n", p=P)


def load_stage(nc, net):
    with stage(nc, "load", ["zeroed", "x_in", "c_in"]) as (block, s):
        @block.vector
        def _(dve):
            dve.memset(net.X[:, TILES - 1, :], 0.0).then_inc(s["zeroed"], 1)
            dve.memset(net.zeros[:, :], 0.0)
            dve.memset(net.stat[:, 0:1], 0.0)

        @block.sync
        def _(sp):
            sp.dma_start(net.C[:, :], net.inp["consts"]).then_inc(s["c_in"], 16)
            sp.dma_start(net.X[:, 0:TILES - 1, :],
                         net.inp["x"][0:(TILES - 1) * P, :].rearrange("(t p) d -> p t d", p=P)).then_inc(s["x_in"], 16)
            sp.wait_ge(s["zeroed"], 1)
            sp.dma_start(net.X[0:LAST, TILES - 1, :], net.inp["x"][(TILES - 1) * P:N, :]).then_inc(s["x_in"], 16)
            sp.wait_ge(s["x_in"], 32)
            sp.wait_ge(s["c_in"], 16)


def norm_stage(nc, net, name):
    with ExitStack() as c:
        b = buffers(nc, c, name, six=[TILES, 6], mean=[TILES], gap=[TILES], var=[TILES])
        with stage(nc, name, ["stats", "rstd"]) as (block, s):
            @block.vector
            def _(dve):
                with dve.Fori(0, TILES) as t:
                    dve.bn_stats(rows(b["six"][:, bass.ds(t, 1), :]), rows(net.X[:, bass.ds(t, 1), :]))
                dve.drain()
                even, odd = b["six"][:, :, 0:3], b["six"][:, :, 3:6]
                dve.tensor_tensor(b["mean"][:, :], even[:, :, 1], odd[:, :, 1], ALU.add)
                dve.tensor_tensor(b["gap"][:, :], even[:, :, 1], odd[:, :, 1], ALU.subtract)
                dve.tensor_tensor(b["var"][:, :], even[:, :, 2], odd[:, :, 2], ALU.add)
                dve.drain()
                dve.tensor_tensor(b["gap"][:, :], b["gap"][:, :], b["gap"][:, :], ALU.mult)
                dve.drain()
                dve.scalar_tensor_tensor(b["var"][:, :], b["gap"][:, :], D / 4.0, b["var"][:, :], ALU.mult, ALU.add)
                dve.drain()
                dve.tensor_scalar(b["var"][:, :], b["var"][:, :], 1.0 / D, LN_EPS, ALU.mult, ALU.add).then_inc(s["stats"], 1)
                dve.wait_ge(s["rstd"], 1)
                dve.scalar_tensor_tensor(net.shift[:, :], b["mean"][:, :], -0.5, net.rstd[:, :], ALU.mult, ALU.mult)

            @block.gpsimd
            def _(pool):
                pool.wait_ge(s["stats"], 1)
                pool.tensor_tensor(net.rstd[:, :], b["var"][:, :], net.const("mhalf").to_broadcast([P, TILES]),
                                   ALU.pow).then_inc(s["rstd"], 1)


def project_stage(nc, net):
    with ExitStack() as c:
        b = buffers(nc, c, "proj", w=[2, 264], wT=[2, D], al=[2, 8], wkv=[2, 512], xn=[D], xnT=[2, P],
                    tab=[264], kx=[D], ke=[D], vv=[2, 132], kvacc=[2, 132])
        ps_tr, ps_tab, ps_kv, ps_sum = net.PS[0], net.PS[1], net.PS[2], net.PS[3]
        names = ["w_in", "folded", "fold_ps", "xn", "tr", "xnT", "mm", "tab_sb", "tab_out", "kmin", "kexp",
                 "v_ready", "kv_ready", "kv_mm", "kv_used", "end"]
        with stage(nc, "proj", names) as (block, s):
            @block.sync
            def _(sp):
                sp.dma_start(b["w"][:, :, 0:D], weight(net.inp["g0_w"])).then_inc(s["w_in"], 16)
                sp.dma_start(b["wT"][:, :, :], weight(net.inp["g0_wT"])).then_inc(s["w_in"], 16)
                sp.dma_start(b["al"][:, :, :], weight(net.inp["g0_al"])).then_inc(s["w_in"], 16)
                sp.dma_start(b["wkv"][:, :, :], weight(net.inp["m0_wkv"])).then_inc(s["w_in"], 16)
                with sp.Fori(0, TILES) as t:
                    wait(net, sp, s["tab_sb"], t + 1)
                    sp.dma_start(net.table[bass.ds(t * P, P), :], b["tab"][:, 0:D]).then_inc(s["tab_out"], 16)
                sp.wait_ge(s["end"], 1)
                sp.dma_start(net.src_tab.rearrange("(t p) c -> p t c", p=P), net.node_src[:, :, :]).then_inc(s["tab_out"], 16)
                sp.wait_ge(s["tab_out"], 16 * (TILES + 1) + 1)

            @block.vector
            def _(dve):
                dve.memset(b["kvacc"][:, :, :], 0.0)
                dve.wait_ge(s["fold_ps"], 1)
                for i in range(2):
                    ins = dve.tensor_copy(b["w"][:, i, D:D + 8], ps_tab[:, 8 * i:8 * i + 8])
                ins.then_inc(s["folded"], 1)
                with dve.Fori(0, TILES) as t:
                    dve.tensor_scalar(b["xn"][:, :], rows(net.X[:, bass.ds(t, 1), :]), net.rstd[:, bass.ds(t, 1)],
                                      net.shift[:, bass.ds(t, 1)], ALU.mult, ALU.add).then_inc(s["xn"], 1)
                    wait(net, dve, s["mm"], t + 1)
                    dve.tensor_scalar(b["kx"][:, :], ps_kv[:, 0:D], 0.0, None, ALU.min).then_inc(s["kmin"], 1)
                    dve.tensor_copy(b["vv"][:, :, 0:P], ps_kv[:, D:2 * D].rearrange("p (a b) -> p a b", a=2))
                    for i in range(2):
                        dve.tensor_scalar(b["vv"][:, i, P:P + 1], net.const("valid")[:, bass.ds(t, 1)], 1.0, None, ALU.mult)
                    wait(net, dve, s["kexp"], t + 1)
                    dve.scalar_tensor_tensor(b["ke"][:, :], ps_kv[:, 0:D], 0.0, b["kx"][:, :], ALU.max, ALU.add).then_inc(s["kv_ready"], 1)
                    wait(net, dve, s["kv_mm"], t + 1)
                    dve.tensor_tensor(b["kvacc"][:, :, 0:P + 1], b["kvacc"][:, :, 0:P + 1],
                                      ps_sum[:, 0:264].rearrange("p (a b) -> p a b", a=2)[:, :, 0:P + 1],
                                      ALU.add).then_inc(s["kv_used"], 1)
                    dve.drain()
                for i in range(2):
                    dve.tensor_tensor(net.kv[:, i, :], b["kvacc"][:, i, 0:P], net.const("block32"), ALU.mult)
                    dve.tensor_scalar(net.ksum[:, i, :], net.const("head32"), b["kvacc"][:, i, P:P + 1], None, ALU.mult)

            @block.scalar
            def _(act):
                act.sem_inc(s["tab_out"], 1)
                with act.Fori(0, TILES) as t:
                    wait(net, act, s["tr"], t + 1)
                    act.activation(rows(b["xnT"][:, :, :]), ps_tr[:, 0:D], ACT.Copy).then_inc(s["xnT"], 1)
                    wait(net, act, s["kmin"], t + 1)
                    act.activation(b["kx"][:, :], b["kx"][:, :], ACT.Exp).then_inc(s["kexp"], 1)
                    wait(net, act, s["mm"], t + 1)
                    act.activation(net.node_src[:, bass.ds(t, 1), :].rearrange("p a b -> p (a b)"), ps_tab[:, D:D + 4], ACT.Copy)
                    act.activation(net.node_dst[:, bass.ds(t, 1), :].rearrange("p a b -> p (a b)"), ps_tab[:, D + 4:D + 8], ACT.Copy)
                    wait(net, act, s["tab_out"], 16 * t + 1)
                    act.activation(b["tab"][:, 0:D], ps_tab[:, 0:D], ACT.Copy).then_inc(s["tab_sb"], 1)
                act.sem_inc(s["end"], 1)

            @block.tensor
            def _(pe):
                pe.wait_ge(s["w_in"], 64)
                for i in range(2):
                    for k in range(2):
                        ins = pe.matmul(ps_tab[:, 8 * i:8 * i + 8], b["wT"][:, k, i * P:(i + 1) * P], b["al"][:, k, :],
                                        start=(k == 0), stop=(k == 1))
                ins.then_inc(s["fold_ps"], 1)
                pe.wait_ge(s["folded"], 1)
                with pe.Fori(0, TILES) as t:
                    wait(net, pe, s["xn"], t + 1)
                    for k in range(2):
                        ins = pe.transpose(ps_tr[:, k * P:(k + 1) * P], b["xn"][:, k * P:(k + 1) * P], net.const("ident"))
                    ins.then_inc(s["tr"], 1)
                    wait(net, pe, s["xnT"], t + 1)
                    for k in range(2):
                        pe.matmul(ps_tab[:, 0:264], b["xnT"][:, k, :], b["w"][:, k, :], start=(k == 0), stop=(k == 1))
                    for k in range(2):
                        ins = pe.matmul(ps_kv[:, :], b["xnT"][:, k, :], b["wkv"][:, k, :], start=(k == 0), stop=(k == 1))
                    ins.then_inc(s["mm"], 1)
                    wait(net, pe, s["kv_ready"], t + 1)
                    for i in range(2):
                        ins = pe.matmul(ps_sum[:, i * 132:i * 132 + P + 1], b["ke"][:, i * P:(i + 1) * P], b["vv"][:, i, 0:P + 1],
                                        start=True, stop=True)
                    ins.then_inc(s["kv_mm"], 1)



def pad_edges_stage(nc, net):
    with ExitStack() as c:
        b = buffers(nc, c, "pad", minus_i=[64])
        with stage(nc, "pad", ["ready", "moved"]) as (block, s):
            @block.vector
            def _(dve):
                dve.memset(b["minus_i"][:, :], -1).then_inc(s["ready"], 1)

            @block.sync
            def _(sp):
                pads = EPAD - E
                for src, dst in ((net.inp["src"], net.src_pad), (net.inp["dst"], net.dst_pad)):
                    flat = dst.rearrange("t e -> (t e)")
                    sp.dma_start(flat[0:E].rearrange("(a b) -> a b", a=125),
                                 src.rearrange("o (a b) -> (o a) b", a=125)).then_inc(s["moved"], 16)
                sp.wait_ge(s["ready"], 1)
                for dst in (net.src_pad, net.dst_pad):
                    sp.dma_start(dst.rearrange("t e -> (t e)")[E:EPAD].rearrange("(a b) -> a b", b=64),
                                 b["minus_i"][0:pads // 64, :]).then_inc(s["moved"], 16)
                sp.dma_start(net.start_rec.rearrange("(p a b) c -> p a (b c)", p=P, a=28), net.zeros[:, 0:448].unsqueeze(1).to_broadcast([P, 28, 448])).then_inc(s["moved"], 16)
                sp.wait_ge(s["moved"], 80)


def degree_work(nc, net, c, block, s, b):
    G = 8
    oh = dict(
        lo=c.enter_context(nc.sbuf_tensor("deg_hot_lo", [P, 2, G, P], mybir.dt.bfloat16)),
        hi=c.enter_context(nc.sbuf_tensor("deg_hot_hi", [P, 2, G, TILES], mybir.dt.bfloat16)))
    d = buffers(nc, c, "deg", raw_i=[EROW], lo_i=[EROW])
    digits = net.agg[:, :, :].rearrange("p a b -> p (a b)")[:, 0:4 * EROW].rearrange("p (a q g) -> p a q g", a=2, q=2)
    d["lo"], d["hi"] = digits[:, 0, :, :], digits[:, 1, :, :]
    ps = net.PS[0:2]
    iota = net.PS[7][:, 0:P]
    acc = [net.degree, net.src_degree]

    @block.vector
    def _(dve):
        dve.sem_inc(s["deg_add"], 2)
        dve.tensor_copy(iota, net.const("iota"))
        for q in range(2):
            dve.memset(acc[q][:, :], 0.0)
        for q, raw in enumerate((b["dst_i"], b["src_i"])):
            dve.wait_ge(s["edges_in"], 32)
            dve.tensor_scalar(d["raw_i"][:, :], raw[:, :], 7, None, ALU.arith_shift_right)
            dve.tensor_scalar(d["lo_i"][:, :], raw[:, :], P - 1, None, ALU.bitwise_and)
            dve.drain()
            dve.tensor_copy(d["hi"][:, q, :], d["raw_i"][:, :])
            dve.tensor_copy(d["lo"][:, q, :], d["lo_i"][:, :])
            dve.drain()
        with dve.Fori(0, EROW // G) as it:
            for q in range(2):
                for wide, num, out in ((P, d["lo"], oh["lo"]), (TILES, d["hi"], oh["hi"])):
                    ins = dve.tensor_tensor(out[:, q, :, :], iota[:, 0:wide].unsqueeze(1).to_broadcast([P, G, wide]),
                                            num[:, q, bass.ds(it * G, G)].unsqueeze(2).to_broadcast([P, G, wide]), ALU.is_equal)
                ins.then_inc(s["deg_hot"], 1)
            for q in range(2):
                wait(net, dve, s["deg_mm"], it * 2 + q + 1)
                dve.tensor_tensor(acc[q][:, :], acc[q][:, :], ps[q][:, 0:TILES], ALU.add).then_inc(s["deg_add"], 1)
            dve.drain()

    @block.tensor
    def _(pe):
        with pe.Fori(0, EROW // G) as it:
            for q in range(2):
                wait(net, pe, s["deg_hot"], it * 2 + q + 1)
                wait(net, pe, s["deg_add"], 2 * it + q + 1)
                for g in range(G):
                    ins = pe.matmul(ps[q][:, 0:TILES], oh["lo"][:, q, g, :], oh["hi"][:, q, g, :],
                                    start=(g == 0), stop=(g == G - 1))
                ins.then_inc(s["deg_mm"], 1)


def gather_stage(nc, net, name, work):
    SET = 8
    with ExitStack() as c:
        b = buffers(nc, c, name, src_i=[EROW], dst_i=[EROW], idx_src_i=[EROW], idx_i=[2, SET], land=[2, SET, H])
        names = ["edges_in", "clipped", "idx_ready", "gp_landed0", "gp_landed1", "taken0", "taken1",
                 "deg_hot", "deg_mm", "deg_add", "w0", "w1", "w2", "w3"]
        with stage(nc, name, names) as (block, s):
            landed, taken = (s["gp_landed0"], s["gp_landed1"]), (s["taken0"], s["taken1"])

            @block.sync
            def _(sp):
                sp.dma_start(b["src_i"][:, :], net.src_pad.rearrange("(p a) e -> p (a e)", p=P) if EROW % P == 0 else
                             net.src_pad.rearrange("t e -> (t e)").rearrange("(p g) -> p g", p=P)).then_inc(s["edges_in"], 16)
                sp.dma_start(b["dst_i"][:, :], net.dst_pad.rearrange("t e -> (t e)").rearrange("(p g) -> p g", p=P)).then_inc(s["edges_in"], 16)
                sp.wait_ge(s["edges_in"], 32)

            @block.gpsimd
            def _(pool):
                pool.wait_ge(s["edges_in"], 32)
                pool.tensor_scalar(b["idx_src_i"][:, :], b["src_i"][:, :], 0, None, ALU.max).then_inc(s["clipped"], 1)
                pool.wait_ge(s["clipped"], 1)
                with pool.Fori(0, EROW // (2 * SET)) as it:
                    for q in range(2):
                        wait(net, pool, taken[q], it + 1)
                        pool.tensor_copy(b["idx_i"][:, q, :], b["idx_src_i"][:, bass.ds((it * 2 + q) * SET, SET)]).then_inc(s["idx_ready"], 1)
                        wait_apart(net, pool, s["idx_ready"], it * 2 + q + 1)
                        for r in range(SET):
                            pool.indirect_dma_start(b["land"][:, q, r, :], None, net.src_tab,
                                                    bass.IndirectOffsetOnAxis(ap=b["idx_i"][:, q, r:r + 1], axis=0)).then_inc(landed[q], 16)

            @block.scalar
            def _(act):
                for q in range(2):
                    act.sem_inc(taken[q], 1)
                with act.Fori(0, EROW // (2 * SET)) as it:
                    for q in range(2):
                        wait(net, act, landed[q], (it + 1) * 16 * SET)
                        act.activation(net.edge[:, bass.ds((it * 2 + q) * SET * H, SET * H)], b["land"][:, q, :, :].rearrange("p a b -> p (a b)"),
                                       ACT.Copy).then_inc(taken[q], 1)

            work(nc, net, c, block, s, b)


def index_stage(nc, net):
    with ExitStack() as c:
        b = buffers(nc, c, "index", within=[TILES], total=[TILES], run=[TILES], f=[TILES], thr_i=[TILES], thr=[TILES],
                    hit=[TILES], tile=[SBLK], tile128=[SBLK], tile_i=[SBLK], etile=[SBLK], 
                    rows_i=[SBLK, 2, P], rows=[SBLK, 2, P])
        pa, pb, pt = net.PS[0], net.PS[1], net.PS[2]
        with stage(nc, "index", ["sums", "etile", "gp_rows_in", "rows_f", "tr", "copied", "tile_out", "tile_rdy"]) as (block, s):
            @block.tensor
            def _(pe):
                pe.matmul(pa[:, 0:TILES], net.const("upper"), net.degree[:, :], start=True, stop=True)
                pe.matmul(pb[:, 0:TILES], net.const("ones"), net.degree[:, :], start=True, stop=True).then_inc(s["sums"], 1)
                for j in range(SBLK):
                    pe.wait_ge(s["rows_f"], j + 1)
                    if j:
                        pe.wait_ge(s["copied"], j)
                    for q in range(2):
                        ins = pe.transpose(pt[:, q * P:(q + 1) * P], b["rows"][:, j, q, :], net.const("ident"))
                    ins.then_inc(s["tr"], 1)

            @block.vector
            def _(dve):
                dve.wait_ge(s["sums"], 1)
                dve.tensor_copy(b["total"][:, :], pb[:, 0:TILES])
                dve.tensor_copy(b["within"][:, :], pa[:, 0:TILES])
                dve.drain()
                dve.tensor_tensor_scan(b["run"][:, :], net.const("ones")[:, 0:TILES], b["total"][:, :], 0.0, ALU.mult, ALU.add)
                dve.drain()
                dve.tensor_tensor(b["run"][:, :], b["run"][:, :], b["total"][:, :], ALU.subtract)
                dve.drain()
                dve.tensor_tensor(b["f"][:, :], b["run"][:, :], b["within"][:, :], ALU.add)
                dve.drain()
                dve.tensor_scalar(b["hit"][:, :], net.degree[:, :], 0.0, float(FAR), ALU.is_equal, ALU.mult)
                dve.drain()
                dve.tensor_tensor(net.starts[:, :], b["f"][:, :], b["hit"][:, :], ALU.add)
                dve.tensor_tensor(b["f"][:, :], b["f"][:, :], net.degree[:, :], ALU.add)
                dve.drain()
                dve.tensor_scalar(net.ends[:, :], b["f"][:, :], 1.0, 0.0, ALU.subtract, ALU.max)
                dve.tensor_copy(b["thr_i"][:, :], b["run"][:, :])
                dve.drain()
                dve.tensor_scalar(b["thr_i"][:, :], b["thr_i"][:, :], 7, None, ALU.arith_shift_right)
                dve.drain()
                dve.tensor_copy(b["thr"][:, :], b["thr_i"][:, :])
                dve.drain()
                dve.tensor_tensor(b["thr"][:, 1:TILES], b["thr"][:, 1:TILES], net.const("bound"), ALU.add)
                dve.drain()
                for j in range(SBLK):
                    dve.tensor_scalar(b["hit"][:, 1:TILES], b["thr"][:, 1:TILES], net.const("step")[:, j:j + 1], None, ALU.is_le,
                                      ALU.add, accum_out=b["tile"][:, j:j + 1])
                    dve.drain()
                dve.tensor_tensor(b["etile"][:, :], net.const("step"), b["tile"][:, :], ALU.subtract)
                dve.tensor_scalar(b["tile128"][:, :], b["tile"][:, :], float(P), None, ALU.mult)
                dve.tensor_scalar(b["tile_i"][:, :], b["tile"][:, :], float(D + H), None, ALU.mult).then_inc(s["tile_rdy"], 1)
                dve.drain()
                dve.tensor_scalar(net.step_et[:, :], b["etile"][:, :], float(ETILES - 1), None, ALU.min).then_inc(s["etile"], 1)
                for j in range(SBLK):
                    dve.wait_ge(s["gp_rows_in"], 32 * SBLK)
                    dve.tensor_scalar(b["rows"][:, j, 0, :], b["rows_i"][:, j, 0, :], 0.0, None, ALU.max)
                    dve.tensor_scalar(b["rows"][:, j, 1, :], b["rows_i"][:, j, 1, :], b["tile128"][:, j:j + 1], None, ALU.subtract).then_inc(s["rows_f"], 1)
                    dve.wait_ge(s["tr"], j + 1)
                    dve.tensor_copy(net.step_src[:, j * P:(j + 1) * P], pt[:, 0:P])
                    dve.tensor_copy(net.step_dst[:, j * P:(j + 1) * P], pt[:, P:2 * P]).then_inc(s["copied"], 1)

            @block.gpsimd
            def _(pool):
                pool.wait_ge(s["etile"], 1)
                for j in range(SBLK):
                    for q, tab in enumerate((net.src_pad, net.dst_pad)):
                        pool.indirect_dma_start(b["rows_i"][:, j, q, :], None, tab,
                                                bass.IndirectOffsetOnAxis(ap=net.step_et[:, j:j + 1], axis=0)).then_inc(s["gp_rows_in"], 16)

            @block.sync
            def _(sp):
                sp.wait_ge(s["tile_rdy"], 1)
                with nc.allow_non_contiguous_dma("13 x 128 step numbers"):
                    sp.dma_start(net.tile_row.rearrange("o (j p) -> p (o j)", p=P), b["tile_i"][:, :]).then_inc(s["tile_out"], 16)
                sp.wait_ge(s["tile_out"], 16)


def weight_stage(nc, net, name, slope):
    rec = net.agg[:, :, :].rearrange("p a b -> p (a b)")[:, 0:EROW * 8].rearrange("p (g c) -> p g c", c=8)
    edge = net.edge[:, 0:EROW * H].rearrange("p (g c) -> p g c", c=H)
    w_rows = net.agg[:, :, :].rearrange("p a b -> p (a b)")[:, 0:SBLK * 512].rearrange("p (j c) -> p j c", c=512)
    with ExitStack() as c:
        b = buffers(nc, c, name, dst=[EROW], pen=[EROW], keep=[EROW], run=[EROW, H],
                    match=[P], diag=[H, P], spread=[H, P], carry=[H], node=[TILES, 8], z=[TILES, H],
                    first_i=[1], first=[8], hit=[TILES])
        dst_i = net.agg[:, :, :].rearrange("p a b -> p (a b)")[:, 0:EROW].bitcast(I32)
        p_last, p_row, p_t = net.PS[0], net.PS[1], net.PS[2:6]
        names = ["dst_in", "last_ps", "diag", "spread", "carried", "run_out", "gp_node_in", "node_done", "node_out", "first_idx",
                 "gp_first_in", "gp_scatter", "rec_in", "rec_ready", "exp_in", "exp_out", "w_out", "gp_rows_in", "tr", "copied", "dcopy", "etile", "sums"]
        with stage(nc, name, names) as (block, s):
            edges_of = lambda a: a.rearrange("(p g) c -> p g c", p=P)

            @block.sync
            def _(sp):
                sp.dma_start(dst_i, net.dst_pad.rearrange("t e -> (t e)").rearrange("(p g) -> p g", p=P)).then_inc(s["dst_in"], 16)
                sp.wait_ge(s["carried"], 1)
                sp.dma_start(edges_of(net.run_max), b["run"][:, :, :]).then_inc(s["run_out"], 16)
                sp.wait_ge(s["node_done"], 1)
                sp.dma_start(net.node_rec.rearrange("(t p) c -> p t c", p=P), b["node"][:, :, :]).then_inc(s["node_out"], 16)
                sp.wait_ge(s["gp_scatter"], 16 * TILES)
                sp.dma_start(rec, edges_of(net.start_rec)).then_inc(s["rec_in"], 16)
                sp.wait_ge(s["exp_out"], 1)
                sp.dma_start(net.weights.rearrange("t c -> (t c)").rearrange("(p g) -> p g", p=P), net.edge[:, 0:EROW * H]).then_inc(s["w_out"], 16)
                sp.wait_ge(s["w_out"], 16)

            @block.gpsimd
            def _(pool):
                pool.wait_ge(s["run_out"], 16)
                for t in range(TILES):
                    pool.indirect_dma_start(net.node_max[:, t, :], None, net.run_max,
                                            bass.IndirectOffsetOnAxis(ap=net.ends[:, t:t + 1], axis=0)).then_inc(s["gp_node_in"], 16)
                pool.wait_ge(s["node_done"], 1)
                for t in range(TILES):
                    pool.indirect_dma_start(net.start_rec, bass.IndirectOffsetOnAxis(ap=net.starts[:, t:t + 1], axis=0),
                                            b["node"][:, t, :], None, bounds_check=EPAD - 1, oob_is_err=False).then_inc(s["gp_scatter"], 16)
                pool.wait_ge(s["node_out"], 16)
                pool.wait_ge(s["first_idx"], 1)
                pool.indirect_dma_start(b["first"][:, :], None, net.node_rec,
                                        bass.IndirectOffsetOnAxis(ap=b["first_i"][:, 0:1], axis=0)).then_inc(s["gp_first_in"], 16)
                pool.wait_ge(s["w_out"], 16)
                for j in range(SBLK):
                    pool.indirect_dma_start(w_rows[:, j, :], None, net.weights,
                                            bass.IndirectOffsetOnAxis(ap=net.step_et[:, j:j + 1], axis=0)).then_inc(s["gp_rows_in"], 16)

            @block.tensor
            def _(pe):
                pe.wait_ge(s["diag"], 1)
                pe.matmul(p_last[:, 0:P], net.const("ones"), b["diag"][:, 0, :], start=True, stop=True).then_inc(s["last_ps"], 1)
                pe.wait_ge(s["diag"], 2)
                pe.matmul(p_row[:, :], net.const("ones"), b["diag"][:, :, :].rearrange("p a b -> p (a b)"), start=True, stop=True).then_inc(s["spread"], 1)
                for j in range(SBLK):
                    pe.wait_ge(s["gp_rows_in"], 16 * SBLK)
                    if j >= 4:
                        pe.wait_ge(s["copied"], j - 3)
                    for h in range(H):
                        ins = pe.transpose(p_t[j % 4][:, h * P:(h + 1) * P],
                                           w_rows[:, j, :].rearrange("p (e h) -> p e h", h=H)[:, :, h], net.const("ident"))
                    ins.then_inc(s["tr"], 1)

            @block.scalar
            def _(act):
                act.wait_ge(s["exp_in"], 1)
                act.activation(net.edge[:, 0:EROW * H], net.edge[:, 0:EROW * H], ACT.Exp).then_inc(s["exp_out"], 1)
                for j in range(SBLK):
                    act.wait_ge(s["tr"], j + 1)
                    act.wait_ge(s["w_out"], 16)
                    act.activation(net.edge[:, j * P * H:(j + 1) * P * H].rearrange("p (s h) -> p h s", h=H),
                                   p_t[j % 4][:, :].rearrange("p (h s) -> p h s", h=H), ACT.Copy).then_inc(s["copied"], 1)

            @block.vector
            def _(dve):
                flat = lambda a: a.rearrange("p a b -> p (a b)")
                dve.wait_ge(s["dst_in"], 16)
                dve.tensor_copy(b["dst"][:, :], dst_i)
                dve.drain()
                dve.tensor_scalar(b["first_i"][:, :], b["dst"][:, 0:1], 0.0, None, ALU.max).then_inc(s["first_idx"], 1)
                dve.tensor_scalar(b["diag"][:, 0, :], net.const("ident"), b["dst"][:, EROW - 1:EROW], None, ALU.mult).then_inc(s["diag"], 1)
                dve.tensor_tensor(b["keep"][:, 1:EROW], b["dst"][:, 1:EROW], b["dst"][:, 0:EROW - 1], ALU.is_equal)
                dve.memset(b["keep"][:, 0:1], 0.0)
                dve.drain()
                dve.tensor_scalar(b["pen"][:, :], b["keep"][:, :], BIG, BIG, ALU.mult, ALU.subtract)
                dve.drain()
                dve.memset(b["pen"][:, 0:1], 0.0)
                dve.wait_ge(s["last_ps"], 1)
                dve.tensor_scalar(b["match"][:, :], p_last[:, 0:P], b["dst"][:, 0:1], None, ALU.is_equal)
                dve.drain()
                dve.tensor_tensor(b["match"][:, :], b["match"][:, :], net.const("lower"), ALU.mult)
                dve.drain()
                dve.tensor_scalar(b["match"][:, :], b["match"][:, :], BIG, BIG, ALU.mult, ALU.subtract)
                for h in range(H):
                    dve.tensor_tensor_scan(b["run"][:, :, h], b["pen"][:, :], edge[:, :, h], -BIG, ALU.add, ALU.max)
                dve.drain()
                for h in range(H):
                    ins = dve.tensor_scalar(b["diag"][:, h, :], net.const("ident"), b["run"][:, EROW - 1, h:h + 1], None, ALU.mult)
                ins.then_inc(s["diag"], 1)
                dve.wait_ge(s["spread"], 1)
                for h in range(H):
                    dve.tensor_tensor(b["spread"][:, h, :], b["match"][:, :], p_row[:, h * P:(h + 1) * P], ALU.add)
                dve.drain()
                dve.tensor_reduce(b["carry"][:, :], b["spread"][:, :, :], AX.X, ALU.max)
                dve.drain()
                for h in range(H):
                    ins = dve.tensor_tensor_scan(b["run"][:, :, h], b["pen"][:, :], edge[:, :, h], b["carry"][:, h:h + 1], ALU.add, ALU.max)
                ins.then_inc(s["carried"], 1)
                dve.wait_ge(s["gp_node_in"], 16 * TILES)
                dve.tensor_tensor(flat(b["z"][:, :, :]), flat(net.node_dst[:, :, :]), flat(net.node_max[:, :, :]), ALU.add)
                dve.tensor_copy(b["node"][:, :, 0:H], net.node_dst[:, :, :])
                dve.drain()
                dve.scalar_tensor_tensor(flat(net.node_max[:, :, :]), flat(b["z"][:, :, :]), slope, flat(b["z"][:, :, :]), ALU.mult, ALU.max)
                dve.drain()
                dve.tensor_scalar(b["hit"][:, :], net.degree[:, :], 0.0, None, ALU.is_gt)
                dve.drain()
                for h in range(H):
                    dve.tensor_tensor(net.node_max[:, :, h], net.node_max[:, :, h], b["hit"][:, :], ALU.mult)
                dve.drain()
                dve.tensor_copy(b["node"][:, :, H:2 * H], net.node_max[:, :, :]).then_inc(s["node_done"], 1)
                dve.wait_ge(s["rec_in"], 16)
                dve.wait_ge(s["gp_first_in"], 16)
                dve.tensor_copy(rec[:, 0, :], b["first"][:, :])
                dve.drain()
                for k in range(8):
                    dve.tensor_tensor_scan(rec[:, :, k], b["keep"][:, :], rec[:, :, k], 0.0, ALU.mult, ALU.add)
                dve.drain()
                dve.tensor_tensor(edge, edge, rec[:, :, 0:H], ALU.add)
                dve.drain()
                dve.scalar_tensor_tensor(flat(edge), flat(edge), slope, flat(edge), ALU.mult, ALU.max)
                dve.drain()
                dve.tensor_tensor(edge, edge, rec[:, :, H:2 * H], ALU.subtract)
                dve.drain()
                dve.tensor_scalar(flat(edge), flat(edge), 0.0, None, ALU.min).then_inc(s["exp_in"], 1)


def aggregate_stage(nc, net, name):
    SETS, SET, RING = 4, 4, 4
    U = SETS * SET
    aggf = net.agg[:, :, :].rearrange("p a b -> p (a b)")
    with ExitStack() as c:
        b = buffers(nc, c, name, idx_i=[SETS, SET], got=[U, D], hot=[4, P], wx=[4, D])
        where = c.enter_context(nc.sbuf_tensor(f"{name}_where", [1, SPAD], I32))
        names = ["where_in", "idx_ready"] + [f"gp_landed{i}" for i in range(SETS)] + \
                ["weighed", "hot", "mm"]
        with stage(nc, name, names) as (block, s):
            landed = (s["gp_landed0"], s["gp_landed1"], s["gp_landed2"], s["gp_landed3"])

            @block.sync
            def _(sp):
                sp.dma_start(where[:, :], net.tile_row).then_inc(s["where_in"], 16)
                sp.wait_ge(s["where_in"], 16)

            @block.gpsimd
            def _(pool):
                with pool.Fori(0, STEPS // U) as it:
                    for q in range(SETS):
                        wait(net, pool, s["weighed"], it * U + (q + 1) * SET)
                        pool.tensor_copy(b["idx_i"][:, q, :], net.step_src[:, bass.ds((it * SETS + q) * SET, SET)]).then_inc(s["idx_ready"], 1)
                        wait_apart(net, pool, s["idx_ready"], it * SETS + q + 1)
                        for r in range(SET):
                            pool.indirect_dma_start(b["got"][:, q * SET + r, :], None, net.table,
                                                    bass.IndirectOffsetOnAxis(ap=b["idx_i"][:, q, r:r + 1], axis=0)).then_inc(landed[q], 16)

            @block.scalar
            def _(act):
                act.sem_inc(s["weighed"], U)
                with act.Fori(0, STEPS // U) as it:
                    for q in range(SETS):
                        wait(net, act, landed[q], (it + 1) * 16 * SET)
                        for r in range(SET):
                            wait(net, act, s["mm"], it * U + q * SET + r + 1)
                            for h in range(H):
                                ins = act.activation(b["wx"][:, r, h * 64:(h + 1) * 64], b["got"][:, q * SET + r, h * 64:(h + 1) * 64], ACT.Copy,
                                                     scale=net.edge[:, bass.ds((it * U + q * SET + r) * H + h, 1)])
                            ins.then_inc(s["weighed"], 1)

            @block.tensor
            def _(pe):
                pe.sem_inc(s["mm"], RING)
                with pe.Fori(0, STEPS // U) as it:
                    for u in range(U):
                        r = u % RING
                        ps = net.PS[r]
                        wait(net, pe, s["hot"], it * U + u + 1)
                        wait(net, pe, s["weighed"], it * U + u + 1 + U)
                        pe.matmul(ps[:, 0:D], b["hot"][:, r, :], b["wx"][:, r, :], start=True, stop=True)
                        pe.matmul(ps[:, D:D + H], b["hot"][:, r, :], net.edge[:, bass.ds((it * U + u) * H, H)], start=True, stop=True).then_inc(s["mm"], 1)

            @block.vector
            def _(dve):
                dve.memset(aggf, 0.0)
                dve.wait_ge(s["where_in"], 16)

                def one_hot(step, u):
                    wait(net, dve, s["mm"], step + u + 1)
                    dve.tensor_scalar(b["hot"][:, u % RING, :], net.const("iota"), net.step_dst[:, bass.ds(step + u, 1)], None,
                                      ALU.is_equal).then_inc(s["hot"], 1)

                def add(step, u):
                    at = dve.value_load(where[0:1, bass.ds(step + u, 1)], min_val=0, max_val=(TILES - 1) * (D + H))
                    wait(net, dve, s["mm"], step + u + 1 + RING)
                    dve.tensor_tensor(aggf[:, bass.ds(at, D + H)], aggf[:, bass.ds(at, D + H)], net.PS[u % RING][:, 0:D + H], ALU.add)
                    dve.drain()

                with dve.Fori(0, STEPS // U) as it:
                    for u in range(U + RING - 1):
                        if u >= RING - 1:
                            add(it * U, u - RING + 1)
                        if u < U:
                            one_hot(it * U, u)


def layer_norm(net, dve, s, b, x, out, value, gain=None, shift=None):
    dve.bn_stats(b["six"][:, :], x)
    dve.drain()
    dve.bn_aggr(b["mv"][:, :], b["six"][:, :])
    dve.drain()
    dve.tensor_scalar(b["var"][:, :], b["mv"][:, 1:2], LN_EPS, None, ALU.add).then_inc(s["var_ready"], 1)
    wait(net, dve, s["rstd_ready"], value)
    dve.tensor_scalar(out, x, b["mv"][:, 0:1], b["rs"][:, :], ALU.subtract, ALU.mult)
    dve.drain()
    if gain is not None:
        dve.tensor_tensor(out, out, gain, ALU.mult)
        dve.drain()
        dve.tensor_tensor(out, out, shift, ALU.add)
        dve.drain()


def norm_power(net, pool, s, b, value):
    wait(net, pool, s["var_ready"], value)
    pool.tensor_tensor(b["rs"][:, :], b["var"][:, :], net.const("mhalf"), ALU.pow).then_inc(s["rstd_ready"], 1)


def top_two(dve, net, n, g, b):
    pair = lambda t: t[:, 0:n * n].rearrange("p (e j) -> p e j", e=n)
    mine = g.unsqueeze(2).to_broadcast([P, n, n])
    theirs = g.unsqueeze(1).to_broadcast([P, n, n])
    dve.tensor_tensor(pair(b["gt"]), theirs, mine, ALU.is_gt)
    dve.tensor_tensor(pair(b["eq"]), theirs, mine, ALU.is_equal)
    dve.drain()
    dve.tensor_tensor(pair(b["eq"]), pair(b["eq"]), pair(b["before"]), ALU.mult)
    dve.drain()
    dve.tensor_tensor(pair(b["gt"]), pair(b["gt"]), pair(b["eq"]), ALU.add)
    dve.drain()
    dve.tensor_reduce(b["sel"][:, 0:n], pair(b["gt"]), AX.X, ALU.add)
    dve.drain()
    dve.tensor_scalar(b["sel"][:, 0:n], b["sel"][:, 0:n], 2.0, None, ALU.is_lt)
    dve.drain()


def make_before(dve, n, b):
    dve.memset(b["before"][:, :], 0.0)
    dve.drain()
    for e in range(1, n):
        dve.memset(b["before"][:, e * n:e * n + e], 1.0)


def gates(net, dve, s, b, t):
    dve.tensor_reduce(b["gmax"][:, :], net.PS[2][:, 0:4], AX.X, ALU.max)
    dve.drain()
    dve.tensor_scalar(b["g"][:, :], net.PS[2][:, 0:4], b["gmax"][:, :], None, ALU.subtract).then_inc(s["gexp_in"], 1)
    wait(net, dve, s["gexp"], t + 1)
    dve.tensor_reduce(b["gsum"][:, :], b["g"][:, :], AX.X, ALU.add)
    dve.drain()
    dve.reciprocal(b["gsum"][:, :], b["gsum"][:, :])
    dve.drain()
    dve.tensor_scalar(b["g"][:, :], b["g"][:, :], b["gsum"][:, :], None, ALU.mult)
    dve.drain()
    top_two(dve, net, 4, b["g"][:, :], b)
    dve.tensor_reduce(b["gmax"][:, :], b["g"][:, :], AX.X, ALU.max)
    dve.drain()
    dve.tensor_scalar(b["g"][:, :], b["g"][:, :], b["gmax"][:, :], None, ALU.subtract).then_inc(s["g2_in"], 1)
    wait(net, dve, s["g2"], t + 1)
    dve.tensor_tensor(b["sel"][:, :], b["sel"][:, :], b["g"][:, :], ALU.mult)
    dve.drain()
    dve.tensor_reduce(b["gsum"][:, :], b["sel"][:, :], AX.X, ALU.add)
    dve.drain()
    dve.reciprocal(b["gsum"][:, :], b["gsum"][:, :])
    dve.drain()
    dve.tensor_scalar(b["sel"][:, :], b["sel"][:, :], b["gsum"][:, :], None, ALU.mult)
    dve.drain()


def combine_stage(nc, net):
    with ExitStack() as c:
        b = buffers(nc, c, "comb", wq=[2, D], wres=[2, D], wm=[2, D], w1=[4, 512], w2=[4, D], norms=[4, D],
                    f1=[2, 768], f1b=[6], f2=[2, P], f2b=[1], e2=[4, 64], eb2=[4], f3=[D], b3=[D], e3=[4, D], gw=[2, 4], gb=[4],
                    xn=[D], cat=[4, P], qx=[D], qe=[D], den=[8], msg=[D], hT=[4, P], sum=[D], rden=[4], nb=[D],
                    six=[6], mv=[2], var=[1], rs=[1], yT=[2, P], h1=[6, P], h2=[P], h2e=[4, P],
                    gt=[16], eq=[16], before=[16], sel=[4], g=[4], gmax=[1], gsum=[1], x1=[D], y=[D])
        B = net.PS
        names = ["w_in", "xn", "tr_x", "xT", "q", "qmin", "qexp", "qe", "msg", "msgn", "tr_m", "mT", "wm", "m1", "tr_1", "oT",
                 "h", "hr", "w2", "x1y", "tr_y", "yT", "f1", "f1r", "f2", "f2r", "f3", "gl", "gexp_in", "gexp", "g2_in", "g2",
                 "var_ready", "rstd_ready", "done"]
        with stage(nc, "comb", names) as (block, s):
            ident = net.const("ident")

            @block.sync
            def _(sp):
                i = net.inp
                loads = [(b["wq"][:, :, :], weight(i["m0_wq"])), (b["wres"][:, :, :], weight(i["g0_res"])), (b["wm"][:, :, :], weight(i["m0_wm"])),
                         (b["w1"][:, :, :], weight(i["m0_w1"])), (b["w2"][:, :, :], weight(i["m0_w2"])),
                         (b["norms"][:, :, :].rearrange("p a b -> p (a b)"), i["m0_norms"].to_broadcast([P, 4 * D])),
                         (b["f1"][:, :, :], weight(i["f0_w1"])), (b["f1b"][:, :], i["f0_b1"]), (b["f2"][:, :, :], weight(i["f0_w2"])),
                         (b["f2b"][:, :], i["f0_b2"]), (b["e2"][:, :, :].rearrange("p a b -> p (a b)"), i["f0_e2"]), (b["eb2"][0:64, :], i["f0_eb2"]),
                         (b["f3"][:, :], i["f0_w3"]), (b["b3"][0:1, :], i["f0_b3"]), (b["e3"][0:64, :, :].rearrange("p a b -> p (a b)"), i["f0_e3"]),
                         (b["e3"][64:65, :, :].rearrange("p a b -> p (a b)"), i["f0_eb3"]), (b["gw"][:, :, :], weight(i["f0_gw"])), (b["gb"][0:1, :], i["f0_gb"])]
                for dst, src in loads:
                    sp.dma_start(dst, src).then_inc(s["w_in"], 16)
                sp.wait_ge(s["w_in"], 16 * len(loads))
                sp.sem_inc(s["done"], 1)

            @block.gpsimd
            def _(pool):
                with pool.Fori(0, TILES) as t:
                    for k in range(3):
                        norm_power(net, pool, s, b, 3 * t + k + 1)

            @block.tensor
            def _(pe):
                pe.wait_ge(s["done"], 1)
                ones = net.const("ones")

                def turn(out, src, n):
                    for k in range(n):
                        ins = pe.transpose(out[:, k * P:(k + 1) * P], src[:, k * P:(k + 1) * P], ident)
                    return ins

                def product(out, parts):
                    for k, (l, r) in enumerate(parts):
                        ins = pe.matmul(out, l, r, start=(k == 0), stop=(k == len(parts) - 1))
                    return ins

                with pe.Fori(0, TILES) as t:
                    wait(net, pe, s["xn"], t + 1)
                    turn(B[0], b["xn"], 2).then_inc(s["tr_x"], 1)
                    wait(net, pe, s["xT"], t + 1)
                    for i in range(2):
                        ins = product(B[1][:, i * P:(i + 1) * P], [(b["wq"][:, k, i * P:(i + 1) * P], b["cat"][:, k, :]) for k in range(2)])
                    ins.then_inc(s["q"], 1)
                    product(B[4][:, 0:D], [(b["cat"][:, k, :], b["wres"][:, k, :]) for k in range(2)])
                    wait(net, pe, s["qe"], t + 1)
                    for i in range(2):
                        product(B[2][:, i * P:(i + 1) * P], [(b["qe"][:, i * P:(i + 1) * P], net.kv[:, i, :])])
                        ins = product(B[2][:, D + 4 * i:D + 4 * i + 4], [(b["qe"][:, i * P:(i + 1) * P], net.ksum[:, i, :])])
                    ins.then_inc(s["msg"], 1)
                    wait(net, pe, s["msgn"], t + 1)
                    turn(B[0], b["msg"], 2).then_inc(s["tr_m"], 1)
                    wait(net, pe, s["mT"], t + 1)
                    product(B[1][:, 0:D], [(b["cat"][:, 2 + k, :], b["wm"][:, k, :]) for k in range(2)]).then_inc(s["wm"], 1)
                    wait(net, pe, s["m1"], t + 1)
                    turn(B[0], b["msg"], 2).then_inc(s["tr_1"], 1)
                    wait(net, pe, s["oT"], t + 1)
                    for i in range(4):
                        ins = product(B[3][:, i * P:(i + 1) * P], [(b["w1"][:, k, i * P:(i + 1) * P], b["cat"][:, k, :]) for k in range(4)])
                    ins.then_inc(s["h"], 1)
                    wait(net, pe, s["hr"], t + 1)
                    product(B[2][:, 0:D], [(b["hT"][:, k, :], b["w2"][:, k, :]) for k in range(4)]).then_inc(s["w2"], 1)
                    wait(net, pe, s["x1y"], t + 1)
                    turn(B[0], b["y"], 2).then_inc(s["tr_y"], 1)
                    wait(net, pe, s["yT"], t + 1)
                    product(B[2][:, 0:4], [(b["yT"][:, k, :], b["gw"][:, k, :]) for k in range(2)] + [(ones[0:1, :], b["gb"][0:1, :])]).then_inc(s["gl"], 1)
                    for i in range(6):
                        out = B[5][:, i * P:(i + 1) * P] if i < 4 else B[6][:, (i - 4) * P:(i - 3) * P]
                        ins = product(out, [(b["f1"][:, k, i * P:(i + 1) * P], b["yT"][:, k, :]) for k in range(2)])
                    ins.then_inc(s["f1"], 1)
                    wait(net, pe, s["f1r"], t + 1)
                    product(B[3][:, 0:P], [(b["f2"][:, k, :], b["h1"][:, k, :]) for k in range(2)])
                    for e in range(4):
                        ins = product(B[7][0:64, e * P:(e + 1) * P], [(b["e2"][:, e, :], b["h1"][:, 2 + e, :])])
                    ins.then_inc(s["f2"], 1)
                    wait(net, pe, s["f2r"], t + 1)
                    product(B[1][:, 0:D], [(b["h2"][:, :], b["f3"][:, :]), (ones[0:1, :], b["b3"][0:1, :])])
                    for e in range(4):
                        ins = product(B[5 + e // 2][:, (e % 2) * D:(e % 2 + 1) * D], [(b["h2e"][0:65, e, :], b["e3"][0:65, e, :])])
                    ins.then_inc(s["f3"], 1)

            @block.scalar
            def _(act):
                copy = lambda dst, src: act.activation(dst, src, ACT.Copy)
                act.wait_ge(s["done"], 1)
                with act.Fori(0, TILES) as t:
                    wait(net, act, s["tr_x"], t + 1)
                    copy(b["cat"][:, 0:2, :].rearrange("p a b -> p (a b)"), B[0][:, 0:D]).then_inc(s["xT"], 1)
                    wait(net, act, s["qmin"], t + 1)
                    act.activation(b["qx"][:, :], b["qx"][:, :], ACT.Exp).then_inc(s["qexp"], 1)
                    wait(net, act, s["tr_m"], t + 1)
                    copy(b["cat"][:, 2:4, :].rearrange("p a b -> p (a b)"), B[0][:, 0:D]).then_inc(s["mT"], 1)
                    wait(net, act, s["tr_1"], t + 1)
                    copy(b["cat"][:, 2:4, :].rearrange("p a b -> p (a b)"), B[0][:, 0:D]).then_inc(s["oT"], 1)
                    wait(net, act, s["h"], t + 1)
                    act.activation(b["hT"][:, :, :].rearrange("p a b -> p (a b)"), B[3][:, :], ACT.Relu).then_inc(s["hr"], 1)
                    wait(net, act, s["tr_y"], t + 1)
                    copy(b["yT"][:, :, :].rearrange("p a b -> p (a b)"), B[0][:, 0:D]).then_inc(s["yT"], 1)
                    wait(net, act, s["gexp_in"], t + 1)
                    act.activation(b["g"][:, :], b["g"][:, :], ACT.Exp).then_inc(s["gexp"], 1)
                    wait(net, act, s["f1"], t + 1)
                    for i in range(6):
                        src = B[5][:, i * P:(i + 1) * P] if i < 4 else B[6][:, (i - 4) * P:(i - 3) * P]
                        ins = act.activation(b["h1"][:, i, :], src, ACT.Relu, bias=b["f1b"][:, i:i + 1])
                    ins.then_inc(s["f1r"], 1)
                    wait(net, act, s["f2"], t + 1)
                    act.activation(b["h2"][:, :], B[3][:, 0:P], ACT.Relu, bias=b["f2b"][:, :])
                    for e in range(4):
                        ins = act.activation(b["h2e"][0:64, e, :], B[7][0:64, e * P:(e + 1) * P], ACT.Relu, bias=b["eb2"][0:64, e:e + 1])
                    ins.then_inc(s["f2r"], 1)
                    wait(net, act, s["g2_in"], t + 1)
                    act.activation(b["g"][:, :], b["g"][:, :], ACT.Exp).then_inc(s["g2"], 1)

            @block.vector
            def _(dve):
                heads = lambda a, n: a.rearrange("p (h d) -> p h d", h=n)
                spread = lambda a, n, d: a.unsqueeze(2).to_broadcast([P, n, d])
                norm = lambda k: b["norms"][:, k, :]
                make_before(dve, 4, b)
                dve.memset(b["h2e"][64:65, :, :], 1.0)
                dve.wait_ge(s["done"], 1)
                with dve.Fori(0, TILES) as t:
                    x = rows(net.X[:, bass.ds(t, 1), :])
                    dve.tensor_scalar(b["xn"][:, :], x, net.rstd[:, bass.ds(t, 1)], net.shift[:, bass.ds(t, 1)], ALU.mult, ALU.add).then_inc(s["xn"], 1)
                    wait(net, dve, s["q"], t + 1)
                    dve.tensor_scalar(b["qx"][:, :], B[1][:, 0:D], 0.0, None, ALU.min).then_inc(s["qmin"], 1)
                    wait(net, dve, s["qexp"], t + 1)
                    dve.scalar_tensor_tensor(b["qe"][:, :], B[1][:, 0:D], 0.0, b["qx"][:, :], ALU.max, ALU.add).then_inc(s["qe"], 1)
                    wait(net, dve, s["msg"], t + 1)
                    dve.tensor_scalar(b["den"][:, :], B[2][:, D:D + 8], 1e-6, None, ALU.add)
                    dve.drain()
                    dve.reciprocal(b["den"][:, :], b["den"][:, :])
                    dve.drain()
                    dve.tensor_tensor(heads(b["msg"][:, :], 8), heads(B[2][:, 0:D], 8), spread(b["den"][:, :], 8, 32), ALU.mult).then_inc(s["msgn"], 1)
                    agg = rows(net.agg[:, bass.ds(t, 1), :])
                    dve.tensor_scalar(b["rden"][:, :], agg[:, D:D + H], 1e-9, None, ALU.max)
                    dve.drain()
                    dve.reciprocal(b["rden"][:, :], b["rden"][:, :])
                    dve.drain()
                    dve.tensor_tensor(heads(b["sum"][:, :], H), heads(agg[:, 0:D], H), spread(b["rden"][:, :], H, 64), ALU.mult)
                    dve.drain()
                    dve.tensor_tensor(b["sum"][:, :], b["sum"][:, :], B[4][:, 0:D], ALU.add)
                    dve.drain()
                    dve.scalar_tensor_tensor(b["sum"][:, :], b["sum"][:, :], 0.0, x, ALU.max, ALU.add)
                    dve.drain()
                    dve.tensor_tensor(b["sum"][:, :], b["sum"][:, :], b["xn"][:, :], ALU.add)
                    wait(net, dve, s["wm"], t + 1)
                    layer_norm(net, dve, s, b, B[1][:, 0:D], b["msg"][:, :], 3 * t + 1, norm(0), norm(1))
                    dve.sem_inc(s["m1"], 1)
                    wait(net, dve, s["w2"], t + 1)
                    layer_norm(net, dve, s, b, B[2][:, 0:D], b["nb"][:, :], 3 * t + 2, norm(2), norm(3))
                    dve.tensor_tensor(b["x1"][:, :], b["sum"][:, :], b["nb"][:, :], ALU.add)
                    dve.drain()
                    layer_norm(net, dve, s, b, b["x1"][:, :], b["y"][:, :], 3 * t + 3)
                    dve.sem_inc(s["x1y"], 1)
                    wait(net, dve, s["gl"], t + 1)
                    gates(net, dve, s, b, t)
                    wait(net, dve, s["f3"], t + 1)
                    dve.tensor_tensor(b["x1"][:, :], b["x1"][:, :], B[1][:, 0:D], ALU.add)
                    dve.drain()
                    for e in range(4):
                        src = B[5 + e // 2][:, (e % 2) * D:(e % 2 + 1) * D]
                        if e < 3:
                            dve.scalar_tensor_tensor(b["x1"][:, :], src, b["sel"][:, e:e + 1], b["x1"][:, :], ALU.mult, ALU.add)
                        else:
                            dve.scalar_tensor_tensor(x, src, b["sel"][:, e:e + 1], b["x1"][:, :], ALU.mult, ALU.add)
                        dve.drain()


def products(pe, out, parts):
    for k, (left, right) in enumerate(parts):
        ins = pe.matmul(out, left, right, start=(k == 0), stop=(k == len(parts) - 1))
    return ins


def turned(pe, net, out, src, n):
    for k in range(n):
        ins = pe.transpose(out[:, k * P:(k + 1) * P], src[:, k * P:(k + 1) * P], net.const("ident"))
    return ins


def project1_stage(nc, net):
    with ExitStack() as c:
        b = buffers(nc, c, "proj1", w=[2, 264], wT=[2, D], al=[2, 8], wkv=[2, 512], bkv=[512], xn=[D], xnT=[2, P],
                    tab=[D], top=[D], pen=[TILES], col=[2], diag=[2, P])
        p_tr, p_tab, p_k, p_top = net.PS[0:4]
        names = ["w_in", "loaded", "folded", "fold_ps", "xn", "tr", "xnT", "mm", "k_used", "tab_sb", "tab_out", "end", "top", "top_tr", "diag", "top_row"]
        with stage(nc, "proj1", names) as (block, s):
            @block.sync
            def _(sp):
                for dst, src in ((b["w"][:, :, 0:D], weight(net.inp["g1_w"])), (b["wT"][:, :, :], weight(net.inp["g1_wT"])),
                                 (b["al"][:, :, :], weight(net.inp["g1_al"])), (b["wkv"][:, :, :], weight(net.inp["m1_wkv"])),
                                 (b["bkv"][0:1, :], net.inp["m1_bkv"])):
                    sp.dma_start(dst, src).then_inc(s["w_in"], 16)
                with sp.Fori(0, TILES) as t:
                    wait(net, sp, s["tab_sb"], t + 1)
                    sp.dma_start(net.table[bass.ds(t * P, P), :], b["tab"][:, 0:D]).then_inc(s["tab_out"], 16)
                sp.wait_ge(s["end"], 1)
                sp.dma_start(net.src_tab.rearrange("(t p) c -> p t c", p=P), net.node_src[:, :, :]).then_inc(s["tab_out"], 16)
                sp.wait_ge(s["tab_out"], 16 * (TILES + 1) + 1)

            @block.vector
            def _(dve):
                dve.memset(b["top"][:, :], -BIG)
                dve.tensor_scalar(b["pen"][:, :], net.const("valid"), BIG, BIG, ALU.mult, ALU.subtract)
                dve.wait_ge(s["fold_ps"], 1)
                for i in range(2):
                    ins = dve.tensor_copy(b["w"][:, i, D:D + 8], p_tab[:, 8 * i:8 * i + 8])
                ins.then_inc(s["folded"], 1)
                with dve.Fori(0, TILES) as t:
                    dve.tensor_scalar(b["xn"][:, :], rows(net.X[:, bass.ds(t, 1), :]), net.rstd[:, bass.ds(t, 1)],
                                      net.shift[:, bass.ds(t, 1)], ALU.mult, ALU.add).then_inc(s["xn"], 1)
                    wait(net, dve, s["mm"], t + 1)
                    dve.scalar_tensor_tensor(b["top"][:, :], p_k[:, 0:D], b["pen"][:, bass.ds(t, 1)], b["top"][:, :], ALU.add, ALU.max).then_inc(s["k_used"], 1)
                    dve.drain()
                dve.sem_inc(s["top"], 1)
                dve.wait_ge(s["top_tr"], 1)
                dve.tensor_reduce(b["col"][:, :], p_top[:, 0:D].rearrange("p (a b) -> p a b", a=2), AX.X, ALU.max)
                dve.drain()
                for i in range(2):
                    ins = dve.tensor_scalar(b["diag"][:, i, :], net.const("ident"), b["col"][:, i:i + 1], None, ALU.mult)
                ins.then_inc(s["diag"], 1)
                dve.wait_ge(s["top_row"], 1)
                dve.tensor_copy(net.key_top[:, :], p_tr[:, 0:D])

            @block.scalar
            def _(act):
                act.sem_inc(s["tab_out"], 1)
                with act.Fori(0, TILES) as t:
                    wait(net, act, s["tr"], t + 1)
                    act.activation(rows(b["xnT"][:, :, :]), p_tr[:, 0:D], ACT.Copy).then_inc(s["xnT"], 1)
                    wait(net, act, s["mm"], t + 1)
                    act.activation(net.node_src[:, bass.ds(t, 1), :].rearrange("p a b -> p (a b)"), p_tab[:, D:D + 4], ACT.Copy)
                    act.activation(net.node_dst[:, bass.ds(t, 1), :].rearrange("p a b -> p (a b)"), p_tab[:, D + 4:D + 8], ACT.Copy)
                    wait(net, act, s["tab_out"], 16 * t + 1)
                    act.activation(b["tab"][:, 0:D], p_tab[:, 0:D], ACT.Copy).then_inc(s["tab_sb"], 1)
                act.sem_inc(s["end"], 1)

            @block.tensor
            def _(pe):
                pe.wait_ge(s["w_in"], 80)
                for i in range(2):
                    ins = products(pe, p_tab[:, 8 * i:8 * i + 8], [(b["wT"][:, k, i * P:(i + 1) * P], b["al"][:, k, :]) for k in range(2)])
                ins.then_inc(s["fold_ps"], 1)
                pe.wait_ge(s["folded"], 1)
                pe.sem_inc(s["k_used"], 1)
                with pe.Fori(0, TILES) as t:
                    wait(net, pe, s["xn"], t + 1)
                    turned(pe, net, p_tr, b["xn"], 2).then_inc(s["tr"], 1)
                    wait(net, pe, s["xnT"], t + 1)
                    products(pe, p_tab[:, 0:264], [(b["xnT"][:, k, :], b["w"][:, k, :]) for k in range(2)])
                    wait(net, pe, s["k_used"], t + 1)
                    products(pe, p_k[:, 0:D], [(b["xnT"][:, k, :], b["wkv"][:, k, 0:D]) for k in range(2)] +
                             [(net.const("ones")[0:1, :], b["bkv"][0:1, 0:D])]).then_inc(s["mm"], 1)
                pe.wait_ge(s["top"], 1)
                turned(pe, net, p_top, b["top"], 2).then_inc(s["top_tr"], 1)
                pe.wait_ge(s["diag"], 1)
                pe.matmul(p_tr[:, 0:D], net.const("ones"), b["diag"][:, :, :].rearrange("p a b -> p (a b)"), start=True, stop=True).then_inc(s["top_row"], 1)


def lambda_stage(nc, net):
    with ExitStack() as c:
        b = buffers(nc, c, "lam", wkv=[2, 512], bkv=[512], cols=[2, 3], xn=[D], xnT=[2, P], kx=[D], v=[D + 4], acc=[2, D + 4],
                    sum=[2], six=[2, 6], mv=[2, 2], var=[2], rs=[2], xf=[2])
        p_tr, p_kv, p_l0, p_l1 = net.PS[0:4]
        names = ["w_in", "xn", "tr", "xnT", "mm", "kx", "kexp", "v_ready", "kv_ready", "lam_mm", "var_ready", "rstd_ready"]
        with stage(nc, "lam", names) as (block, s):
            @block.sync
            def _(sp):
                for dst, src in ((b["wkv"][:, :, :], weight(net.inp["m1_wkv"])), (b["bkv"][0:1, :], net.inp["m1_bkv"]),
                                 (b["cols"][:, :, :].rearrange("p a b -> p (a b)"), net.inp["m1_cols"])):
                    sp.dma_start(dst, src).then_inc(s["w_in"], 16)

            @block.vector
            def _(dve):
                dve.memset(b["acc"][:, :, :], 0.0)
                dve.wait_ge(s["w_in"], 48)
                with dve.Fori(0, TILES) as t:
                    dve.tensor_scalar(b["xn"][:, :], rows(net.X[:, bass.ds(t, 1), :]), net.rstd[:, bass.ds(t, 1)],
                                      net.shift[:, bass.ds(t, 1)], ALU.mult, ALU.add).then_inc(s["xn"], 1)
                    wait(net, dve, s["mm"], t + 1)
                    dve.tensor_tensor(b["kx"][:, :], p_kv[:, 0:D], net.key_top[:, :], ALU.subtract).then_inc(s["kx"], 1)
                    dve.tensor_copy(b["v"][:, 0:D], p_kv[:, D:2 * D])
                    dve.memset(b["v"][:, D:D + 1], 1.0)
                    wait(net, dve, s["kexp"], t + 1)
                    dve.tensor_scalar(b["kx"][:, :], b["kx"][:, :], net.const("valid")[:, bass.ds(t, 1)], None, ALU.mult).then_inc(s["kv_ready"], 1)
                    wait(net, dve, s["lam_mm"], t + 1)
                    for i, ps in enumerate((p_l0, p_l1)):
                        dve.tensor_tensor(b["acc"][:, i, 0:D + 1], b["acc"][:, i, 0:D + 1], ps[:, 0:D + 1], ALU.add)
                    dve.drain()
                for i in range(2):
                    dve.reciprocal(b["sum"][:, i:i + 1], b["acc"][:, i, D:D + 1])
                    dve.drain()
                    dve.tensor_scalar(b["acc"][:, i, 0:D], b["acc"][:, i, 0:D], b["sum"][:, i:i + 1], None, ALU.mult)
                    dve.drain()
                    dve.bn_stats(b["six"][:, i, :], b["acc"][:, i, 0:D])
                    dve.drain()
                    dve.bn_aggr(b["mv"][:, i, :], b["six"][:, i, :])
                    dve.drain()
                dve.tensor_scalar(b["var"][:, :], b["mv"][:, :, 1], 1e-5, None, ALU.add).then_inc(s["var_ready"], 1)
                dve.wait_ge(s["rstd_ready"], 1)
                dve.tensor_tensor(b["rs"][:, :], b["rs"][:, :], b["cols"][:, :, 1], ALU.mult)
                dve.drain()
                for i in range(2):
                    dve.tensor_scalar(net.lam[:, i, :], b["acc"][:, i, 0:D], b["mv"][:, i, 0:1], b["rs"][:, i:i + 1], ALU.subtract, ALU.mult)
                dve.drain()
                for i in range(2):
                    dve.tensor_scalar(net.lam[:, i, :], net.lam[:, i, :], b["cols"][:, i, 2:3], None, ALU.add)

            @block.gpsimd
            def _(pool):
                pool.wait_ge(s["var_ready"], 1)
                pool.tensor_tensor(b["rs"][:, :], b["var"][:, :], net.const("mhalf").to_broadcast([P, 2]), ALU.pow).then_inc(s["rstd_ready"], 1)

            @block.scalar
            def _(act):
                with act.Fori(0, TILES) as t:
                    wait(net, act, s["tr"], t + 1)
                    act.activation(rows(b["xnT"][:, :, :]), p_tr[:, 0:D], ACT.Copy).then_inc(s["xnT"], 1)
                    wait(net, act, s["kx"], t + 1)
                    act.activation(b["kx"][:, :], b["kx"][:, :], ACT.Exp).then_inc(s["kexp"], 1)

            @block.tensor
            def _(pe):
                pe.wait_ge(s["w_in"], 48)
                with pe.Fori(0, TILES) as t:
                    wait(net, pe, s["xn"], t + 1)
                    turned(pe, net, p_tr, b["xn"], 2).then_inc(s["tr"], 1)
                    wait(net, pe, s["xnT"], t + 1)
                    products(pe, p_kv[:, :], [(b["xnT"][:, k, :], b["wkv"][:, k, :]) for k in range(2)] +
                             [(net.const("ones")[0:1, :], b["bkv"][0:1, :])]).then_inc(s["mm"], 1)
                    wait(net, pe, s["kv_ready"], t + 1)
                    for i, ps in enumerate((p_l0, p_l1)):
                        ins = pe.matmul(ps[:, 0:D + 1], b["kx"][:, i * P:(i + 1) * P], b["v"][:, 0:D + 1], start=True, stop=True)
                    ins.then_inc(s["lam_mm"], 1)


def rank_work(nc, net, c, block, s, b):
    flat = net.agg[:, :, :].rearrange("p a b -> p (a b)")
    row, sink = flat[:, 0:NPAD], flat[:, NPAD:NPAD + NPAD // 2]
    d = buffers(nc, c, "rank", key=[TILES], noise=[TILES], part=[4, TILES], far=[TILES])

    @block.sync
    def _(sp):
        sp.wait_ge(s["w0"], 1)
        with nc.allow_non_contiguous_dma("one number a node"):
            sp.dma_start(d["noise"][:, 0:TILES - 1], net.inp["noise"][:, 0:(TILES - 1) * P].rearrange("o (t p) -> p (o t)", p=P)).then_inc(s["w1"], 16)
            sp.dma_start(d["noise"][0:LAST, TILES - 1:TILES], net.inp["noise"][:, (TILES - 1) * P:N].rearrange("o (t p) -> p (o t)", p=LAST)).then_inc(s["w1"], 16)
            sp.wait_ge(s["w2"], 1)
            sp.dma_start(net.keys.rearrange("o (t p) -> p (o t)", p=P), d["key"][:, :]).then_inc(s["w3"], 16)
        sp.wait_ge(s["w3"], 16)
        sp.dma_start(row, net.keys.to_broadcast([P, NPAD])).then_inc(s["deg_hot"], 16)

    @block.vector
    def _(dve):
        dve.memset(d["noise"][:, :], 0.0).then_inc(s["w0"], 1)
        dve.memset(d["part"][:, :, :], 0.0)
        dve.wait_ge(s["w1"], 32)
        dve.tensor_tensor(d["key"][:, :], net.src_degree[:, :], d["noise"][:, :], ALU.add)
        dve.drain()
        dve.tensor_tensor(d["key"][:, :], d["key"][:, :], net.const("valid"), ALU.mult)
        dve.tensor_scalar(d["far"][:, :], net.const("valid"), -BIG, BIG, ALU.mult, ALU.add)
        dve.drain()
        dve.tensor_tensor(d["key"][:, :], d["key"][:, :], d["far"][:, :], ALU.add).then_inc(s["w2"], 1)
        dve.wait_ge(s["deg_hot"], 16)
        half = NPAD // 2

        def count(t, k, lo, hi, op):
            for a in range(lo, hi, half):
                z = min(hi, a + half)
                kk = k + (a > lo)
                dve.tensor_scalar(sink[:, 0:z - a], row[:, a:z], d["key"][:, t:t + 1], None, op, ALU.add, accum_out=d["part"][:, kk, t:t + 1])
                dve.drain()

        for t in range(TILES):
            lo, hi = t * P, (t + 1) * P
            count(t, 0, 0, lo, ALU.is_le)
            for k, (first, last) in enumerate(((lo, NPAD),)):
                for a in range(first, last, half):
                    z = min(last, a + half)
                    dve.tensor_scalar(sink[:, 0:z - a], row[:, a:z], d["key"][:, t:t + 1], None, ALU.is_lt, ALU.add,
                                      accum_out=d["far"][:, t:t + 1])
                    dve.drain()
                    dve.tensor_tensor(d["part"][:, 2, t:t + 1], d["part"][:, 2, t:t + 1], d["far"][:, t:t + 1], ALU.add)
                    dve.drain()
            dve.scalar_tensor_tensor(sink[:, 0:P], row[:, lo:hi], d["key"][:, t:t + 1], net.const("lower"), ALU.is_equal, ALU.mult,
                                     accum_out=d["part"][:, 3, t:t + 1])
            dve.drain()
        for k in range(1, 4):
            dve.tensor_tensor(d["part"][:, 0, :], d["part"][:, 0, :], d["part"][:, k, :], ALU.add)
            dve.drain()
        dve.tensor_copy(net.rank[:, :], d["part"][:, 0, :])


def sort_stage(nc, net):
    R = 4
    with ExitStack() as c:
        b = buffers(nc, c, "sort", xn=[R, D])
        with stage(nc, "sort", ["xn", "gp_out0", "gp_out1", "gp_out2", "gp_out3"]) as (block, s):
            out = (s["gp_out0"], s["gp_out1"], s["gp_out2"], s["gp_out3"])

            @block.vector
            def _(dve):
                for t in range(TILES):
                    if t >= R:
                        dve.wait_ge(out[t % R], 16 * (t // R))
                    dve.tensor_scalar(b["xn"][:, t % R, :], net.X[:, t, :], net.rstd[:, t:t + 1], net.shift[:, t:t + 1],
                                      ALU.mult, ALU.add).then_inc(s["xn"], 1)

            @block.gpsimd
            def _(pool):
                for t in range(TILES):
                    pool.wait_ge(s["xn"], t + 1)
                    pool.indirect_dma_start(net.sorted_x, bass.IndirectOffsetOnAxis(ap=net.rank[:, t:t + 1], axis=0),
                                            b["xn"][:, t % R, :], None).then_inc(out[t % R], 16)
                for r in range(R):
                    pool.wait_ge(out[r], 16 * len(range(r, TILES, R)))


CHUNK = 448
PART = 112
CHUNKS = NPAD // CHUNK
STATES = 16
LOG1P = [2.0000000078777487, 0.6666631593508171, 0.4002485372345264, 0.2796141883488086, 0.28174657263251685]


def mamba_stage(nc, net):
    spare = net.edge
    with ExitStack() as c:
        b = buffers(nc, c, "mamba", w_in=[2, 512], w_x=[2, 48], w_dt=[D], w_out=[2, D], cols=[2, 23], neg=[2, STATES],
                    xs=[4, D], xsT=[2, CHUNK], raw=[2, CHUNK + 4], xc=[2, CHUNK], z=[2, CHUNK], dbc=[CHUNK], dt=[2, CHUNK],
                    dtx=[2, CHUNK], dA=[2, 2, CHUNK], dB=[2, CHUNK], h=[2, 2, CHUNK], state=[2, STATES])
        A2 = lambda t: t.rearrange("p a b -> p (a b)")
        tmp = [spare[:, i * 2 * CHUNK:(i + 1) * 2 * CHUNK] for i in range(5)]
        hc = spare[:, 10 * CHUNK:14 * CHUNK].rearrange("p (q i c) -> p q i c", q=2, i=2)
        yo = net.step_dst[:, 0:4 * D].rearrange("p (a d) -> p a d", a=4)
        B = net.PS
        names = ["w", "xs_in", "tr", "xsT", "in_mm", "raw", "conv", "silu", "x_mm", "dbc", "dt_mm", "sp_in", "sp_e", "dt_ready",
                 "bc", "dA", "dB", "h_ready", "hc", "y_mm", "state", "yz", "out_mm", "yo", "y_out", "z_ready", "neg", "halo"]
        with stage(nc, "mamba", names) as (block, s):
            @block.sync
            def _(sp):
                i = net.inp
                for dst, src in ((b["w_in"][:, :, :], weight(i["s_in"])), (b["w_x"][:, :, :], weight(i["s_x"])), (b["w_dt"][0:16, :], i["s_dt"]),
                                 (b["w_out"][:, :, :], weight(i["s_out"])), (A2(b["cols"][:, :, :]), i["s_cols"])):
                    sp.dma_start(dst, src).then_inc(s["w"], 16)
                sp.sem_inc(s["tr"], 1)
                with sp.Fori(0, CHUNKS) as j:
                    wait(net, sp, s["tr"], j + 1)
                    sp.dma_start(b["xs"][0:PART, :, :], net.sorted_x[bass.ds(j * CHUNK, CHUNK), :].rearrange("(a p) d -> p a d", p=PART)).then_inc(s["xs_in"], 16)
                    wait(net, sp, s["yo"], j + 1)
                    sp.dma_start(net.mamba_y[bass.ds(j * CHUNK, CHUNK), :].rearrange("(a p) d -> p a d", p=PART), yo[0:PART, :, :]).then_inc(s["y_out"], 16)
                sp.wait_ge(s["y_out"], 16 * CHUNKS + 1)

            @block.gpsimd
            def _(pool):
                with pool.Fori(0, CHUNKS) as j:
                    for k in range(STATES):
                        wait_apart(net, pool, s["h_ready"], j * STATES + k + 1)
                        pool.tensor_copy(b["state"][:, :, k], b["h"][:, k % 2, :, CHUNK - 1]).then_inc(s["state"], 1)

            @block.scalar
            def _(act):
                act.wait_ge(s["w"], 80)
                for i in range(2):
                    ins = act.activation(b["neg"][:, i, :], b["cols"][:, i, 7:23], ACT.Exp)
                ins.then_inc(s["neg"], 1)
                act.wait_ge(s["neg"], 2)
                act.sem_inc(s["y_out"], 1)
                with act.Fori(0, CHUNKS) as j:
                    wait(net, act, s["tr"], j + 2)
                    for i in range(2):
                        ins = act.activation(b["xsT"][:, i, :], B[i][:, 0:CHUNK], ACT.Copy)
                    ins.then_inc(s["xsT"], 1)
                    wait(net, act, s["in_mm"], j + 1)
                    wait(net, act, s["halo"], j + 1)
                    for i in range(2):
                        ins = act.activation(b["raw"][:, i, 3:3 + CHUNK], B[2 + i][:, 0:CHUNK], ACT.Copy)
                    ins.then_inc(s["raw"], 1)
                    for i in range(2):
                        ins = act.activation(b["z"][:, i, :], B[4 + i][:, 0:CHUNK], ACT.Silu)
                    ins.then_inc(s["z_ready"], 1)
                    wait(net, act, s["conv"], j + 1)
                    for i in range(2):
                        ins = act.activation(b["xc"][:, i, :], tmp[0][:, i * CHUNK:(i + 1) * CHUNK], ACT.Silu, bias=b["cols"][:, i, 4:5])
                    ins.then_inc(s["silu"], 1)
                    wait(net, act, s["x_mm"], j + 1)
                    act.activation(b["dbc"][0:48, :], B[6][0:48, 0:CHUNK], ACT.Copy).then_inc(s["dbc"], 1)
                    wait(net, act, s["sp_in"], j + 1)
                    for i in range(2):
                        ins = act.activation(tmp[2][:, i * CHUNK:(i + 1) * CHUNK], tmp[1][:, i * CHUNK:(i + 1) * CHUNK], ACT.Exp, bias=b["cols"][:, i, 5:6])
                    ins.then_inc(s["sp_e"], 1)
                    wait(net, act, s["dt_ready"], j + 1)
                    for k in range(STATES):
                        wait(net, act, s["h_ready"], j * STATES + k - 1) if k >= 2 else None
                        for i in range(2):
                            ins = act.activation(b["dA"][:, k % 2, i, :], b["dt"][:, i, :], ACT.Exp, scale=b["neg"][:, i, k:k + 1])
                        ins.then_inc(s["dA"], 1)
                    wait(net, act, s["out_mm"], j + 1)
                    wait(net, act, s["y_out"], 16 * j + 1)
                    for a in range(4):
                        ins = act.activation(yo[0:PART, a, :], B[2 + a][0:PART, 0:D], ACT.Copy)
                    ins.then_inc(s["yo"], 1)

            @block.vector
            def _(dve):
                both = lambda ps: ps[:, 0:CHUNK].unsqueeze(1).to_broadcast([P, 2, CHUNK])
                dve.memset(b["state"][:, :, :], 0.0).then_inc(s["state"], 2)
                dve.memset(b["raw"][:, :, CHUNK:CHUNK + 3], 0.0)
                dve.wait_ge(s["neg"], 1)
                dve.tensor_scalar(A2(b["neg"][:, :, :]), A2(b["neg"][:, :, :]), -1.0, None, ALU.mult).then_inc(s["neg"], 1)
                with dve.Fori(0, CHUNKS) as j:
                    dve.drain()
                    for i in range(2):
                        ins = dve.tensor_copy(b["raw"][:, i, 0:3], b["raw"][:, i, CHUNK:CHUNK + 3])
                    ins.then_inc(s["halo"], 1)
                    wait(net, dve, s["raw"], j + 1)
                    for i in range(2):
                        u = tmp[0][:, i * CHUNK:(i + 1) * CHUNK]
                        for k in range(4):
                            tap, x = b["cols"][:, i, k:k + 1], b["raw"][:, i, k:k + CHUNK]
                            if k == 0:
                                ins = dve.tensor_scalar(u, x, tap, None, ALU.mult)
                            else:
                                dve.drain()
                                ins = dve.scalar_tensor_tensor(u, x, tap, u, ALU.mult, ALU.add)
                    ins.then_inc(s["conv"], 1)
                    wait(net, dve, s["dt_mm"], j + 1)
                    for i in range(2):
                        v, bias = B[2 + i][:, 0:CHUNK], b["cols"][:, i, 5:6]
                        dve.tensor_scalar(b["dt"][:, i, :], v, bias, 0.0, ALU.add, ALU.max)
                        dve.drain()
                        ins = dve.scalar_tensor_tensor(tmp[1][:, i * CHUNK:(i + 1) * CHUNK], b["dt"][:, i, :], -2.0, v, ALU.mult, ALU.add)
                    ins.then_inc(s["sp_in"], 1)
                    wait(net, dve, s["sp_e"], j + 1)
                    e, den, q, s2 = tmp[2], tmp[3], tmp[4], tmp[1]
                    dve.tensor_scalar(den, e, 2.0, None, ALU.add)
                    dve.drain()
                    dve.reciprocal(den, den)
                    dve.drain()
                    dve.tensor_tensor(e, e, den, ALU.mult)
                    dve.drain()
                    dve.tensor_tensor(s2, e, e, ALU.mult)
                    dve.drain()
                    dve.tensor_scalar(q, s2, LOG1P[-1], None, ALU.mult)
                    dve.drain()
                    for coeff in LOG1P[-2:0:-1]:
                        dve.scalar_tensor_tensor(q, q, coeff, s2, ALU.add, ALU.mult)
                        dve.drain()
                    dve.scalar_tensor_tensor(q, q, LOG1P[0], e, ALU.add, ALU.mult)
                    dve.drain()
                    dve.tensor_tensor(A2(b["dt"][:, :, :]), A2(b["dt"][:, :, :]), q, ALU.add).then_inc(s["dt_ready"], 1)
                    dve.drain()
                    wait(net, dve, s["silu"], j + 1)
                    dve.tensor_tensor(A2(b["dtx"][:, :, :]), A2(b["dt"][:, :, :]), A2(b["xc"][:, :, :]), ALU.mult)
                    dve.drain()
                    for k in range(STATES):
                        g = j * STATES + k + 1
                        wait(net, dve, s["bc"], g)
                        dve.tensor_tensor(b["dB"][:, :, :], b["dtx"][:, :, :], both(B[6 - 2 * (k % 2)]), ALU.mult)
                        dve.drain()
                        wait(net, dve, s["dA"], g)
                        wait(net, dve, s["state"], g)
                        for i in range(2):
                            ins = dve.tensor_tensor_scan(b["h"][:, k % 2, i, :], b["dA"][:, k % 2, i, :], b["dB"][:, i, :], b["state"][:, i, k:k + 1], ALU.mult, ALU.add)
                        ins.then_inc(s["h_ready"], 1)
                        dve.drain()
                        if k >= 2:
                            wait(net, dve, s["y_mm"], g - 2)
                        dve.tensor_tensor(hc[:, k % 2, :, :], b["h"][:, k % 2, :, :], both(B[7 - 2 * (k % 2)]), ALU.mult).then_inc(s["hc"], 1)
                    wait(net, dve, s["y_mm"], (j + 1) * STATES)
                    wait(net, dve, s["z_ready"], j + 1)
                    for i in range(2):
                        dve.scalar_tensor_tensor(b["dtx"][:, i, :], b["xc"][:, i, :], b["cols"][:, i, 6:7], B[i][:, 0:CHUNK], ALU.mult, ALU.add)
                    dve.drain()
                    dve.tensor_tensor(A2(b["dtx"][:, :, :]), A2(b["dtx"][:, :, :]), A2(b["z"][:, :, :]), ALU.mult).then_inc(s["yz"], 1)

            @block.tensor
            def _(pe):
                pe.wait_ge(s["w"], 80)

                def add_state(g, k):
                    wait(net, pe, s["hc"], g)
                    for i in range(2):
                        ins = pe.matmul(B[i][:, 0:CHUNK], net.const("ident"), hc[:, k % 2, i, :], start=(k == 0), stop=(k == STATES - 1))
                    ins.then_inc(s["y_mm"], 1)

                with pe.Fori(0, CHUNKS) as j:
                    wait(net, pe, s["xs_in"], 16 * j + 16)
                    for a in range(4):
                        for i in range(2):
                            ins = pe.transpose(B[i][:, a * PART:(a + 1) * PART], b["xs"][0:PART, a, i * P:(i + 1) * P], net.const("ident")[0:PART, 0:PART])
                    ins.then_inc(s["tr"], 1)
                    wait(net, pe, s["xsT"], j + 1)
                    for m in range(4):
                        ins = products(pe, B[2 + m][:, 0:CHUNK], [(b["w_in"][:, k, m * P:(m + 1) * P], b["xsT"][:, k, :]) for k in range(2)])
                    ins.then_inc(s["in_mm"], 1)
                    wait(net, pe, s["silu"], j + 1)
                    products(pe, B[6][0:48, 0:CHUNK], [(b["w_x"][:, k, :], b["xc"][:, k, :]) for k in range(2)]).then_inc(s["x_mm"], 1)
                    wait(net, pe, s["dbc"], j + 1)
                    for i in range(2):
                        ins = products(pe, B[2 + i][:, 0:CHUNK], [(b["w_dt"][0:16, i * P:(i + 1) * P], b["dbc"][0:16, :])])
                    ins.then_inc(s["dt_mm"], 1)
                    for k in range(STATES):
                        g = j * STATES + k + 1
                        if k >= 2:
                            wait(net, pe, s["hc"], g - 2)
                        for row, bank in ((16 + k, B[6 - 2 * (k % 2)]), (32 + k, B[7 - 2 * (k % 2)])):
                            ins = pe.matmul(bank[:, 0:CHUNK], net.const("ident")[0:48, row:row + 1].to_broadcast([48, P]), b["dbc"][0:48, :], start=True, stop=True)
                        ins.then_inc(s["bc"], 1)
                        if k:
                            add_state(g - 1, k - 1)
                    add_state((j + 1) * STATES, STATES - 1)
                    wait(net, pe, s["yz"], j + 1)
                    for a in range(4):
                        ins = products(pe, B[2 + a][0:PART, 0:D], [(b["dtx"][:, k, a * PART:(a + 1) * PART], b["w_out"][:, k, :]) for k in range(2)])
                    ins.then_inc(s["out_mm"], 1)


def guard_stage(nc, net):
    m, g = (a[:, :, :].rearrange("p a b -> p (a b)") for a in (net.node_max, net.guard))
    with ExitStack() as c:
        b = buffers(nc, c, "guard", has=[TILES], far=[TILES], masked=[TILES, H], top=[1], turn=[P], all=[1])
        with stage(nc, "guard", ["top", "row", "all", "ps", "diff", "exp"]) as (block, s):
            @block.vector
            def _(dve):
                dve.tensor_scalar(b["has"][:, :], net.degree[:, :], 0.0, None, ALU.is_gt)
                dve.drain()
                dve.tensor_scalar(b["far"][:, :], b["has"][:, :], BIG, BIG, ALU.mult, ALU.subtract)
                dve.drain()
                dve.tensor_tensor(b["masked"][:, :, :], net.node_max[:, :, :], b["far"][:, :].unsqueeze(2).to_broadcast([P, TILES, H]), ALU.add)
                dve.drain()
                dve.tensor_reduce(b["top"][:, :], b["masked"][:, :, :], AX.XY, ALU.max)
                dve.drain()
                dve.tensor_scalar(b["turn"][:, :], net.const("ident"), b["top"][:, :], None, ALU.mult).then_inc(s["top"], 1)
                dve.wait_ge(s["row"], 1)
                dve.tensor_reduce(b["all"][:, :], net.PS[0][:, 0:P], AX.X, ALU.max)
                dve.drain()
                dve.tensor_scalar(g, m, b["all"][:, :], -1.0, ALU.subtract, ALU.mult)
                dve.drain()
                dve.tensor_scalar(g, g, 87.0, None, ALU.min).then_inc(s["diff"], 1)
                dve.wait_ge(s["exp"], 1)
                dve.tensor_scalar(g, g, 1e-16, None, ALU.mult)

            @block.tensor
            def _(pe):
                pe.wait_ge(s["top"], 1)
                pe.matmul(net.PS[0][:, 0:P], net.const("ones"), b["turn"][:, :], start=True, stop=True).then_inc(s["row"], 1)

            @block.scalar
            def _(act):
                act.wait_ge(s["diff"], 1)
                act.activation(g, g, ACT.Exp).then_inc(s["exp"], 1)


def final_stage(nc, net):
    with ExitStack() as c:
        b = buffers(nc, c, "fin", rows=[8, D], gates=[4, D], ff1=[2, 512], ff1b=[4], ff2=[4, D], wq=[2, D], cols=[2, 3],
                    xn=[D], xnT=[2, P], den=[H], v=[D], ex=[D], pair=[2, D], pT=[4, P], g=[D], h=[D], hT=[2, P], fT=[4, P],
                    qT=[2, P], y=[D], idx_i=[1], six=[6], mv=[2], var=[1], rs=[1])
        B = net.PS
        names = ["w_in", "loaded", "xn", "tr", "xnT", "q", "qT", "mix", "e_in", "e_out", "idx", "y_used", "pair", "tr_p", "pT", "gate",
                 "g_in", "g_out", "h", "tr_h", "hT", "f1", "f1r", "f2", "var_ready", "rstd_ready", "gp_y"]
        with stage(nc, "fin", names) as (block, s):
            GAT_B, LOC_G, LOC_B, GLO_G, GLO_B, LN2_G, LN2_B, FF2_B = range(8)

            @block.sync
            def _(sp):
                i = net.inp
                loads = [(b["rows"][:, :, :].rearrange("p a b -> p (a b)"), i["g1_rows"].to_broadcast([P, 8 * D])), (b["gates"][:, :, :], weight(i["g1_gates"])),
                         (b["ff1"][:, :, :], weight(i["g1_ff1"])), (b["ff1b"][:, :], i["g1_ff1b"]), (b["ff2"][:, :, :], weight(i["g1_ff2"])),
                         (b["wq"][:, :, :], weight(i["m1_wq"])), (b["cols"][:, :, :].rearrange("p a b -> p (a b)"), i["m1_cols"])]
                for dst, src in loads:
                    sp.dma_start(dst, src).then_inc(s["w_in"], 16)
                sp.wait_ge(s["w_in"], 16 * len(loads))
                sp.sem_inc(s["loaded"], 1)

            @block.gpsimd
            def _(pool):
                with pool.Fori(0, TILES) as t:
                    wait(net, pool, s["y_used"], t + 1)
                    pool.tensor_copy(b["idx_i"][:, :], net.rank[:, bass.ds(t, 1)]).then_inc(s["idx"], 1)
                    wait_apart(net, pool, s["idx"], t + 1)
                    pool.indirect_dma_start(b["y"][:, :], None, net.mamba_y, bass.IndirectOffsetOnAxis(ap=b["idx_i"][:, 0:1], axis=0)).then_inc(s["gp_y"], 16)
                    for k in range(3):
                        norm_power(net, pool, s, b, 3 * t + k + 1)

            @block.tensor
            def _(pe):
                pe.wait_ge(s["loaded"], 1)
                with pe.Fori(0, TILES) as t:
                    wait(net, pe, s["xn"], t + 1)
                    turned(pe, net, B[0], b["xn"], 2).then_inc(s["tr"], 1)
                    wait(net, pe, s["xnT"], t + 1)
                    for i in range(2):
                        ins = products(pe, B[1][:, i * P:(i + 1) * P], [(b["wq"][:, k, i * P:(i + 1) * P], b["xnT"][:, k, :]) for k in range(2)])
                    ins.then_inc(s["q"], 1)
                    wait(net, pe, s["qT"], t + 1)
                    products(pe, B[2][:, 0:D], [(b["qT"][:, k, :], net.lam[:, k, :]) for k in range(2)]).then_inc(s["mix"], 1)
                    wait(net, pe, s["pair"], t + 1)
                    turned(pe, net, B[3], b["pair"][:, :, :].rearrange("p a b -> p (a b)"), 4).then_inc(s["tr_p"], 1)
                    wait(net, pe, s["pT"], t + 1)
                    products(pe, B[4][:, 0:D], [(b["pT"][:, k, :], b["gates"][:, k, :]) for k in range(4)]).then_inc(s["gate"], 1)
                    wait(net, pe, s["h"], t + 1)
                    turned(pe, net, B[5], b["h"], 2).then_inc(s["tr_h"], 1)
                    wait(net, pe, s["hT"], t + 1)
                    for i in range(4):
                        ins = products(pe, B[6][:, i * P:(i + 1) * P], [(b["ff1"][:, k, i * P:(i + 1) * P], b["hT"][:, k, :]) for k in range(2)])
                    ins.then_inc(s["f1"], 1)
                    wait(net, pe, s["f1r"], t + 1)
                    products(pe, B[7][:, 0:D], [(b["fT"][:, k, :], b["ff2"][:, k, :]) for k in range(4)]).then_inc(s["f2"], 1)

            @block.scalar
            def _(act):
                copy = lambda dst, src: act.activation(dst.rearrange("p a b -> p (a b)"), src, ACT.Copy)
                act.wait_ge(s["loaded"], 1)
                with act.Fori(0, TILES) as t:
                    wait(net, act, s["tr"], t + 1)
                    copy(b["xnT"][:, :, :], B[0][:, 0:D]).then_inc(s["xnT"], 1)
                    wait(net, act, s["q"], t + 1)
                    for i in range(2):
                        ins = act.activation(b["qT"][:, i, :], B[1][:, i * P:(i + 1) * P], ACT.Identity, bias=b["cols"][:, i, 0:1])
                    ins.then_inc(s["qT"], 1)
                    wait(net, act, s["e_in"], t + 1)
                    act.activation(b["ex"][:, :], b["ex"][:, :], ACT.Exp).then_inc(s["e_out"], 1)
                    wait(net, act, s["tr_p"], t + 1)
                    copy(b["pT"][:, :, :], B[3][:, :]).then_inc(s["pT"], 1)
                    wait(net, act, s["g_in"], t + 1)
                    act.activation(b["g"][:, :], b["g"][:, :], ACT.Exp, scale=-1.0).then_inc(s["g_out"], 1)
                    wait(net, act, s["tr_h"], t + 1)
                    copy(b["hT"][:, :, :], B[5][:, 0:D]).then_inc(s["hT"], 1)
                    wait(net, act, s["f1"], t + 1)
                    for i in range(4):
                        ins = act.activation(b["fT"][:, i, :], B[6][:, i * P:(i + 1) * P], ACT.Relu, bias=b["ff1b"][:, i:i + 1])
                    ins.then_inc(s["f1r"], 1)

            @block.vector
            def _(dve):
                heads = lambda a: a.rearrange("p (h d) -> p h d", h=H)
                row = lambda k: b["rows"][:, k, :]
                local, globe = b["pair"][:, 0, :], b["pair"][:, 1, :]
                dve.wait_ge(s["loaded"], 1)
                dve.sem_inc(s["y_used"], 1)
                with dve.Fori(0, TILES) as t:
                    x = rows(net.X[:, bass.ds(t, 1), :])
                    agg = rows(net.agg[:, bass.ds(t, 1), :])
                    dve.tensor_scalar(b["xn"][:, :], x, net.rstd[:, bass.ds(t, 1)], net.shift[:, bass.ds(t, 1)], ALU.mult, ALU.add).then_inc(s["xn"], 1)
                    dve.tensor_tensor(b["den"][:, :], agg[:, D:D + H], rows(net.guard[:, bass.ds(t, 1), :]), ALU.add)
                    dve.drain()
                    dve.reciprocal(b["den"][:, :], b["den"][:, :])
                    dve.drain()
                    dve.tensor_tensor(heads(b["v"][:, :]), heads(agg[:, 0:D]), b["den"][:, :].unsqueeze(2).to_broadcast([P, H, 64]), ALU.mult)
                    dve.drain()
                    dve.tensor_tensor(b["v"][:, :], b["v"][:, :], b["xn"][:, :], ALU.add)
                    dve.drain()
                    dve.tensor_tensor(b["v"][:, :], b["v"][:, :], row(GAT_B), ALU.add)
                    dve.drain()
                    dve.tensor_scalar(b["ex"][:, :], b["v"][:, :], 0.0, None, ALU.min).then_inc(s["e_in"], 1)
                    wait(net, dve, s["e_out"], t + 1)
                    dve.tensor_scalar(b["ex"][:, :], b["ex"][:, :], 1.0, None, ALU.subtract)
                    dve.drain()
                    dve.scalar_tensor_tensor(b["v"][:, :], b["v"][:, :], 0.0, b["ex"][:, :], ALU.max, ALU.add)
                    dve.drain()
                    layer_norm(net, dve, s, b, b["v"][:, :], local, 3 * t + 1, row(LOC_G), row(LOC_B))
                    wait(net, dve, s["gp_y"], 16 * t + 16)
                    dve.tensor_tensor(b["v"][:, :], b["y"][:, :], b["xn"][:, :], ALU.add).then_inc(s["y_used"], 1)
                    dve.drain()
                    layer_norm(net, dve, s, b, b["v"][:, :], globe, 3 * t + 2, row(GLO_G), row(GLO_B))
                    dve.sem_inc(s["pair"], 1)
                    wait(net, dve, s["gate"], t + 1)
                    dve.tensor_scalar(b["g"][:, :], B[4][:, 0:D], -87.0, None, ALU.max).then_inc(s["g_in"], 1)
                    wait(net, dve, s["g_out"], t + 1)
                    dve.tensor_scalar(b["g"][:, :], b["g"][:, :], 1.0, None, ALU.add)
                    dve.drain()
                    dve.reciprocal(b["g"][:, :], b["g"][:, :])
                    dve.tensor_tensor(b["v"][:, :], local, globe, ALU.subtract)
                    dve.drain()
                    dve.tensor_tensor(b["v"][:, :], b["v"][:, :], b["g"][:, :], ALU.mult)
                    dve.drain()
                    dve.tensor_tensor(b["h"][:, :], b["v"][:, :], globe, ALU.add).then_inc(s["h"], 1)
                    wait(net, dve, s["mix"], t + 1)
                    dve.tensor_tensor(x, x, B[2][:, 0:D], ALU.add)
                    wait(net, dve, s["f2"], t + 1)
                    dve.tensor_tensor(b["v"][:, :], b["h"][:, :], B[7][:, 0:D], ALU.add)
                    dve.drain()
                    dve.tensor_tensor(b["v"][:, :], b["v"][:, :], row(FF2_B), ALU.add)
                    dve.drain()
                    layer_norm(net, dve, s, b, b["v"][:, :], b["g"][:, :], 3 * t + 3, row(LN2_G), row(LN2_B))
                    dve.tensor_tensor(x, x, b["g"][:, :], ALU.add)
                    dve.drain()


EXPERTS = 8


def expert_stage(nc, net):
    with ExitStack() as c:
        w1 = net.agg[:, :, :].rearrange("p a b -> p (a b)")[:, 0:EXPERTS * 1024].rearrange("p (e k n) -> p e k n", e=EXPERTS, k=2)
        b = buffers(nc, c, "exp", gw=[2, EXPERTS], gb=[EXPERTS], b1=[32], b2=[EXPERTS, D], w2=[EXPERTS, 4, D],
                    xn=[D], xnT=[2, P], hT=[2, 4, P], gt=[64], eq=[64], before=[64], sel=[EXPERTS], g=[EXPERTS], o=[D])
        B = net.PS
        names = ["w_in", "loaded", "xn", "tr", "xnT", "gl", "h", "gelu", "y", "y_used", "acc", "stored"]
        with stage(nc, "exp", names) as (block, s):
            @block.sync
            def _(sp):
                i = net.inp
                loads = [(w1.rearrange("p e k n -> p (e k) n"), i["e_w1"].rearrange("(a p) n -> p a n", p=P)),
                         (b["w2"][:, :, :, :].rearrange("p e k n -> p (e k) n"), i["e_w2"].rearrange("(a p) n -> p a n", p=P)),
                         (b["gw"][:, :, :], weight(i["e_gw"])), (b["gb"][0:1, :], i["e_gb"]), (b["b1"][:, :], i["e_b1"]),
                         (b["b2"][0:1, :, :].rearrange("p a b -> p (a b)"), i["e_b2"].rearrange("e n -> (e n)").unsqueeze(0))]
                for dst, src in loads:
                    sp.dma_start(dst, src).then_inc(s["w_in"], 16)
                sp.wait_ge(s["w_in"], 16 * len(loads))
                sp.sem_inc(s["loaded"], 1)
                with sp.Fori(0, TILES - 1) as t:
                    wait(net, sp, s["acc"], t + 1)
                    sp.dma_start(net.out[bass.ds(t * P, P), :], rows(net.X[:, bass.ds(t, 1), :])).then_inc(s["stored"], 16)
                sp.wait_ge(s["acc"], TILES)
                sp.dma_start(net.out[(TILES - 1) * P:N, :], net.X[0:LAST, TILES - 1, :]).then_inc(s["stored"], 16)
                sp.wait_ge(s["stored"], 16 * TILES)

            @block.tensor
            def _(pe):
                pe.wait_ge(s["loaded"], 1)
                ones = net.const("ones")[0:1, :]
                with pe.Fori(0, TILES) as t:
                    wait(net, pe, s["xn"], t + 1)
                    turned(pe, net, B[0], b["xn"], 2).then_inc(s["tr"], 1)
                    wait(net, pe, s["xnT"], t + 1)
                    products(pe, B[1][:, 0:EXPERTS], [(b["xnT"][:, k, :], b["gw"][:, k, :]) for k in range(2)] + [(ones, b["gb"][0:1, :])]).then_inc(s["gl"], 1)

                    def up(e):
                        wait(net, pe, s["gelu"], t * EXPERTS + e + 1)
                        for i in range(4):
                            ins = products(pe, B[2 + e % 2][:, i * P:(i + 1) * P], [(w1[:, e, k, i * P:(i + 1) * P], b["xnT"][:, k, :]) for k in range(2)])
                        ins.then_inc(s["h"], 1)

                    def down(e):
                        wait(net, pe, s["gelu"], t * EXPERTS + e + 3)
                        wait(net, pe, s["y_used"], t * EXPERTS + e + 1)
                        products(pe, B[4 + e % 2][:, 0:D], [(b["hT"][:, e % 2, k, :], b["w2"][:, e, k, :]) for k in range(4)] +
                                 [(ones, b["b2"][0:1, e, :])]).then_inc(s["y"], 1)

                    up(0)
                    for e in range(1, EXPERTS):
                        up(e)
                        down(e - 1)
                    down(EXPERTS - 1)

            @block.scalar
            def _(act):
                act.wait_ge(s["loaded"], 1)
                act.sem_inc(s["gelu"], 2)
                with act.Fori(0, TILES) as t:
                    wait(net, act, s["tr"], t + 1)
                    act.activation(b["xnT"][:, :, :].rearrange("p a b -> p (a b)"), B[0][:, 0:D], ACT.Copy).then_inc(s["xnT"], 1)
                    for e in range(EXPERTS):
                        wait(net, act, s["h"], t * EXPERTS + e + 1)
                        wait(net, act, s["y"], t * EXPERTS + e + 1)
                        for i in range(4):
                            ins = act.activation(b["hT"][:, e % 2, i, :], B[2 + e % 2][:, i * P:(i + 1) * P], ACT.Gelu, bias=b["b1"][:, e * 4 + i:e * 4 + i + 1])
                        ins.then_inc(s["gelu"], 1)

            @block.vector
            def _(dve):
                make_before(dve, EXPERTS, b)
                dve.wait_ge(s["loaded"], 1)
                dve.sem_inc(s["y_used"], 2)
                dve.sem_inc(s["y"], 2)
                with dve.Fori(0, TILES) as t:
                    x = rows(net.X[:, bass.ds(t, 1), :])
                    dve.tensor_scalar(b["xn"][:, :], x, net.rstd[:, bass.ds(t, 1)], net.shift[:, bass.ds(t, 1)], ALU.mult, ALU.add).then_inc(s["xn"], 1)
                    wait(net, dve, s["gl"], t + 1)
                    dve.tensor_copy(b["g"][:, :], B[1][:, 0:EXPERTS])
                    dve.drain()
                    top_two(dve, net, EXPERTS, b["g"][:, :], b)
                    for e in range(EXPERTS):
                        wait(net, dve, s["y"], t * EXPERTS + e + 3)
                        ins = dve.scalar_tensor_tensor(x, B[4 + e % 2][:, 0:D], b["sel"][:, e:e + 1], x, ALU.mult, ALU.add).then_inc(s["y_used"], 1)
                        dve.drain()
                    dve.sem_inc(s["acc"], 1)


def build(nc, ins, out):
    net = Net()
    pool_sems[0] = POOL_SEM
    net.inp, net.out = ins, out
    dram = lambda name, shape, dt=F32: nc.dram_tensor(name, shape, dt, kind="Internal").ap()
    net.table = dram("table", (NPAD, D))
    net.src_tab = dram("src_tab", (NPAD, H))
    net.node_rec = dram("node_rec", (NPAD, 2 * H))
    net.src_pad = dram("src_pad", (ETILES, P), I32)
    net.dst_pad = dram("dst_pad", (ETILES, P), I32)
    net.run_max = dram("run_max", (EPAD, H))
    net.start_rec = dram("start_rec", (EPAD, 2 * H))
    net.weights = dram("weights", (ETILES, P * H))
    net.tile_row = dram("tile_row", (1, SPAD), I32)
    net.keys = dram("keys", (1, NPAD))
    net.sorted_x = dram("sorted_x", (NPAD, D))
    net.mamba_y = dram("mamba_y", (NPAD, D))
    with ExitStack() as c:
        net.tick = c.enter_context(nc.semaphore("tick"))
        sb = lambda name, shape, dt=F32: c.enter_context(nc.sbuf_tensor(name, shape, dt))
        net.PS = [c.enter_context(nc.psum_tensor(f"bank{i}", [P, 512], F32)) for i in range(8)]
        net.C = sb("consts", [P, CONST_N])
        net.const = lambda k: net.C[:, slice(*CONST_COLS[k])]
        net.X = sb("X", [P, TILES, D])
        net.zeros = sb("zeros", [P, 512])
        net.stat = sb("stat", [P, 8])
        net.rstd, net.shift = sb("rstd", [P, TILES]), sb("shift", [P, TILES])
        net.node_src, net.node_dst = sb("node_src", [P, TILES, H]), sb("node_dst", [P, TILES, H])
        net.node_max = sb("node_max", [P, TILES, H])
        net.kv, net.ksum = sb("kv", [P, 2, P]), sb("ksum", [P, 2, 4])
        net.starts, net.ends, net.degree = sb("starts", [P, TILES], I32), sb("ends", [P, TILES], I32), sb("degree", [P, TILES])
        net.src_degree = sb("src_degree", [P, TILES])
        net.agg = sb("agg", [P, TILES, D + H])
        net.step_src = sb("step_src", [P, SPAD], I32)
        net.step_et = sb("step_et", [P, SBLK], I32)
        net.step_dst = sb("step_dst", [P, SPAD])
        net.edge = sb("edge", [P, SPAD * H])
        net.key_top, net.lam, net.guard = sb("key_top", [P, D]), sb("lam", [P, 2, D]), sb("guard", [P, TILES, H])
        net.rank = sb("rank", [P, TILES], I32)
        stages = [load_stage,
                  lambda nc, net: norm_stage(nc, net, "norm0"),
                  project_stage, pad_edges_stage,
                  lambda nc, net: gather_stage(nc, net, "gather0", degree_work), index_stage,
                  lambda nc, net: weight_stage(nc, net, "weight0", 0.01),
                  lambda nc, net: aggregate_stage(nc, net, "agg0"), combine_stage,
                  lambda nc, net: norm_stage(nc, net, "norm1"), project1_stage, lambda_stage,
                  lambda nc, net: gather_stage(nc, net, "gather1", rank_work), sort_stage,
                  lambda nc, net: weight_stage(nc, net, "weight1", 0.2), guard_stage,
                  lambda nc, net: aggregate_stage(nc, net, "agg1"), mamba_stage, final_stage,
                  lambda nc, net: norm_stage(nc, net, "norm2"), expert_stage]
        for run in stages:
            run(nc, net)


def layout(i):
    f = {}
    a = lambda x: np.ascontiguousarray(np.asarray(x))

    def diagonal(src, dst):
        out = np.zeros((D, 8), np.float32)
        for h in range(H):
            out[h * 64:(h + 1) * 64, h] = np.asarray(src[h]).reshape(64)
            out[h * 64:(h + 1) * 64, 4 + h] = np.asarray(dst[h]).reshape(64)
        return out

    f["consts"] = constants()
    f["x"], f["src"], f["dst"] = a(i["x"]), a(i["src"]).reshape(1, E), a(i["dst"]).reshape(1, E)
    f["noise"] = a(i["node_vec"]).reshape(1, N)
    heads = lambda w: np.asarray(w).transpose(1, 0, 2).reshape(D, D)
    f["g0_w"] = a(heads(i["L0_gnn_W_fc"]))
    f["g0_wT"] = a(f["g0_w"].T)
    f["g0_al"] = diagonal(i["L0_gnn_W_ar"], i["L0_gnn_W_al"])
    f["g0_res"] = a(heads(i["L0_gnn_W_res"]))
    f["m0_wkv"] = a(np.concatenate([i["L0_mix_Wk"], i["L0_mix_Wv"]], 1))
    f["m0_wq"], f["m0_wm"], f["m0_w1"], f["m0_w2"] = (a(i["L0_mix_" + k]) for k in ("Wq", "Wm", "W1", "W2"))
    row = lambda *v: a(np.stack([np.asarray(x).reshape(-1) for x in v]).reshape(1, -1))
    f["m0_norms"] = row(i["L0_mix_g1"], i["L0_mix_b1"], i["L0_mix_g2"], i["L0_mix_b2"])
    experts = lambda w: np.asarray(w).transpose(1, 0, 2).reshape(w.shape[1], -1)
    f["f0_w1"] = a(np.concatenate([i["L0_ffn_sW1"], experts(i["L0_ffn_eW1"])], 1))
    f["f0_b1"] = a(np.concatenate([np.asarray(i["L0_ffn_sb1"]), np.asarray(i["L0_ffn_eb1"]).reshape(-1)]).reshape(6, P).T)
    f["f0_w2"], f["f0_e2"] = a(i["L0_ffn_sW2"]), a(experts(i["L0_ffn_eW2"]))
    f["f0_b2"] = a(np.asarray(i["L0_ffn_sb2"]).reshape(P, 1))
    f["f0_eb2"] = a(np.asarray(i["L0_ffn_eb2"]).T)
    f["f0_w3"], f["f0_e3"] = a(i["L0_ffn_sW3"]), a(np.asarray(i["L0_ffn_eW3"]).transpose(1, 0, 2).reshape(64, -1))
    f["f0_b3"] = a(np.asarray(i["L0_ffn_sb3"]).reshape(1, D))
    f["f0_eb3"] = a(np.asarray(i["L0_ffn_eb3"]).reshape(1, -1))
    f["f0_gw"], f["f0_gb"] = a(i["L0_ffn_gW"]), a(np.asarray(i["L0_ffn_gb"]).reshape(1, -1))
    g = {k[7:]: np.asarray(v) for k, v in i.items() if k.startswith("L1_gnn_")}
    f["g1_w"], f["g1_wT"] = a(g["gat_w"].T), a(g["gat_w"])
    f["g1_al"] = diagonal(g["gat_a_src"], g["gat_a_tgt"])
    f["g1_rows"] = row(g["gat_b"], g["ln_local_g"], g["ln_local_b"], g["ln_global_g"], g["ln_global_b"], g["ln2_g"],
                       g["ln2_b"], g["ff2_b"])
    f["s_in"], f["s_x"], f["s_dt"], f["s_out"] = (a(g[k].T) for k in ("in_proj_w", "x_proj_w", "dt_proj_w", "out_proj_w"))
    cols = lambda v: np.asarray(v).reshape(2, P, -1).transpose(1, 0, 2)
    f["s_cols"] = a(np.concatenate([cols(g[k]) for k in ("conv_w", "conv_b", "dt_proj_b", "D_param", "A_log")], 2).reshape(P, -1))
    f["g1_gates"] = a(np.concatenate([g["wl"].T, g["wg"].T], 0))
    f["g1_ff1"], f["g1_ff2"] = a(g["ff1_w"].T), a(g["ff2_w"].T)
    f["g1_ff1b"] = a(g["ff1_b"].reshape(4, P).T)
    m = {k[7:]: np.asarray(v) for k, v in i.items() if k.startswith("L1_mix_")}
    f["m1_wq"] = a(m["W_qk"][0])
    f["m1_wkv"] = a(np.concatenate([m["W_qk"][1], m["W_v"]], 1))
    f["m1_bkv"] = a(np.concatenate([m["b_qk"][1], m["b_v"]]).reshape(1, -1))
    f["m1_cols"] = a(np.stack([m["b_qk"][0], m["gamma"], m["beta"]], 1).reshape(2, P, 3).transpose(1, 0, 2).reshape(P, 6))
    f["e_gw"], f["e_gb"] = a(i["L1_ffn_Wg"]), a(np.asarray(i["L1_ffn_bg"]).reshape(1, -1))
    f["e_w1"] = a(i["L1_ffn_W1"]).reshape(8 * D, 512)
    f["e_b1"] = a(np.asarray(i["L1_ffn_b1"]).reshape(8 * 4, P).T)
    f["e_w2"] = a(i["L1_ffn_W2"]).reshape(8 * 512, D)
    f["e_b2"] = a(i["L1_ffn_b2"])
    return f


def kernel(**inputs):
    import concourse.bacc as _bacc
    from concourse.bass_utils import run_bass_kernel_spmd as _run

    nc = _bacc.Bacc("TRN2", target_bir_lowering=False, num_devices=1)
    arrays = layout(inputs)
    ins = {k: nc.dram_tensor(f"in_{k}", v.shape, mybir.dt.from_np(v.dtype), kind="ExternalInput").ap() for k, v in arrays.items()}
    out = nc.dram_tensor("out_x", (N, D), F32, kind="ExternalOutput").ap()
    build(nc, ins, out)
    got = _run(nc, [{f"in_{k}": v for k, v in arrays.items()}], core_ids=[0])
    return got.results[0]["out_x"]
```

```python
from contextlib import ExitStack, contextmanager

import numpy as np

import concourse.bass as bass
from concourse import mybir

F32 = mybir.dt.float32
I32 = mybir.dt.int32
ALU = mybir.AluOpType
ACT = mybir.ActivationFunctionType
AX = mybir.AxisListType

P = 128
N = 6250
E = 200000
D = 256
H = 4
TILES = (N + P - 1) // P
NPAD = TILES * P
LAST = N - (TILES - 1) * P
GROUP = 16
ETILES = -(-E // (P * GROUP)) * GROUP
EPAD = ETILES * P
EROW = EPAD // P
STEPS = -(-2 * (-(-E // (2 * P)) + TILES - 1) // GROUP) * GROUP
SBLK = (STEPS + P - 1) // P
SPAD = SBLK * P
FIRST_SEM = 100
POOL_SEM = 220
pool_sems = [POOL_SEM]
BIG = 1.0e30
FAR = 1 << 20
LN_EPS = 1e-5

CONST_COLS = dict(ident=(0, 128), iota=(128, 256), upper=(256, 384), ones=(384, 512), block32=(512, 640),
                  valid=(640, 640 + TILES), step=(700, 700 + SBLK), bound=(720, 720 + TILES - 1),
                  head32=(780, 784), pid=(784, 785), eps=(785, 786), mhalf=(786, 787), zero=(787, 788),
                  one=(788, 789), lower=(800, 928), half=(928, 928 + SBLK))
CONST_N = 928 + SBLK


def constants():
    c = np.zeros((P, CONST_N), np.float32)
    p = np.arange(P)

    def put(k, v):
        lo, hi = CONST_COLS[k]
        c[:, lo:hi] = v

    put("ident", np.eye(P))
    put("iota", np.broadcast_to(p, (P, P)))
    put("upper", p[:, None] < p[None, :])
    put("lower", p[:, None] > p[None, :])
    put("ones", 1.0)
    put("block32", p[:, None] // 32 == p[None, :] // 32)
    put("valid", p[:, None] + P * np.arange(TILES)[None, :] < N)
    steps = p[:, None] + P * np.arange(SBLK)[None, :]
    put("step", steps // 2)
    put("half", steps % 2)
    put("bound", np.arange(1, TILES)[None, :])
    put("head32", p[:, None] // 32 == np.arange(4)[None, :])
    put("pid", p[:, None])
    put("eps", LN_EPS)
    put("mhalf", -0.5)
    put("one", 1.0)
    return c


class Net:
    pass


def rows(ap):
    return ap.rearrange("p a b -> p (a b)")


def wait(net, eng, sem, value):
    eng.wait_ge(sem, value)


def wait_apart(net, eng, sem, value):
    eng.wait_ge(sem, value)
    eng.sem_inc(net.tick, 1)


@contextmanager
def stage(nc, name, sems):
    pool = [x for x in sems if x.startswith("gp_")]
    rest = [x for x in sems if not x.startswith("gp_")]
    with ExitStack() as c:
        ns = {x: c.enter_context(nc.semaphore(f"{name}_{x}", num=first + i))
              for first, group in ((FIRST_SEM, rest), (pool_sems[0], pool)) for i, x in enumerate(group)}
        pool_sems[0] += len(pool)
        with nc.Block() as block:
            yield block, ns
        nc.all_engine_barrier(sems_to_clear=range(FIRST_SEM, FIRST_SEM + len(rest)))


def buffers(nc, c, name, **shapes):
    return {k: c.enter_context(nc.sbuf_tensor(f"{name}_{k}", [P] + list(v), I32 if k.endswith("_i") else F32))
            for k, v in shapes.items()}


def weight(dram):
    return dram.rearrange("(a p) n -> p a n", p=P)


def load_stage(nc, net):
    with stage(nc, "load", ["zeroed", "x_in", "c_in"]) as (block, s):
        @block.vector
        def _(dve):
            dve.memset(net.X[:, TILES - 1, :], 0.0).then_inc(s["zeroed"], 1)
            dve.memset(net.zeros[:, :], 0.0)
            dve.memset(net.stat[:, 0:1], 0.0)

        @block.sync
        def _(sp):
            sp.dma_start(net.C[:, :], net.inp["consts"]).then_inc(s["c_in"], 16)
            sp.dma_start(net.X[:, 0:TILES - 1, :],
                         net.inp["x"][0:(TILES - 1) * P, :].rearrange("(t p) d -> p t d", p=P)).then_inc(s["x_in"], 16)
            sp.wait_ge(s["zeroed"], 1)
            sp.dma_start(net.X[0:LAST, TILES - 1, :], net.inp["x"][(TILES - 1) * P:N, :]).then_inc(s["x_in"], 16)
            sp.wait_ge(s["x_in"], 32)
            sp.wait_ge(s["c_in"], 16)


def norm_stage(nc, net, name):
    with ExitStack() as c:
        b = buffers(nc, c, name, six=[TILES, 6], mean=[TILES], gap=[TILES], var=[TILES])
        with stage(nc, name, ["stats", "rstd"]) as (block, s):
            @block.vector
            def _(dve):
                with dve.Fori(0, TILES) as t:
                    dve.bn_stats(rows(b["six"][:, bass.ds(t, 1), :]), rows(net.X[:, bass.ds(t, 1), :]))
                dve.drain()
                even, odd = b["six"][:, :, 0:3], b["six"][:, :, 3:6]
                dve.tensor_tensor(b["mean"][:, :], even[:, :, 1], odd[:, :, 1], ALU.add)
                dve.tensor_tensor(b["gap"][:, :], even[:, :, 1], odd[:, :, 1], ALU.subtract)
                dve.tensor_tensor(b["var"][:, :], even[:, :, 2], odd[:, :, 2], ALU.add)
                dve.drain()
                dve.tensor_tensor(b["gap"][:, :], b["gap"][:, :], b["gap"][:, :], ALU.mult)
                dve.drain()
                dve.scalar_tensor_tensor(b["var"][:, :], b["gap"][:, :], D / 4.0, b["var"][:, :], ALU.mult, ALU.add)
                dve.drain()
                dve.tensor_scalar(b["var"][:, :], b["var"][:, :], 1.0 / D, LN_EPS, ALU.mult, ALU.add).then_inc(s["stats"], 1)
                dve.wait_ge(s["rstd"], 1)
                dve.scalar_tensor_tensor(net.shift[:, :], b["mean"][:, :], -0.5, net.rstd[:, :], ALU.mult, ALU.mult)

            @block.gpsimd
            def _(pool):
                pool.wait_ge(s["stats"], 1)
                pool.tensor_tensor(net.rstd[:, :], b["var"][:, :], net.const("mhalf").to_broadcast([P, TILES]),
                                   ALU.pow).then_inc(s["rstd"], 1)


def project_stage(nc, net):
    with ExitStack() as c:
        b = buffers(nc, c, "proj", w=[2, 264], wT=[2, D], al=[2, 8], wkv=[2, 512], xn=[D], xnT=[2, P],
                    tab=[264], kx=[D], ke=[D], vv=[2, 132], kvacc=[2, 132])
        ps_tr, ps_tab, ps_kv, ps_sum = net.PS[0], net.PS[1], net.PS[2], net.PS[3]
        names = ["w_in", "folded", "fold_ps", "xn", "tr", "xnT", "mm", "tab_sb", "tab_out", "kmin", "kexp",
                 "v_ready", "kv_ready", "kv_mm", "kv_used", "end"]
        with stage(nc, "proj", names) as (block, s):
            @block.sync
            def _(sp):
                sp.dma_start(b["w"][:, :, 0:D], weight(net.inp["g0_w"])).then_inc(s["w_in"], 16)
                sp.dma_start(b["wT"][:, :, :], weight(net.inp["g0_wT"])).then_inc(s["w_in"], 16)
                sp.dma_start(b["al"][:, :, :], weight(net.inp["g0_al"])).then_inc(s["w_in"], 16)
                sp.dma_start(b["wkv"][:, :, :], weight(net.inp["m0_wkv"])).then_inc(s["w_in"], 16)
                with sp.Fori(0, TILES) as t:
                    wait(net, sp, s["tab_sb"], t + 1)
                    sp.dma_start(net.table[bass.ds(t * P, P), :], b["tab"][:, 0:D]).then_inc(s["tab_out"], 16)
                sp.wait_ge(s["end"], 1)
                sp.dma_start(net.src_tab.rearrange("(t p) c -> p t c", p=P), net.node_src[:, :, :]).then_inc(s["tab_out"], 16)
                sp.wait_ge(s["tab_out"], 16 * (TILES + 1) + 1)

            @block.vector
            def _(dve):
                dve.memset(b["kvacc"][:, :, :], 0.0)
                dve.wait_ge(s["fold_ps"], 1)
                for i in range(2):
                    ins = dve.tensor_copy(b["w"][:, i, D:D + 8], ps_tab[:, 8 * i:8 * i + 8])
                ins.then_inc(s["folded"], 1)
                with dve.Fori(0, TILES) as t:
                    dve.tensor_scalar(b["xn"][:, :], rows(net.X[:, bass.ds(t, 1), :]), net.rstd[:, bass.ds(t, 1)],
                                      net.shift[:, bass.ds(t, 1)], ALU.mult, ALU.add).then_inc(s["xn"], 1)
                    wait(net, dve, s["mm"], t + 1)
                    dve.tensor_scalar(b["kx"][:, :], ps_kv[:, 0:D], 0.0, None, ALU.min).then_inc(s["kmin"], 1)
                    dve.tensor_copy(b["vv"][:, :, 0:P], ps_kv[:, D:2 * D].rearrange("p (a b) -> p a b", a=2))
                    for i in range(2):
                        dve.tensor_scalar(b["vv"][:, i, P:P + 1], net.const("valid")[:, bass.ds(t, 1)], 1.0, None, ALU.mult)
                    wait(net, dve, s["kexp"], t + 1)
                    dve.scalar_tensor_tensor(b["ke"][:, :], ps_kv[:, 0:D], 0.0, b["kx"][:, :], ALU.max, ALU.add).then_inc(s["kv_ready"], 1)
                    wait(net, dve, s["kv_mm"], t + 1)
                    dve.tensor_tensor(b["kvacc"][:, :, 0:P + 1], b["kvacc"][:, :, 0:P + 1],
                                      ps_sum[:, 0:264].rearrange("p (a b) -> p a b", a=2)[:, :, 0:P + 1],
                                      ALU.add).then_inc(s["kv_used"], 1)
                    dve.drain()
                for i in range(2):
                    dve.tensor_tensor(net.kv[:, i, :], b["kvacc"][:, i, 0:P], net.const("block32"), ALU.mult)
                    dve.tensor_scalar(net.ksum[:, i, :], net.const("head32"), b["kvacc"][:, i, P:P + 1], None, ALU.mult)

            @block.scalar
            def _(act):
                act.sem_inc(s["tab_out"], 1)
                with act.Fori(0, TILES) as t:
                    wait(net, act, s["tr"], t + 1)
                    act.activation(rows(b["xnT"][:, :, :]), ps_tr[:, 0:D], ACT.Copy).then_inc(s["xnT"], 1)
                    wait(net, act, s["kmin"], t + 1)
                    act.activation(b["kx"][:, :], b["kx"][:, :], ACT.Exp).then_inc(s["kexp"], 1)
                    wait(net, act, s["mm"], t + 1)
                    act.activation(net.node_src[:, bass.ds(t, 1), :].rearrange("p a b -> p (a b)"), ps_tab[:, D:D + 4], ACT.Copy)
                    act.activation(net.node_dst[:, bass.ds(t, 1), :].rearrange("p a b -> p (a b)"), ps_tab[:, D + 4:D + 8], ACT.Copy)
                    wait(net, act, s["tab_out"], 16 * t + 1)
                    act.activation(b["tab"][:, 0:D], ps_tab[:, 0:D], ACT.Copy).then_inc(s["tab_sb"], 1)
                act.sem_inc(s["end"], 1)

            @block.tensor
            def _(pe):
                pe.wait_ge(s["w_in"], 64)
                for i in range(2):
                    for k in range(2):
                        ins = pe.matmul(ps_tab[:, 8 * i:8 * i + 8], b["wT"][:, k, i * P:(i + 1) * P], b["al"][:, k, :],
                                        start=(k == 0), stop=(k == 1))
                ins.then_inc(s["fold_ps"], 1)
                pe.wait_ge(s["folded"], 1)
                with pe.Fori(0, TILES) as t:
                    wait(net, pe, s["xn"], t + 1)
                    for k in range(2):
                        ins = pe.transpose(ps_tr[:, k * P:(k + 1) * P], b["xn"][:, k * P:(k + 1) * P], net.const("ident"))
                    ins.then_inc(s["tr"], 1)
                    wait(net, pe, s["xnT"], t + 1)
                    for k in range(2):
                        pe.matmul(ps_tab[:, 0:264], b["xnT"][:, k, :], b["w"][:, k, :], start=(k == 0), stop=(k == 1))
                    for k in range(2):
                        ins = pe.matmul(ps_kv[:, :], b["xnT"][:, k, :], b["wkv"][:, k, :], start=(k == 0), stop=(k == 1))
                    ins.then_inc(s["mm"], 1)
                    wait(net, pe, s["kv_ready"], t + 1)
                    for i in range(2):
                        ins = pe.matmul(ps_sum[:, i * 132:i * 132 + P + 1], b["ke"][:, i * P:(i + 1) * P], b["vv"][:, i, 0:P + 1],
                                        start=True, stop=True)
                    ins.then_inc(s["kv_mm"], 1)



def pad_edges_stage(nc, net):
    with ExitStack() as c:
        b = buffers(nc, c, "pad", minus_i=[64])
        with stage(nc, "pad", ["ready", "moved"]) as (block, s):
            @block.vector
            def _(dve):
                dve.memset(b["minus_i"][:, :], -1).then_inc(s["ready"], 1)

            @block.sync
            def _(sp):
                pads = EPAD - E
                for src, dst in ((net.inp["src"], net.src_pad), (net.inp["dst"], net.dst_pad)):
                    flat = dst.rearrange("t e -> (t e)")
                    sp.dma_start(flat[0:E].rearrange("(a b) -> a b", a=125),
                                 src.rearrange("o (a b) -> (o a) b", a=125)).then_inc(s["moved"], 16)
                sp.wait_ge(s["ready"], 1)
                for dst in (net.src_pad, net.dst_pad):
                    sp.dma_start(dst.rearrange("t e -> (t e)")[E:EPAD].rearrange("(a b) -> a b", b=64),
                                 b["minus_i"][0:pads // 64, :]).then_inc(s["moved"], 16)
                sp.dma_start(net.start_rec.rearrange("(p a b) c -> p a (b c)", p=P, a=28), net.zeros[:, 0:448].unsqueeze(1).to_broadcast([P, 28, 448])).then_inc(s["moved"], 16)
                sp.wait_ge(s["moved"], 80)


def degree_work(nc, net, c, block, s, b):
    G = 8
    oh = dict(
        lo=c.enter_context(nc.sbuf_tensor("deg_hot_lo", [P, 2, G, P], mybir.dt.bfloat16)),
        hi=c.enter_context(nc.sbuf_tensor("deg_hot_hi", [P, 2, G, TILES], mybir.dt.bfloat16)))
    d = buffers(nc, c, "deg", raw_i=[EROW], lo_i=[EROW])
    digits = net.agg[:, :, :].rearrange("p a b -> p (a b)")[:, 0:4 * EROW].rearrange("p (a q g) -> p a q g", a=2, q=2)
    d["lo"], d["hi"] = digits[:, 0, :, :], digits[:, 1, :, :]
    ps = net.PS[0:2]
    iota = net.PS[7][:, 0:P]
    acc = [net.degree, net.src_degree]

    @block.vector
    def _(dve):
        dve.sem_inc(s["deg_add"], 2)
        dve.tensor_copy(iota, net.const("iota"))
        for q in range(2):
            dve.memset(acc[q][:, :], 0.0)
        for q, raw in enumerate((b["dst_i"], b["src_i"])):
            dve.wait_ge(s["edges_in"], 32)
            dve.tensor_scalar(d["raw_i"][:, :], raw[:, :], 7, None, ALU.arith_shift_right)
            dve.tensor_scalar(d["lo_i"][:, :], raw[:, :], P - 1, None, ALU.bitwise_and)
            dve.drain()
            dve.tensor_copy(d["hi"][:, q, :], d["raw_i"][:, :])
            dve.tensor_copy(d["lo"][:, q, :], d["lo_i"][:, :])
            dve.drain()
        with dve.Fori(0, EROW // G) as it:
            for q in range(2):
                for wide, num, out in ((P, d["lo"], oh["lo"]), (TILES, d["hi"], oh["hi"])):
                    ins = dve.tensor_tensor(out[:, q, :, :], iota[:, 0:wide].unsqueeze(1).to_broadcast([P, G, wide]),
                                            num[:, q, bass.ds(it * G, G)].unsqueeze(2).to_broadcast([P, G, wide]), ALU.is_equal)
                ins.then_inc(s["deg_hot"], 1)
            for q in range(2):
                wait(net, dve, s["deg_mm"], it * 2 + q + 1)
                dve.tensor_tensor(acc[q][:, :], acc[q][:, :], ps[q][:, 0:TILES], ALU.add).then_inc(s["deg_add"], 1)
            dve.drain()

    @block.tensor
    def _(pe):
        with pe.Fori(0, EROW // G) as it:
            for q in range(2):
                wait(net, pe, s["deg_hot"], it * 2 + q + 1)
                wait(net, pe, s["deg_add"], 2 * it + q + 1)
                for g in range(G):
                    ins = pe.matmul(ps[q][:, 0:TILES], oh["lo"][:, q, g, :], oh["hi"][:, q, g, :],
                                    start=(g == 0), stop=(g == G - 1))
                ins.then_inc(s["deg_mm"], 1)


def gather_stage(nc, net, name, works):
    SET = 8
    with ExitStack() as c:
        b = buffers(nc, c, name, src_i=[EROW], dst_i=[EROW], idx_src_i=[EROW], idx_i=[2, SET], land=[2, SET, H])
        names = ["edges_in", "clipped", "idx_ready", "gp_landed0", "gp_landed1", "taken0", "taken1",
                 "deg_hot", "deg_mm", "deg_add", "noise_clear", "noise_in", "keys_ready", "keys_out", "keys_in"]
        with stage(nc, name, names) as (block, s):
            landed, taken = (s["gp_landed0"], s["gp_landed1"]), (s["taken0"], s["taken1"])

            @block.sync
            def _(sp):
                sp.dma_start(b["src_i"][:, :], net.src_pad.rearrange("(p a) e -> p (a e)", p=P) if EROW % P == 0 else
                             net.src_pad.rearrange("t e -> (t e)").rearrange("(p g) -> p g", p=P)).then_inc(s["edges_in"], 16)
                sp.dma_start(b["dst_i"][:, :], net.dst_pad.rearrange("t e -> (t e)").rearrange("(p g) -> p g", p=P)).then_inc(s["edges_in"], 16)
                sp.wait_ge(s["edges_in"], 32)

            @block.gpsimd
            def _(pool):
                pool.wait_ge(s["edges_in"], 32)
                pool.tensor_scalar(b["idx_src_i"][:, :], b["src_i"][:, :], 0, None, ALU.max).then_inc(s["clipped"], 1)
                pool.wait_ge(s["clipped"], 1)
                with pool.Fori(0, EROW // (2 * SET)) as it:
                    for q in range(2):
                        wait(net, pool, taken[q], it + 1)
                        pool.tensor_copy(b["idx_i"][:, q, :], b["idx_src_i"][:, bass.ds((it * 2 + q) * SET, SET)]).then_inc(s["idx_ready"], 1)
                        wait_apart(net, pool, s["idx_ready"], it * 2 + q + 1)
                        for r in range(SET):
                            pool.indirect_dma_start(b["land"][:, q, r, :], None, net.src_tab,
                                                    bass.IndirectOffsetOnAxis(ap=b["idx_i"][:, q, r:r + 1], axis=0)).then_inc(landed[q], 16)

            @block.scalar
            def _(act):
                for q in range(2):
                    act.sem_inc(taken[q], 1)
                with act.Fori(0, EROW // (2 * SET)) as it:
                    for q in range(2):
                        wait(net, act, landed[q], (it + 1) * 16 * SET)
                        act.activation(net.edge[:, bass.ds((it * 2 + q) * SET * H, SET * H)], b["land"][:, q, :, :].rearrange("p a b -> p (a b)"),
                                       ACT.Copy).then_inc(taken[q], 1)

            for work in works:
                work(nc, net, c, block, s, b)


def index_stage(nc, net):
    with ExitStack() as c:
        b = buffers(nc, c, "index", within=[TILES], total=[TILES], run=[TILES], f=[TILES], thr_i=[TILES], thr=[TILES],
                    hit=[TILES], tile=[SBLK], tile128=[SBLK], tile_i=[SBLK], etile=[SBLK], 
                    rows_i=[SBLK, 2, P], rows=[SBLK, 2, P])
        pa, pb, pt = net.PS[0], net.PS[1], net.PS[2]
        with stage(nc, "index", ["sums", "etile", "gp_rows_in", "rows_f", "tr", "copied", "tile_out", "tile_rdy"]) as (block, s):
            @block.tensor
            def _(pe):
                pe.matmul(pa[:, 0:TILES], net.const("upper"), net.degree[:, :], start=True, stop=True)
                pe.matmul(pb[:, 0:TILES], net.const("ones"), net.degree[:, :], start=True, stop=True).then_inc(s["sums"], 1)
                for j in range(SBLK):
                    pe.wait_ge(s["rows_f"], j + 1)
                    if j:
                        pe.wait_ge(s["copied"], j)
                    for q in range(2):
                        ins = pe.transpose(pt[:, q * P:(q + 1) * P], b["rows"][:, j, q, :], net.const("ident"))
                    ins.then_inc(s["tr"], 1)

            @block.vector
            def _(dve):
                dve.wait_ge(s["sums"], 1)
                dve.tensor_copy(b["total"][:, :], pb[:, 0:TILES])
                dve.tensor_copy(b["within"][:, :], pa[:, 0:TILES])
                dve.drain()
                dve.tensor_tensor_scan(b["run"][:, :], net.const("ones")[:, 0:TILES], b["total"][:, :], 0.0, ALU.mult, ALU.add)
                dve.drain()
                dve.tensor_tensor(b["run"][:, :], b["run"][:, :], b["total"][:, :], ALU.subtract)
                dve.drain()
                dve.tensor_tensor(b["f"][:, :], b["run"][:, :], b["within"][:, :], ALU.add)
                dve.drain()
                dve.tensor_scalar(b["hit"][:, :], net.degree[:, :], 0.0, float(FAR), ALU.is_equal, ALU.mult)
                dve.drain()
                dve.tensor_tensor(net.starts[:, :], b["f"][:, :], b["hit"][:, :], ALU.add)
                dve.tensor_tensor(b["f"][:, :], b["f"][:, :], net.degree[:, :], ALU.add)
                dve.drain()
                dve.tensor_scalar(net.ends[:, :], b["f"][:, :], 1.0, 0.0, ALU.subtract, ALU.max)
                dve.tensor_copy(b["thr_i"][:, :], b["run"][:, :])
                dve.drain()
                dve.tensor_scalar(b["thr_i"][:, :], b["thr_i"][:, :], 8, None, ALU.arith_shift_right)
                dve.drain()
                dve.tensor_copy(b["thr"][:, :], b["thr_i"][:, :])
                dve.drain()
                dve.tensor_tensor(b["thr"][:, 1:TILES], b["thr"][:, 1:TILES], net.const("bound"), ALU.add)
                dve.drain()
                for j in range(SBLK):
                    dve.tensor_scalar(b["hit"][:, 1:TILES], b["thr"][:, 1:TILES], net.const("step")[:, j:j + 1], None, ALU.is_le,
                                      ALU.add, accum_out=b["tile"][:, j:j + 1])
                    dve.drain()
                dve.tensor_tensor(b["etile"][:, :], net.const("step"), b["tile"][:, :], ALU.subtract)
                dve.tensor_scalar(b["tile128"][:, :], b["tile"][:, :], float(P), None, ALU.mult)
                dve.tensor_scalar(b["tile_i"][:, :], b["tile"][:, :], float(D + H), None, ALU.mult).then_inc(s["tile_rdy"], 1)
                dve.drain()
                dve.scalar_tensor_tensor(b["etile"][:, :], b["etile"][:, :], 2.0, net.const("half"), ALU.mult, ALU.add)
                dve.drain()
                dve.tensor_scalar(net.step_et[:, :], b["etile"][:, :], float(ETILES - 1), None, ALU.min).then_inc(s["etile"], 1)
                for j in range(SBLK):
                    dve.wait_ge(s["gp_rows_in"], 32 * SBLK)
                    dve.tensor_scalar(b["rows"][:, j, 0, :], b["rows_i"][:, j, 0, :], 0.0, None, ALU.max)
                    dve.tensor_scalar(b["rows"][:, j, 1, :], b["rows_i"][:, j, 1, :], b["tile128"][:, j:j + 1], None, ALU.subtract).then_inc(s["rows_f"], 1)
                    dve.wait_ge(s["tr"], j + 1)
                    dve.tensor_copy(net.step_src[:, j * P:(j + 1) * P], pt[:, 0:P])
                    dve.tensor_copy(net.step_dst[:, j * P:(j + 1) * P], pt[:, P:2 * P]).then_inc(s["copied"], 1)

            @block.gpsimd
            def _(pool):
                pool.wait_ge(s["etile"], 1)
                for j in range(SBLK):
                    for q, tab in enumerate((net.src_pad, net.dst_pad)):
                        pool.indirect_dma_start(b["rows_i"][:, j, q, :], None, tab,
                                                bass.IndirectOffsetOnAxis(ap=net.step_et[:, j:j + 1], axis=0)).then_inc(s["gp_rows_in"], 16)

            @block.sync
            def _(sp):
                sp.wait_ge(s["tile_rdy"], 1)
                with nc.allow_non_contiguous_dma("13 x 128 step numbers"):
                    sp.dma_start(net.tile_row.rearrange("o (j p) -> p (o j)", p=P), b["tile_i"][:, :]).then_inc(s["tile_out"], 16)
                sp.wait_ge(s["tile_out"], 16)


def weight_stage(nc, net, name, slope):
    rec = net.agg[:, :, :].rearrange("p a b -> p (a b)")[:, 0:EROW * 8].rearrange("p (g c) -> p g c", c=8)
    edge = net.edge[:, 0:EROW * H].rearrange("p (g c) -> p g c", c=H)
    w_rows = net.agg[:, :, :].rearrange("p a b -> p (a b)")[:, 0:SBLK * 512].rearrange("p (j c) -> p j c", c=512)
    with ExitStack() as c:
        b = buffers(nc, c, name, dst=[EROW], pen=[EROW], keep=[EROW], run=[EROW, H],
                    match=[P], diag=[H, P], spread=[H, P], carry=[H], node=[TILES, 8], z=[TILES, H],
                    first_i=[1], first=[8], hit=[TILES])
        dst_i = net.agg[:, :, :].rearrange("p a b -> p (a b)")[:, 0:EROW].bitcast(I32)
        p_last, p_row, p_t = net.PS[0], net.PS[1], net.PS[2:6]
        names = ["dst_in", "last_ps", "diag", "spread", "carried", "run_out", "gp_node_in", "node_done", "node_out", "first_idx",
                 "gp_first_in", "gp_scatter", "rec_in", "rec_ready", "exp_in", "exp_out", "w_out", "gp_rows_in", "tr", "copied", "dcopy", "etile", "sums"]
        with stage(nc, name, names) as (block, s):
            edges_of = lambda a: a.rearrange("(p g) c -> p g c", p=P)

            @block.sync
            def _(sp):
                sp.dma_start(dst_i, net.dst_pad.rearrange("t e -> (t e)").rearrange("(p g) -> p g", p=P)).then_inc(s["dst_in"], 16)
                sp.wait_ge(s["carried"], 1)
                sp.dma_start(edges_of(net.run_max), b["run"][:, :, :]).then_inc(s["run_out"], 16)
                sp.wait_ge(s["node_done"], 1)
                sp.dma_start(net.node_rec.rearrange("(t p) c -> p t c", p=P), b["node"][:, :, :]).then_inc(s["node_out"], 16)
                sp.wait_ge(s["gp_scatter"], 16 * TILES)
                sp.dma_start(rec, edges_of(net.start_rec)).then_inc(s["rec_in"], 16)
                sp.wait_ge(s["exp_out"], 1)
                sp.dma_start(net.weights.rearrange("t c -> (t c)").rearrange("(p g) -> p g", p=P), net.edge[:, 0:EROW * H]).then_inc(s["w_out"], 16)
                sp.wait_ge(s["w_out"], 16)

            @block.gpsimd
            def _(pool):
                pool.wait_ge(s["run_out"], 16)
                for t in range(TILES):
                    pool.indirect_dma_start(net.node_max[:, t, :], None, net.run_max,
                                            bass.IndirectOffsetOnAxis(ap=net.ends[:, t:t + 1], axis=0)).then_inc(s["gp_node_in"], 16)
                pool.wait_ge(s["node_done"], 1)
                for t in range(TILES):
                    pool.indirect_dma_start(net.start_rec, bass.IndirectOffsetOnAxis(ap=net.starts[:, t:t + 1], axis=0),
                                            b["node"][:, t, :], None, bounds_check=EPAD - 1, oob_is_err=False).then_inc(s["gp_scatter"], 16)
                pool.wait_ge(s["node_out"], 16)
                pool.wait_ge(s["first_idx"], 1)
                pool.indirect_dma_start(b["first"][:, :], None, net.node_rec,
                                        bass.IndirectOffsetOnAxis(ap=b["first_i"][:, 0:1], axis=0)).then_inc(s["gp_first_in"], 16)
                pool.wait_ge(s["w_out"], 16)
                for j in range(SBLK):
                    pool.indirect_dma_start(w_rows[:, j, :], None, net.weights,
                                            bass.IndirectOffsetOnAxis(ap=net.step_et[:, j:j + 1], axis=0)).then_inc(s["gp_rows_in"], 16)

            @block.tensor
            def _(pe):
                pe.wait_ge(s["diag"], 1)
                pe.matmul(p_last[:, 0:P], net.const("ones"), b["diag"][:, 0, :], start=True, stop=True).then_inc(s["last_ps"], 1)
                pe.wait_ge(s["diag"], 2)
                pe.matmul(p_row[:, :], net.const("ones"), b["diag"][:, :, :].rearrange("p a b -> p (a b)"), start=True, stop=True).then_inc(s["spread"], 1)
                for j in range(SBLK):
                    pe.wait_ge(s["gp_rows_in"], 16 * SBLK)
                    if j >= 4:
                        pe.wait_ge(s["copied"], j - 3)
                    for h in range(H):
                        ins = pe.transpose(p_t[j % 4][:, h * P:(h + 1) * P],
                                           w_rows[:, j, :].rearrange("p (e h) -> p e h", h=H)[:, :, h], net.const("ident"))
                    ins.then_inc(s["tr"], 1)

            @block.scalar
            def _(act):
                act.wait_ge(s["exp_in"], 1)
                act.activation(net.edge[:, 0:EROW * H], net.edge[:, 0:EROW * H], ACT.Exp).then_inc(s["exp_out"], 1)
                for j in range(SBLK):
                    act.wait_ge(s["tr"], j + 1)
                    act.wait_ge(s["w_out"], 16)
                    act.activation(net.edge[:, j * P * H:(j + 1) * P * H].rearrange("p (s h) -> p h s", h=H),
                                   p_t[j % 4][:, :].rearrange("p (h s) -> p h s", h=H), ACT.Copy).then_inc(s["copied"], 1)

            @block.vector
            def _(dve):
                flat = lambda a: a.rearrange("p a b -> p (a b)")
                dve.wait_ge(s["dst_in"], 16)
                dve.tensor_copy(b["dst"][:, :], dst_i)
                dve.drain()
                dve.tensor_scalar(b["first_i"][:, :], b["dst"][:, 0:1], 0.0, None, ALU.max).then_inc(s["first_idx"], 1)
                dve.tensor_scalar(b["diag"][:, 0, :], net.const("ident"), b["dst"][:, EROW - 1:EROW], None, ALU.mult).then_inc(s["diag"], 1)
                dve.tensor_tensor(b["keep"][:, 1:EROW], b["dst"][:, 1:EROW], b["dst"][:, 0:EROW - 1], ALU.is_equal)
                dve.memset(b["keep"][:, 0:1], 0.0)
                dve.drain()
                dve.tensor_scalar(b["pen"][:, :], b["keep"][:, :], BIG, BIG, ALU.mult, ALU.subtract)
                dve.drain()
                dve.memset(b["pen"][:, 0:1], 0.0)
                dve.wait_ge(s["last_ps"], 1)
                dve.tensor_scalar(b["match"][:, :], p_last[:, 0:P], b["dst"][:, 0:1], None, ALU.is_equal)
                dve.drain()
                dve.tensor_tensor(b["match"][:, :], b["match"][:, :], net.const("lower"), ALU.mult)
                dve.drain()
                dve.tensor_scalar(b["match"][:, :], b["match"][:, :], BIG, BIG, ALU.mult, ALU.subtract)
                for h in range(H):
                    dve.tensor_tensor_scan(b["run"][:, :, h], b["pen"][:, :], edge[:, :, h], -BIG, ALU.add, ALU.max)
                dve.drain()
                for h in range(H):
                    ins = dve.tensor_scalar(b["diag"][:, h, :], net.const("ident"), b["run"][:, EROW - 1, h:h + 1], None, ALU.mult)
                ins.then_inc(s["diag"], 1)
                dve.wait_ge(s["spread"], 1)
                for h in range(H):
                    dve.tensor_tensor(b["spread"][:, h, :], b["match"][:, :], p_row[:, h * P:(h + 1) * P], ALU.add)
                dve.drain()
                dve.tensor_reduce(b["carry"][:, :], b["spread"][:, :, :], AX.X, ALU.max)
                dve.drain()
                for h in range(H):
                    ins = dve.tensor_tensor_scan(b["run"][:, :, h], b["pen"][:, :], edge[:, :, h], b["carry"][:, h:h + 1], ALU.add, ALU.max)
                ins.then_inc(s["carried"], 1)
                dve.wait_ge(s["gp_node_in"], 16 * TILES)
                dve.tensor_tensor(flat(b["z"][:, :, :]), flat(net.node_dst[:, :, :]), flat(net.node_max[:, :, :]), ALU.add)
                dve.tensor_copy(b["node"][:, :, 0:H], net.node_dst[:, :, :])
                dve.drain()
                dve.scalar_tensor_tensor(flat(net.node_max[:, :, :]), flat(b["z"][:, :, :]), slope, flat(b["z"][:, :, :]), ALU.mult, ALU.max)
                dve.drain()
                dve.tensor_scalar(b["hit"][:, :], net.degree[:, :], 0.0, None, ALU.is_gt)
                dve.drain()
                for h in range(H):
                    dve.tensor_tensor(net.node_max[:, :, h], net.node_max[:, :, h], b["hit"][:, :], ALU.mult)
                dve.drain()
                dve.tensor_copy(b["node"][:, :, H:2 * H], net.node_max[:, :, :]).then_inc(s["node_done"], 1)
                dve.wait_ge(s["rec_in"], 16)
                dve.wait_ge(s["gp_first_in"], 16)
                dve.tensor_copy(rec[:, 0, :], b["first"][:, :])
                dve.drain()
                for k in range(8):
                    dve.tensor_tensor_scan(rec[:, :, k], b["keep"][:, :], rec[:, :, k], 0.0, ALU.mult, ALU.add)
                dve.drain()
                dve.tensor_tensor(edge, edge, rec[:, :, 0:H], ALU.add)
                dve.drain()
                dve.scalar_tensor_tensor(flat(edge), flat(edge), slope, flat(edge), ALU.mult, ALU.max)
                dve.drain()
                dve.tensor_tensor(edge, edge, rec[:, :, H:2 * H], ALU.subtract)
                dve.drain()
                dve.tensor_scalar(flat(edge), flat(edge), 0.0, None, ALU.min).then_inc(s["exp_in"], 1)


def aggregate_stage(nc, net, name):
    SETS, SET, RING = 4, 4, 4
    U = SETS * SET
    PAIRS = U // 2
    A_HEADS = 3
    AHEAD = RING - 1
    aggf = net.agg[:, :, :].rearrange("p a b -> p (a b)")
    with ExitStack() as c:
        b = buffers(nc, c, name, idx_i=[SETS, SET], got=[U, D], hot=[RING, 2, P], wx=[RING, 2, D])
        where = c.enter_context(nc.sbuf_tensor(f"{name}_where", [1, SPAD], I32))
        names = ["where_in", "idx_ready"] + [f"gp_landed{i}" for i in range(SETS)] + \
                ["weighed", "hot", "mm"]
        with stage(nc, name, names) as (block, s):
            landed = (s["gp_landed0"], s["gp_landed1"], s["gp_landed2"], s["gp_landed3"])

            @block.sync
            def _(sp):
                sp.dma_start(where[:, :], net.tile_row).then_inc(s["where_in"], 16)
                sp.wait_ge(s["where_in"], 16)

            @block.gpsimd
            def _(pool):
                with pool.Fori(0, STEPS // U) as it:
                    for q in range(SETS):
                        wait_apart(net, pool, s["weighed"], it * U + (q + 1) * SET)
                        wait(net, pool, s["hot"], it * U + (q + 1) * SET)
                        pool.tensor_copy(b["idx_i"][:, q, :], net.step_src[:, bass.ds((it * SETS + q) * SET, SET)]).then_inc(s["idx_ready"], 1)
                        wait_apart(net, pool, s["idx_ready"], it * SETS + q + 1)
                        for r in range(SET):
                            pool.indirect_dma_start(b["got"][:, q * SET + r, :], None, net.table,
                                                    bass.IndirectOffsetOnAxis(ap=b["idx_i"][:, q, r:r + 1], axis=0)).then_inc(landed[q], 16)

            @block.scalar
            def _(act):
                act.sem_inc(s["weighed"], U)
                with act.Fori(0, STEPS // U) as it:
                    for u in range(U):
                        if u % SET == 0:
                            wait(net, act, landed[u // SET], (it + 1) * 16 * SET)
                        if u % 2 == 0:
                            wait(net, act, s["mm"], it * PAIRS + u // 2 + 1)
                        for h in range(A_HEADS):
                            ins = act.activation(b["wx"][:, u // 2 % RING, u % 2, h * 64:(h + 1) * 64], b["got"][:, u, h * 64:(h + 1) * 64], ACT.Copy,
                                                 scale=net.edge[:, bass.ds((it * U + u) * H + h, 1)])
                        ins.then_inc(s["weighed"], 1)

            @block.tensor
            def _(pe):
                pe.sem_inc(s["mm"], RING)
                with pe.Fori(0, STEPS // U) as it:
                    for k in range(PAIRS):
                        r = k % RING
                        wait(net, pe, s["hot"], it * U + 2 * (k + 1) + U)
                        wait(net, pe, s["weighed"], it * U + 2 * (k + 1) + U)
                        for i in range(2):
                            pe.matmul(net.PS[r][:, 0:D], b["hot"][:, r, i, :], b["wx"][:, r, i, :], start=(i == 0), stop=(i == 1))
                        for i in range(2):
                            ins = pe.matmul(net.PS[r][:, D:D + H], b["hot"][:, r, i, :], net.edge[:, bass.ds((it * U + 2 * k + i) * H, H)],
                                            start=(i == 0), stop=(i == 1))
                        ins.then_inc(s["mm"], 1)

            @block.vector
            def _(dve):
                dve.sem_inc(s["hot"], U)
                dve.memset(aggf, 0.0)
                dve.wait_ge(s["where_in"], 16)

                def one_hot(it, k):
                    wait(net, dve, s["mm"], it * PAIRS + k + 1)
                    for i in range(2):
                        step = it * U + 2 * k + i
                        dve.tensor_scalar(b["hot"][:, k % RING, i, :], net.const("iota"), net.step_dst[:, bass.ds(step, 1)], None, ALU.is_equal)
                        if i == 0 and 2 * k % SET == 0:
                            wait(net, dve, landed[2 * k // SET], (it + 1) * 16 * SET)
                        for h in range(A_HEADS, H):
                            ins = dve.tensor_scalar(b["wx"][:, k % RING, i, h * 64:(h + 1) * 64], b["got"][:, 2 * k + i, h * 64:(h + 1) * 64],
                                                    net.edge[:, bass.ds(step * H + h, 1)], None, ALU.mult)
                        ins.then_inc(s["hot"], 1)

                def round_of(it, last):
                    for k in range(PAIRS):
                        at = dve.value_load(where[0:1, bass.ds(it * U + 2 * k, 1)], min_val=0, max_val=(TILES - 1) * (D + H))
                        wait(net, dve, s["mm"], it * PAIRS + k + 1 + RING)
                        dve.tensor_tensor(aggf[:, bass.ds(at, D + H)], aggf[:, bass.ds(at, D + H)], net.PS[k % RING][:, 0:D + H], ALU.add)
                        dve.drain()
                        if k + AHEAD < PAIRS:
                            one_hot(it, k + AHEAD)
                        elif not last:
                            one_hot(it + 1, k + AHEAD - PAIRS)

                for k in range(AHEAD):
                    one_hot(0, k)
                with dve.Fori(0, STEPS // U - 1) as it:
                    round_of(it, False)
                round_of(STEPS // U - 1, True)


SMALL = dict(six=[6], mv=[2], var=[1], rs=[1])


def pair_buffers(nc, c, name, spare, **shapes):
    first, second, at = buffers(nc, c, name, **shapes), {}, 0
    for k, v in shapes.items():
        size = int(np.prod(v))
        part = spare[:, at:at + size]
        if len(v) == 2:
            part = part.rearrange("p (a b) -> p a b", a=v[0])
        second[k] = part
        at += size
    return first, second


def norm_value(it, ws, w, k):
    return it * 6 + k * len(ws) + w + 1


def norm_stats(dve, s, b, x):
    dve.bn_stats(b["six"][:, :], x)
    dve.drain()
    dve.bn_aggr(b["mv"][:, :], b["six"][:, :])
    dve.drain()
    dve.tensor_scalar(b["var"][:, :], b["mv"][:, 1:2], LN_EPS, None, ALU.add).then_inc(s["var_ready"], 1)


def norm_apply(net, dve, s, b, x, out, value, gain=None, shift=None):
    wait(net, dve, s["rstd_ready"], value)
    ins = dve.tensor_scalar(out, x, b["mv"][:, 0:1], b["rs"][:, :], ALU.subtract, ALU.mult)
    if gain is not None:
        dve.drain()
        dve.tensor_tensor(out, out, gain, ALU.mult)
        dve.drain()
        ins = dve.tensor_tensor(out, out, shift, ALU.add)
    return ins


def norm_power(net, pool, s, b, value):
    wait(net, pool, s["var_ready"], value)
    pool.tensor_tensor(b["rs"][:, :], b["var"][:, :], net.const("mhalf"), ALU.pow).then_inc(s["rstd_ready"], 1)


def top_two(dve, net, n, g, b):
    pair = lambda t: t[:, 0:n * n].rearrange("p (e j) -> p e j", e=n)
    mine = g.unsqueeze(2).to_broadcast([P, n, n])
    theirs = g.unsqueeze(1).to_broadcast([P, n, n])
    dve.tensor_tensor(pair(b["gt"]), theirs, mine, ALU.is_gt)
    dve.tensor_tensor(pair(b["eq"]), theirs, mine, ALU.is_equal)
    dve.drain()
    dve.tensor_tensor(pair(b["eq"]), pair(b["eq"]), pair(b["before"]), ALU.mult)
    dve.drain()
    dve.tensor_tensor(pair(b["gt"]), pair(b["gt"]), pair(b["eq"]), ALU.add)
    dve.drain()
    dve.tensor_reduce(b["sel"][:, 0:n], pair(b["gt"]), AX.X, ALU.add)
    dve.drain()
    dve.tensor_scalar(b["sel"][:, 0:n], b["sel"][:, 0:n], 2.0, None, ALU.is_lt)
    dve.drain()


def make_before(dve, n, b):
    dve.memset(b["before"][:, :], 0.0)
    dve.drain()
    for e in range(1, n):
        dve.memset(b["before"][:, e * n:e * n + e], 1.0)


def combine_stage(nc, net):
    with ExitStack() as c:
        b = buffers(nc, c, "comb", wq=[2, D], wres=[2, D], wm=[2, D], w1=[4, 512], w2=[4, D], norms=[4, D],
                    f1=[2, 768], f1b=[6], f2=[2, P], f2b=[1], e2=[4, 64], eb2=[4], f3=[D], b3=[D], e3=[4, D], gw=[2, 4], gb=[4],
                    before=[16])
        bw = pair_buffers(nc, c, "comb_t", net.edge,
                          xn=[D], cat=[4, P], qx=[D], qe=[D], den=[8], msg=[D], hT=[4, P], sum=[D], rden=[4], nb=[D],
                          yT=[2, P], h1=[6, P], h2=[P], h2e=[4, P],
                          gt=[16], eq=[16], sel=[4], g=[4], gmax=[1], gsum=[1], x1=[D], y=[D], **SMALL)
        for t in bw:
            t["before"] = b["before"]
        TURN, MAIN, SIDE, KEEP = ([net.PS[4 * w + i] for w in range(2)] for i in range(4))
        names = ["w_in", "xn", "tr_x", "xT", "q", "qmin", "qexp", "qe", "msg", "msgn", "tr_m", "mT", "wm", "m1", "tr_1", "oT",
                 "h", "hr", "w2", "x1y", "tr_y", "yT", "f1", "f1r", "f2", "f2r", "f3", "gl", "gexp_in", "gexp", "g2_in", "g2",
                 "var_ready", "rstd_ready", "done"]
        with stage(nc, "comb", names) as (block, s):
            ident = net.const("ident")

            @block.sync
            def _(sp):
                i = net.inp
                loads = [(b["wq"][:, :, :], weight(i["m0_wq"])), (b["wres"][:, :, :], weight(i["g0_res"])), (b["wm"][:, :, :], weight(i["m0_wm"])),
                         (b["w1"][:, :, :], weight(i["m0_w1"])), (b["w2"][:, :, :], weight(i["m0_w2"])),
                         (rows(b["norms"][:, :, :]), i["m0_norms"].to_broadcast([P, 4 * D])),
                         (b["f1"][:, :, :], weight(i["f0_w1"])), (b["f1b"][:, :], i["f0_b1"]), (b["f2"][:, :, :], weight(i["f0_w2"])),
                         (b["f2b"][:, :], i["f0_b2"]), (rows(b["e2"][:, :, :]), i["f0_e2"]), (b["eb2"][0:64, :], i["f0_eb2"]),
                         (b["f3"][:, :], i["f0_w3"]), (b["b3"][0:1, :], i["f0_b3"]), (rows(b["e3"][0:64, :, :]), i["f0_e3"]),
                         (rows(b["e3"][64:65, :, :]), i["f0_eb3"]), (b["gw"][:, :, :], weight(i["f0_gw"])), (b["gb"][0:1, :], i["f0_gb"])]
                for dst, src in loads:
                    sp.dma_start(dst, src).then_inc(s["w_in"], 16)
                sp.wait_ge(s["w_in"], 16 * len(loads))
                sp.sem_inc(s["done"], 1)

            @block.gpsimd
            def _(pool):
                def tiles(it, ws):
                    for k in range(3):
                        for w in ws:
                            norm_power(net, pool, s, bw[w], norm_value(it, ws, w, k))

                with pool.Fori(0, TILES // 2) as it:
                    tiles(it, (0, 1))
                tiles(TILES // 2, (0,))

            @block.tensor
            def _(pe):
                pe.wait_ge(s["done"], 1)
                ones = net.const("ones")

                def tiles(it, ws):
                    n = lambda w: 2 * it + w + 1
                    for w in ws:
                        wait(net, pe, s["xn"], n(w))
                        turned(pe, net, TURN[w], bw[w]["xn"], 2).then_inc(s["tr_x"], 1)
                    for w in ws:
                        cat = bw[w]["cat"]
                        wait(net, pe, s["xT"], n(w))
                        for i in range(2):
                            ins = products(pe, MAIN[w][:, i * P:(i + 1) * P], [(b["wq"][:, k, i * P:(i + 1) * P], cat[:, k, :]) for k in range(2)])
                        ins.then_inc(s["q"], 1)
                        products(pe, KEEP[w][:, 0:D], [(cat[:, k, :], b["wres"][:, k, :]) for k in range(2)])
                    for w in ws:
                        qe = bw[w]["qe"]
                        wait(net, pe, s["qe"], n(w))
                        for i in range(2):
                            products(pe, SIDE[w][:, i * P:(i + 1) * P], [(qe[:, i * P:(i + 1) * P], net.kv[:, i, :])])
                            ins = products(pe, SIDE[w][:, D + 4 * i:D + 4 * i + 4], [(qe[:, i * P:(i + 1) * P], net.ksum[:, i, :])])
                        ins.then_inc(s["msg"], 1)
                    for w in ws:
                        wait(net, pe, s["msgn"], n(w))
                        turned(pe, net, TURN[w], bw[w]["msg"], 2).then_inc(s["tr_m"], 1)
                    for w in ws:
                        wait(net, pe, s["mT"], n(w))
                        products(pe, MAIN[w][:, 0:D], [(bw[w]["cat"][:, 2 + k, :], b["wm"][:, k, :]) for k in range(2)]).then_inc(s["wm"], 1)
                    for w in ws:
                        wait(net, pe, s["m1"], n(w))
                        turned(pe, net, TURN[w], bw[w]["msg"], 2).then_inc(s["tr_1"], 1)
                    for w in ws:
                        wait(net, pe, s["oT"], n(w))
                        for i in range(4):
                            ins = products(pe, SIDE[w][:, i * P:(i + 1) * P], [(b["w1"][:, k, i * P:(i + 1) * P], bw[w]["cat"][:, k, :]) for k in range(4)])
                        ins.then_inc(s["h"], 1)
                    for w in ws:
                        wait(net, pe, s["hr"], n(w))
                        products(pe, MAIN[w][:, 0:D], [(bw[w]["hT"][:, k, :], b["w2"][:, k, :]) for k in range(4)]).then_inc(s["w2"], 1)
                    for w in ws:
                        wait(net, pe, s["x1y"], n(w))
                        turned(pe, net, TURN[w], bw[w]["y"], 2).then_inc(s["tr_y"], 1)
                    for w in ws:
                        yT = bw[w]["yT"]
                        wait(net, pe, s["yT"], n(w))
                        products(pe, KEEP[w][:, 0:4], [(yT[:, k, :], b["gw"][:, k, :]) for k in range(2)] + [(ones[0:1, :], b["gb"][0:1, :])]).then_inc(s["gl"], 1)
                        for i in range(6):
                            out = MAIN[w][:, i * P:(i + 1) * P] if i < 4 else SIDE[w][:, (i - 4) * P:(i - 3) * P]
                            ins = products(pe, out, [(b["f1"][:, k, i * P:(i + 1) * P], yT[:, k, :]) for k in range(2)])
                        ins.then_inc(s["f1"], 1)
                    for w in ws:
                        h1 = bw[w]["h1"]
                        wait(net, pe, s["f1r"], n(w))
                        products(pe, SIDE[w][:, 0:P], [(b["f2"][:, k, :], h1[:, k, :]) for k in range(2)])
                        for e in range(4):
                            ins = products(pe, TURN[w][0:64, e * P:(e + 1) * P], [(b["e2"][:, e, :], h1[:, 2 + e, :])])
                        ins.then_inc(s["f2"], 1)
                    for w in ws:
                        wait(net, pe, s["f2r"], n(w))
                        products(pe, TURN[w][:, 0:D], [(bw[w]["h2"][:, :], b["f3"][:, :]), (ones[0:1, :], b["b3"][0:1, :])])
                        for e in range(4):
                            ins = products(pe, (MAIN, SIDE)[e // 2][w][:, (e % 2) * D:(e % 2 + 1) * D], [(bw[w]["h2e"][0:65, e, :], b["e3"][0:65, e, :])])
                        ins.then_inc(s["f3"], 1)

                with pe.Fori(0, TILES // 2) as it:
                    tiles(it, (0, 1))
                tiles(TILES // 2, (0,))

            @block.scalar
            def _(act):
                copy = lambda dst, src: act.activation(rows(dst), src, ACT.Copy)

                def tiles(it, ws):
                    n = lambda w: 2 * it + w + 1
                    for w in ws:
                        wait(net, act, s["tr_x"], n(w))
                        copy(bw[w]["cat"][:, 0:2, :], TURN[w][:, 0:D]).then_inc(s["xT"], 1)
                    for w in ws:
                        wait(net, act, s["qmin"], n(w))
                        act.activation(bw[w]["qx"][:, :], bw[w]["qx"][:, :], ACT.Exp).then_inc(s["qexp"], 1)
                    for w in ws:
                        wait(net, act, s["tr_m"], n(w))
                        copy(bw[w]["cat"][:, 2:4, :], TURN[w][:, 0:D]).then_inc(s["mT"], 1)
                    for w in ws:
                        wait(net, act, s["tr_1"], n(w))
                        copy(bw[w]["cat"][:, 2:4, :], TURN[w][:, 0:D]).then_inc(s["oT"], 1)
                    for w in ws:
                        wait(net, act, s["h"], n(w))
                        act.activation(rows(bw[w]["hT"][:, :, :]), SIDE[w][:, :], ACT.Relu).then_inc(s["hr"], 1)
                    for w in ws:
                        wait(net, act, s["tr_y"], n(w))
                        copy(bw[w]["yT"][:, :, :], TURN[w][:, 0:D]).then_inc(s["yT"], 1)
                    for w in ws:
                        wait(net, act, s["gexp_in"], n(w))
                        act.activation(bw[w]["g"][:, :], bw[w]["g"][:, :], ACT.Exp).then_inc(s["gexp"], 1)
                    for w in ws:
                        wait(net, act, s["f1"], n(w))
                        for i in range(6):
                            src = MAIN[w][:, i * P:(i + 1) * P] if i < 4 else SIDE[w][:, (i - 4) * P:(i - 3) * P]
                            ins = act.activation(bw[w]["h1"][:, i, :], src, ACT.Relu, bias=b["f1b"][:, i:i + 1])
                        ins.then_inc(s["f1r"], 1)
                    for w in ws:
                        wait(net, act, s["f2"], n(w))
                        act.activation(bw[w]["h2"][:, :], SIDE[w][:, 0:P], ACT.Relu, bias=b["f2b"][:, :])
                        for e in range(4):
                            ins = act.activation(bw[w]["h2e"][0:64, e, :], TURN[w][0:64, e * P:(e + 1) * P], ACT.Relu, bias=b["eb2"][0:64, e:e + 1])
                        ins.then_inc(s["f2r"], 1)
                    for w in ws:
                        wait(net, act, s["g2_in"], n(w))
                        act.activation(bw[w]["g"][:, :], bw[w]["g"][:, :], ACT.Exp).then_inc(s["g2"], 1)

                act.wait_ge(s["done"], 1)
                with act.Fori(0, TILES // 2) as it:
                    tiles(it, (0, 1))
                tiles(TILES // 2, (0,))

            @block.vector
            def _(dve):
                heads = lambda a, n: a.rearrange("p (h d) -> p h d", h=n)
                spread = lambda a, n, d: a.unsqueeze(2).to_broadcast([P, n, d])
                norm = lambda k: b["norms"][:, k, :]
                make_before(dve, 4, b)
                for w in range(2):
                    dve.memset(bw[w]["h2e"][64:65, :, :], 1.0)

                def tiles(it, ws):
                    n = lambda w: 2 * it + w + 1
                    x = [rows(net.X[:, bass.ds(2 * it + w, 1), :]) for w in ws]
                    for w in ws:
                        dve.tensor_scalar(bw[w]["xn"][:, :], x[w], net.rstd[:, bass.ds(2 * it + w, 1)], net.shift[:, bass.ds(2 * it + w, 1)],
                                          ALU.mult, ALU.add).then_inc(s["xn"], 1)
                    for w in ws:
                        dve.tensor_scalar(bw[w]["rden"][:, :], rows(net.agg[:, bass.ds(2 * it + w, 1), :])[:, D:D + H], 1e-9, None, ALU.max)
                    dve.drain()
                    for w in ws:
                        dve.reciprocal(bw[w]["rden"][:, :], bw[w]["rden"][:, :])
                    dve.drain()
                    for w in ws:
                        dve.tensor_tensor(heads(bw[w]["sum"][:, :], H), heads(rows(net.agg[:, bass.ds(2 * it + w, 1), :])[:, 0:D], H),
                                          spread(bw[w]["rden"][:, :], H, 64), ALU.mult)
                    for w in ws:
                        wait(net, dve, s["q"], n(w))
                        dve.tensor_scalar(bw[w]["qx"][:, :], MAIN[w][:, 0:D], 0.0, None, ALU.min).then_inc(s["qmin"], 1)
                    for w in ws:
                        wait(net, dve, s["qexp"], n(w))
                        dve.scalar_tensor_tensor(bw[w]["qe"][:, :], MAIN[w][:, 0:D], 0.0, bw[w]["qx"][:, :], ALU.max, ALU.add).then_inc(s["qe"], 1)
                    for w in ws:
                        den = bw[w]["den"][:, :]
                        wait(net, dve, s["msg"], n(w))
                        dve.tensor_scalar(den, SIDE[w][:, D:D + 8], 1e-6, None, ALU.add)
                        dve.drain()
                        dve.reciprocal(den, den)
                        dve.drain()
                        dve.tensor_tensor(heads(bw[w]["msg"][:, :], 8), heads(SIDE[w][:, 0:D], 8), spread(den, 8, 32), ALU.mult).then_inc(s["msgn"], 1)
                    for w in ws:
                        dve.tensor_tensor(bw[w]["sum"][:, :], bw[w]["sum"][:, :], KEEP[w][:, 0:D], ALU.add)
                    dve.drain()
                    for w in ws:
                        dve.scalar_tensor_tensor(bw[w]["sum"][:, :], bw[w]["sum"][:, :], 0.0, x[w], ALU.max, ALU.add)
                    dve.drain()
                    for w in ws:
                        dve.tensor_tensor(bw[w]["sum"][:, :], bw[w]["sum"][:, :], bw[w]["xn"][:, :], ALU.add)
                    for w in ws:
                        wait(net, dve, s["wm"], n(w))
                        norm_stats(dve, s, bw[w], MAIN[w][:, 0:D])
                    for w in ws:
                        norm_apply(net, dve, s, bw[w], MAIN[w][:, 0:D], bw[w]["msg"][:, :], norm_value(it, ws, w, 0), norm(0), norm(1)).then_inc(s["m1"], 1)
                    for w in ws:
                        wait(net, dve, s["w2"], n(w))
                        norm_stats(dve, s, bw[w], MAIN[w][:, 0:D])
                    for w in ws:
                        norm_apply(net, dve, s, bw[w], MAIN[w][:, 0:D], bw[w]["nb"][:, :], norm_value(it, ws, w, 1), norm(2), norm(3))
                        dve.drain()
                        dve.tensor_tensor(bw[w]["x1"][:, :], bw[w]["sum"][:, :], bw[w]["nb"][:, :], ALU.add)
                        dve.drain()
                        norm_stats(dve, s, bw[w], bw[w]["x1"][:, :])
                    for w in ws:
                        norm_apply(net, dve, s, bw[w], bw[w]["x1"][:, :], bw[w]["y"][:, :], norm_value(it, ws, w, 2)).then_inc(s["x1y"], 1)
                    for w in ws:
                        g, top = bw[w]["g"][:, :], bw[w]["gmax"][:, :]
                        wait(net, dve, s["gl"], n(w))
                        dve.tensor_reduce(top, KEEP[w][:, 0:4], AX.X, ALU.max)
                        dve.drain()
                        dve.tensor_scalar(g, KEEP[w][:, 0:4], top, None, ALU.subtract).then_inc(s["gexp_in"], 1)
                    for w in ws:
                        g, top, total = bw[w]["g"][:, :], bw[w]["gmax"][:, :], bw[w]["gsum"][:, :]
                        wait(net, dve, s["gexp"], n(w))
                        dve.tensor_reduce(total, g, AX.X, ALU.add)
                        dve.drain()
                        dve.reciprocal(total, total)
                        dve.drain()
                        dve.tensor_scalar(g, g, total, None, ALU.mult)
                        dve.drain()
                        top_two(dve, net, 4, g, bw[w])
                        dve.tensor_reduce(top, g, AX.X, ALU.max)
                        dve.drain()
                        dve.tensor_scalar(g, g, top, None, ALU.subtract).then_inc(s["g2_in"], 1)
                    for w in ws:
                        sel, total = bw[w]["sel"][:, :], bw[w]["gsum"][:, :]
                        wait(net, dve, s["g2"], n(w))
                        dve.tensor_tensor(sel, sel, bw[w]["g"][:, :], ALU.mult)
                        dve.drain()
                        dve.tensor_reduce(total, sel, AX.X, ALU.add)
                        dve.drain()
                        dve.reciprocal(total, total)
                        dve.drain()
                        dve.tensor_scalar(sel, sel, total, None, ALU.mult)
                    for w in ws:
                        wait(net, dve, s["f3"], n(w))
                        dve.tensor_tensor(bw[w]["x1"][:, :], bw[w]["x1"][:, :], TURN[w][:, 0:D], ALU.add)
                    dve.drain()
                    for e in range(4):
                        for w in ws:
                            out = bw[w]["x1"][:, :] if e < 3 else x[w]
                            dve.scalar_tensor_tensor(out, (MAIN, SIDE)[e // 2][w][:, (e % 2) * D:(e % 2 + 1) * D], bw[w]["sel"][:, e:e + 1],
                                                     bw[w]["x1"][:, :], ALU.mult, ALU.add)
                        dve.drain()

                dve.wait_ge(s["done"], 1)
                with dve.Fori(0, TILES // 2) as it:
                    tiles(it, (0, 1))
                tiles(TILES // 2, (0,))


def products(pe, out, parts):
    for k, (left, right) in enumerate(parts):
        ins = pe.matmul(out, left, right, start=(k == 0), stop=(k == len(parts) - 1))
    return ins


def turned(pe, net, out, src, n):
    for k in range(n):
        ins = pe.transpose(out[:, k * P:(k + 1) * P], src[:, k * P:(k + 1) * P], net.const("ident"))
    return ins


def project1_stage(nc, net):
    with ExitStack() as c:
        b = buffers(nc, c, "proj1", w=[2, 264], wT=[2, D], al=[2, 8], wkv=[2, 512], bkv=[512], xn=[D], xnT=[2, P],
                    tab=[D], top=[D], pen=[TILES], col=[2], diag=[2, P])
        p_tr, p_tab, p_k, p_top = net.PS[0:4]
        names = ["w_in", "loaded", "folded", "fold_ps", "xn", "tr", "xnT", "mm", "k_used", "tab_sb", "tab_out", "end", "top", "top_tr", "diag", "top_row"]
        with stage(nc, "proj1", names) as (block, s):
            @block.sync
            def _(sp):
                for dst, src in ((b["w"][:, :, 0:D], weight(net.inp["g1_w"])), (b["wT"][:, :, :], weight(net.inp["g1_wT"])),
                                 (b["al"][:, :, :], weight(net.inp["g1_al"])), (b["wkv"][:, :, :], weight(net.inp["m1_wkv"])),
                                 (b["bkv"][0:1, :], net.inp["m1_bkv"])):
                    sp.dma_start(dst, src).then_inc(s["w_in"], 16)
                with sp.Fori(0, TILES) as t:
                    wait(net, sp, s["tab_sb"], t + 1)
                    sp.dma_start(net.table[bass.ds(t * P, P), :], b["tab"][:, 0:D]).then_inc(s["tab_out"], 16)
                sp.wait_ge(s["end"], 1)
                sp.dma_start(net.src_tab.rearrange("(t p) c -> p t c", p=P), net.node_src[:, :, :]).then_inc(s["tab_out"], 16)
                sp.wait_ge(s["tab_out"], 16 * (TILES + 1) + 1)

            @block.vector
            def _(dve):
                dve.memset(b["top"][:, :], -BIG)
                dve.tensor_scalar(b["pen"][:, :], net.const("valid"), BIG, BIG, ALU.mult, ALU.subtract)
                dve.wait_ge(s["fold_ps"], 1)
                for i in range(2):
                    ins = dve.tensor_copy(b["w"][:, i, D:D + 8], p_tab[:, 8 * i:8 * i + 8])
                ins.then_inc(s["folded"], 1)
                with dve.Fori(0, TILES) as t:
                    dve.tensor_scalar(b["xn"][:, :], rows(net.X[:, bass.ds(t, 1), :]), net.rstd[:, bass.ds(t, 1)],
                                      net.shift[:, bass.ds(t, 1)], ALU.mult, ALU.add).then_inc(s["xn"], 1)
                    wait(net, dve, s["mm"], t + 1)
                    dve.scalar_tensor_tensor(b["top"][:, :], p_k[:, 0:D], b["pen"][:, bass.ds(t, 1)], b["top"][:, :], ALU.add, ALU.max).then_inc(s["k_used"], 1)
                    dve.drain()
                dve.sem_inc(s["top"], 1)
                dve.wait_ge(s["top_tr"], 1)
                dve.tensor_reduce(b["col"][:, :], p_top[:, 0:D].rearrange("p (a b) -> p a b", a=2), AX.X, ALU.max)
                dve.drain()
                for i in range(2):
                    ins = dve.tensor_scalar(b["diag"][:, i, :], net.const("ident"), b["col"][:, i:i + 1], None, ALU.mult)
                ins.then_inc(s["diag"], 1)
                dve.wait_ge(s["top_row"], 1)
                dve.tensor_copy(net.key_top[:, :], p_tr[:, 0:D])

            @block.scalar
            def _(act):
                act.sem_inc(s["tab_out"], 1)
                with act.Fori(0, TILES) as t:
                    wait(net, act, s["tr"], t + 1)
                    act.activation(rows(b["xnT"][:, :, :]), p_tr[:, 0:D], ACT.Copy).then_inc(s["xnT"], 1)
                    wait(net, act, s["mm"], t + 1)
                    act.activation(net.node_src[:, bass.ds(t, 1), :].rearrange("p a b -> p (a b)"), p_tab[:, D:D + 4], ACT.Copy)
                    act.activation(net.node_dst[:, bass.ds(t, 1), :].rearrange("p a b -> p (a b)"), p_tab[:, D + 4:D + 8], ACT.Copy)
                    wait(net, act, s["tab_out"], 16 * t + 1)
                    act.activation(b["tab"][:, 0:D], p_tab[:, 0:D], ACT.Copy).then_inc(s["tab_sb"], 1)
                act.sem_inc(s["end"], 1)

            @block.tensor
            def _(pe):
                pe.wait_ge(s["w_in"], 80)
                for i in range(2):
                    ins = products(pe, p_tab[:, 8 * i:8 * i + 8], [(b["wT"][:, k, i * P:(i + 1) * P], b["al"][:, k, :]) for k in range(2)])
                ins.then_inc(s["fold_ps"], 1)
                pe.wait_ge(s["folded"], 1)
                pe.sem_inc(s["k_used"], 1)
                with pe.Fori(0, TILES) as t:
                    wait(net, pe, s["xn"], t + 1)
                    turned(pe, net, p_tr, b["xn"], 2).then_inc(s["tr"], 1)
                    wait(net, pe, s["xnT"], t + 1)
                    products(pe, p_tab[:, 0:264], [(b["xnT"][:, k, :], b["w"][:, k, :]) for k in range(2)])
                    wait(net, pe, s["k_used"], t + 1)
                    products(pe, p_k[:, 0:D], [(b["xnT"][:, k, :], b["wkv"][:, k, 0:D]) for k in range(2)] +
                             [(net.const("ones")[0:1, :], b["bkv"][0:1, 0:D])]).then_inc(s["mm"], 1)
                pe.wait_ge(s["top"], 1)
                turned(pe, net, p_top, b["top"], 2).then_inc(s["top_tr"], 1)
                pe.wait_ge(s["diag"], 1)
                pe.matmul(p_tr[:, 0:D], net.const("ones"), b["diag"][:, :, :].rearrange("p a b -> p (a b)"), start=True, stop=True).then_inc(s["top_row"], 1)


def lambda_stage(nc, net):
    with ExitStack() as c:
        b = buffers(nc, c, "lam", wkv=[2, 512], bkv=[512], cols=[2, 3], xn=[D], xnT=[2, P], kx=[D], v=[D + 4], acc=[2, D + 4],
                    sum=[2], six=[2, 6], mv=[2, 2], var=[2], rs=[2], xf=[2])
        p_tr, p_kv, p_l0, p_l1 = net.PS[0:4]
        names = ["w_in", "xn", "tr", "xnT", "mm", "kx", "kexp", "v_ready", "kv_ready", "lam_mm", "var_ready", "rstd_ready"]
        with stage(nc, "lam", names) as (block, s):
            @block.sync
            def _(sp):
                for dst, src in ((b["wkv"][:, :, :], weight(net.inp["m1_wkv"])), (b["bkv"][0:1, :], net.inp["m1_bkv"]),
                                 (b["cols"][:, :, :].rearrange("p a b -> p (a b)"), net.inp["m1_cols"])):
                    sp.dma_start(dst, src).then_inc(s["w_in"], 16)

            @block.vector
            def _(dve):
                dve.memset(b["acc"][:, :, :], 0.0)
                dve.wait_ge(s["w_in"], 48)
                with dve.Fori(0, TILES) as t:
                    dve.tensor_scalar(b["xn"][:, :], rows(net.X[:, bass.ds(t, 1), :]), net.rstd[:, bass.ds(t, 1)],
                                      net.shift[:, bass.ds(t, 1)], ALU.mult, ALU.add).then_inc(s["xn"], 1)
                    wait(net, dve, s["mm"], t + 1)
                    dve.tensor_tensor(b["kx"][:, :], p_kv[:, 0:D], net.key_top[:, :], ALU.subtract).then_inc(s["kx"], 1)
                    dve.tensor_copy(b["v"][:, 0:D], p_kv[:, D:2 * D])
                    dve.memset(b["v"][:, D:D + 1], 1.0)
                    wait(net, dve, s["kexp"], t + 1)
                    dve.tensor_scalar(b["kx"][:, :], b["kx"][:, :], net.const("valid")[:, bass.ds(t, 1)], None, ALU.mult).then_inc(s["kv_ready"], 1)
                    wait(net, dve, s["lam_mm"], t + 1)
                    for i, ps in enumerate((p_l0, p_l1)):
                        dve.tensor_tensor(b["acc"][:, i, 0:D + 1], b["acc"][:, i, 0:D + 1], ps[:, 0:D + 1], ALU.add)
                    dve.drain()
                for i in range(2):
                    dve.reciprocal(b["sum"][:, i:i + 1], b["acc"][:, i, D:D + 1])
                    dve.drain()
                    dve.tensor_scalar(b["acc"][:, i, 0:D], b["acc"][:, i, 0:D], b["sum"][:, i:i + 1], None, ALU.mult)
                    dve.drain()
                    dve.bn_stats(b["six"][:, i, :], b["acc"][:, i, 0:D])
                    dve.drain()
                    dve.bn_aggr(b["mv"][:, i, :], b["six"][:, i, :])
                    dve.drain()
                dve.tensor_scalar(b["var"][:, :], b["mv"][:, :, 1], 1e-5, None, ALU.add).then_inc(s["var_ready"], 1)
                dve.wait_ge(s["rstd_ready"], 1)
                dve.tensor_tensor(b["rs"][:, :], b["rs"][:, :], b["cols"][:, :, 1], ALU.mult)
                dve.drain()
                for i in range(2):
                    dve.tensor_scalar(net.lam[:, i, :], b["acc"][:, i, 0:D], b["mv"][:, i, 0:1], b["rs"][:, i:i + 1], ALU.subtract, ALU.mult)
                dve.drain()
                for i in range(2):
                    dve.tensor_scalar(net.lam[:, i, :], net.lam[:, i, :], b["cols"][:, i, 2:3], None, ALU.add)

            @block.gpsimd
            def _(pool):
                pool.wait_ge(s["var_ready"], 1)
                pool.tensor_tensor(b["rs"][:, :], b["var"][:, :], net.const("mhalf").to_broadcast([P, 2]), ALU.pow).then_inc(s["rstd_ready"], 1)

            @block.scalar
            def _(act):
                with act.Fori(0, TILES) as t:
                    wait(net, act, s["tr"], t + 1)
                    act.activation(rows(b["xnT"][:, :, :]), p_tr[:, 0:D], ACT.Copy).then_inc(s["xnT"], 1)
                    wait(net, act, s["kx"], t + 1)
                    act.activation(b["kx"][:, :], b["kx"][:, :], ACT.Exp).then_inc(s["kexp"], 1)

            @block.tensor
            def _(pe):
                pe.wait_ge(s["w_in"], 48)
                with pe.Fori(0, TILES) as t:
                    wait(net, pe, s["xn"], t + 1)
                    turned(pe, net, p_tr, b["xn"], 2).then_inc(s["tr"], 1)
                    wait(net, pe, s["xnT"], t + 1)
                    products(pe, p_kv[:, :], [(b["xnT"][:, k, :], b["wkv"][:, k, :]) for k in range(2)] +
                             [(net.const("ones")[0:1, :], b["bkv"][0:1, :])]).then_inc(s["mm"], 1)
                    wait(net, pe, s["kv_ready"], t + 1)
                    for i, ps in enumerate((p_l0, p_l1)):
                        ins = pe.matmul(ps[:, 0:D + 1], b["kx"][:, i * P:(i + 1) * P], b["v"][:, 0:D + 1], start=True, stop=True)
                    ins.then_inc(s["lam_mm"], 1)


def rank_work(nc, net, c, block, s, b):
    flat = net.agg[:, :, :].rearrange("p a b -> p (a b)")
    row, sink = flat[:, 0:NPAD], flat[:, NPAD:NPAD + NPAD // 2]
    d = buffers(nc, c, "rank", key=[TILES], noise=[TILES], part=[4, TILES], far=[TILES])

    @block.sync
    def _(sp):
        sp.wait_ge(s["noise_clear"], 1)
        with nc.allow_non_contiguous_dma("one number a node"):
            sp.dma_start(d["noise"][:, 0:TILES - 1], net.inp["noise"][:, 0:(TILES - 1) * P].rearrange("o (t p) -> p (o t)", p=P)).then_inc(s["noise_in"], 16)
            sp.dma_start(d["noise"][0:LAST, TILES - 1:TILES], net.inp["noise"][:, (TILES - 1) * P:N].rearrange("o (t p) -> p (o t)", p=LAST)).then_inc(s["noise_in"], 16)
            sp.wait_ge(s["keys_ready"], 1)
            sp.dma_start(net.keys.rearrange("o (t p) -> p (o t)", p=P), d["key"][:, :]).then_inc(s["keys_out"], 16)
        sp.wait_ge(s["keys_out"], 16)
        sp.dma_start(row, net.keys.to_broadcast([P, NPAD])).then_inc(s["keys_in"], 16)

    @block.vector
    def _(dve):
        dve.memset(d["noise"][:, :], 0.0).then_inc(s["noise_clear"], 1)
        dve.memset(d["part"][:, :, :], 0.0)
        dve.wait_ge(s["noise_in"], 32)
        dve.tensor_tensor(d["key"][:, :], net.src_degree[:, :], d["noise"][:, :], ALU.add)
        dve.drain()
        dve.tensor_tensor(d["key"][:, :], d["key"][:, :], net.const("valid"), ALU.mult)
        dve.tensor_scalar(d["far"][:, :], net.const("valid"), -BIG, BIG, ALU.mult, ALU.add)
        dve.drain()
        dve.tensor_tensor(d["key"][:, :], d["key"][:, :], d["far"][:, :], ALU.add).then_inc(s["keys_ready"], 1)
        dve.wait_ge(s["keys_in"], 16)
        half = NPAD // 2

        def count(t, k, lo, hi, op):
            for a in range(lo, hi, half):
                z = min(hi, a + half)
                kk = k + (a > lo)
                dve.tensor_scalar(sink[:, 0:z - a], row[:, a:z], d["key"][:, t:t + 1], None, op, ALU.add, accum_out=d["part"][:, kk, t:t + 1])
                dve.drain()

        for t in range(TILES):
            lo, hi = t * P, (t + 1) * P
            count(t, 0, 0, lo, ALU.is_le)
            for k, (first, last) in enumerate(((lo, NPAD),)):
                for a in range(first, last, half):
                    z = min(last, a + half)
                    dve.tensor_scalar(sink[:, 0:z - a], row[:, a:z], d["key"][:, t:t + 1], None, ALU.is_lt, ALU.add,
                                      accum_out=d["far"][:, t:t + 1])
                    dve.drain()
                    dve.tensor_tensor(d["part"][:, 2, t:t + 1], d["part"][:, 2, t:t + 1], d["far"][:, t:t + 1], ALU.add)
                    dve.drain()
            dve.scalar_tensor_tensor(sink[:, 0:P], row[:, lo:hi], d["key"][:, t:t + 1], net.const("lower"), ALU.is_equal, ALU.mult,
                                     accum_out=d["part"][:, 3, t:t + 1])
            dve.drain()
        for k in range(1, 4):
            dve.tensor_tensor(d["part"][:, 0, :], d["part"][:, 0, :], d["part"][:, k, :], ALU.add)
            dve.drain()
        dve.tensor_copy(net.rank[:, :], d["part"][:, 0, :])


def sort_stage(nc, net):
    R = 4
    with ExitStack() as c:
        b = buffers(nc, c, "sort", xn=[R, D])
        with stage(nc, "sort", ["xn", "gp_out0", "gp_out1", "gp_out2", "gp_out3"]) as (block, s):
            out = (s["gp_out0"], s["gp_out1"], s["gp_out2"], s["gp_out3"])

            @block.vector
            def _(dve):
                for t in range(TILES):
                    if t >= R:
                        dve.wait_ge(out[t % R], 16 * (t // R))
                    dve.tensor_scalar(b["xn"][:, t % R, :], net.X[:, t, :], net.rstd[:, t:t + 1], net.shift[:, t:t + 1],
                                      ALU.mult, ALU.add).then_inc(s["xn"], 1)

            @block.gpsimd
            def _(pool):
                for t in range(TILES):
                    pool.wait_ge(s["xn"], t + 1)
                    pool.indirect_dma_start(net.sorted_x, bass.IndirectOffsetOnAxis(ap=net.rank[:, t:t + 1], axis=0),
                                            b["xn"][:, t % R, :], None).then_inc(out[t % R], 16)
                for r in range(R):
                    pool.wait_ge(out[r], 16 * len(range(r, TILES, R)))


CHUNK = 448
PART = 112
CHUNKS = NPAD // CHUNK
STATES = 16
LOG1P = [2.0000000078777487, 0.6666631593508171, 0.4002485372345264, 0.2796141883488086, 0.28174657263251685]


def mamba_stage(nc, net):
    SET, SLOTS, COPIES = 8, 7, 14
    spare = rows(net.agg[:, :, :])
    with ExitStack() as c:
        b = buffers(nc, c, "mamba", w_in=[2, 512], w_x=[2, 48], w_dt=[D], w_out=[2, D], cols=[2, 23], neg=[2, STATES],
                    xsT=[2, CHUNK], raw=[2, CHUNK + 4], xc=[2, CHUNK], dbc=[CHUNK], dt=[2, CHUNK],
                    dtx=[2, CHUNK], dA=[2, 2, CHUNK], dB=[2, CHUNK], h=[2, 2, CHUNK], state=[2, STATES],
                    idx_src_i=[EROW], idx_i=[SLOTS, SET], land=[SLOTS, SET, H])
        A2 = rows
        tmp = [spare[:, i * 2 * CHUNK:(i + 1) * 2 * CHUNK] for i in range(5)]
        hc = spare[:, 10 * CHUNK:14 * CHUNK].rearrange("p (q i c) -> p q i c", q=2, i=2)
        at = 14 * CHUNK
        yo = spare[:, at:at + 4 * D].rearrange("p (a d) -> p a d", a=4)
        b["xs"] = spare[:, at + 4 * D:at + 8 * D].rearrange("p (a d) -> p a d", a=4)
        at += 8 * D
        b["z"] = spare[:, at:at + 2 * CHUNK].rearrange("p (a d) -> p a d", a=2)
        src_i = spare[:, at + 2 * CHUNK:at + 2 * CHUNK + EROW].bitcast(I32)
        B = net.PS
        names = ["w", "xs_in", "tr", "xsT", "in_mm", "raw", "conv", "silu", "x_mm", "dbc", "dt_mm", "sp_in", "sp_e", "dt_ready",
                 "bc", "dA", "dB", "h_ready", "hc", "y_mm", "yz", "out_mm", "yo", "y_out", "z_ready", "neg", "halo", "edges_in", "clipped", "idx_ready"] + \
                [f"taken{q}" for q in range(SLOTS)] + [f"gp_landed{q}" for q in range(SLOTS)]
        with stage(nc, "mamba", names) as (block, s):
            landed, taken = [s[f"gp_landed{q}"] for q in range(SLOTS)], [s[f"taken{q}"] for q in range(SLOTS)]

            @block.sync
            def _(sp):
                i = net.inp
                sp.dma_start(src_i, net.src_pad.rearrange("t e -> (t e)").rearrange("(p g) -> p g", p=P)).then_inc(s["edges_in"], 16)
                for dst, src in ((b["w_in"][:, :, :], weight(i["s_in"])), (b["w_x"][:, :, :], weight(i["s_x"])), (b["w_dt"][0:16, :], i["s_dt"]),
                                 (b["w_out"][:, :, :], weight(i["s_out"])), (A2(b["cols"][:, :, :]), i["s_cols"])):
                    sp.dma_start(dst, src).then_inc(s["w"], 16)
                sp.sem_inc(s["tr"], 1)
                with sp.Fori(0, CHUNKS) as j:
                    wait(net, sp, s["tr"], j + 1)
                    sp.dma_start(b["xs"][0:PART, :, :], net.sorted_x[bass.ds(j * CHUNK, CHUNK), :].rearrange("(a p) d -> p a d", p=PART)).then_inc(s["xs_in"], 16)
                    wait(net, sp, s["yo"], j + 1)
                    sp.dma_start(net.mamba_y[bass.ds(j * CHUNK, CHUNK), :].rearrange("(a p) d -> p a d", p=PART), yo[0:PART, :, :]).then_inc(s["y_out"], 16)
                sp.wait_ge(s["y_out"], 16 * CHUNKS + 1)

            @block.gpsimd
            def _(pool):
                pool.wait_ge(s["edges_in"], 16)
                pool.tensor_scalar(b["idx_src_i"][:, :], src_i, 0, None, ALU.max).then_inc(s["clipped"], 1)
                pool.wait_ge(s["clipped"], 1)
                with pool.Fori(0, EROW // (SLOTS * SET)) as it:
                    for q in range(SLOTS):
                        wait(net, pool, taken[q], it + 1)
                        pool.tensor_copy(b["idx_i"][:, q, :], b["idx_src_i"][:, bass.ds((it * SLOTS + q) * SET, SET)]).then_inc(s["idx_ready"], 1)
                        wait_apart(net, pool, s["idx_ready"], it * SLOTS + q + 1)
                        for r in range(SET):
                            pool.indirect_dma_start(b["land"][:, q, r, :], None, net.src_tab,
                                                    bass.IndirectOffsetOnAxis(ap=b["idx_i"][:, q, r:r + 1], axis=0)).then_inc(landed[q], 16)

            @block.scalar
            def _(act):
                for q in range(SLOTS):
                    act.sem_inc(taken[q], 1)
                act.wait_ge(s["w"], 80)
                for i in range(2):
                    ins = act.activation(b["neg"][:, i, :], b["cols"][:, i, 7:23], ACT.Exp)
                ins.then_inc(s["neg"], 1)
                act.wait_ge(s["neg"], 2)
                act.sem_inc(s["y_out"], 1)
                with act.Fori(0, CHUNKS) as j:
                    wait(net, act, s["tr"], j + 2)
                    for i in range(2):
                        ins = act.activation(b["xsT"][:, i, :], B[i][:, 0:CHUNK], ACT.Copy)
                    ins.then_inc(s["xsT"], 1)
                    wait(net, act, s["in_mm"], j + 1)
                    wait(net, act, s["halo"], j + 1)
                    for i in range(2):
                        ins = act.activation(b["raw"][:, i, 3:3 + CHUNK], B[2 + i][:, 0:CHUNK], ACT.Copy)
                    ins.then_inc(s["raw"], 1)
                    for i in range(2):
                        ins = act.activation(b["z"][:, i, :], B[4 + i][:, 0:CHUNK], ACT.Silu)
                    ins.then_inc(s["z_ready"], 1)
                    wait(net, act, s["conv"], j + 1)
                    for i in range(2):
                        ins = act.activation(b["xc"][:, i, :], tmp[0][:, i * CHUNK:(i + 1) * CHUNK], ACT.Silu, bias=b["cols"][:, i, 4:5])
                    ins.then_inc(s["silu"], 1)
                    wait(net, act, s["x_mm"], j + 1)
                    act.activation(b["dbc"][0:48, :], B[6][0:48, 0:CHUNK], ACT.Copy).then_inc(s["dbc"], 1)
                    wait(net, act, s["sp_in"], j + 1)
                    for i in range(2):
                        ins = act.activation(tmp[2][:, i * CHUNK:(i + 1) * CHUNK], tmp[1][:, i * CHUNK:(i + 1) * CHUNK], ACT.Exp, bias=b["cols"][:, i, 5:6])
                    ins.then_inc(s["sp_e"], 1)
                    wait(net, act, s["dt_ready"], j + 1)
                    for k in range(STATES):
                        wait(net, act, s["h_ready"], j * STATES + k - 1) if k >= 2 else None
                        for i in range(2):
                            ins = act.activation(b["dA"][:, k % 2, i, :], b["dt"][:, i, :], ACT.Exp, scale=b["neg"][:, i, k:k + 1])
                        ins.then_inc(s["dA"], 1)
                        if k < COPIES:
                            wait(net, act, landed[k % SLOTS], (j * (COPIES // SLOTS) + k // SLOTS + 1) * 16 * SET)
                            act.activation(net.edge[:, bass.ds((j * COPIES + k) * SET * H, SET * H)], rows(b["land"][:, k % SLOTS, :, :]),
                                           ACT.Copy).then_inc(taken[k % SLOTS], 1)
                    wait(net, act, s["out_mm"], j + 1)
                    wait(net, act, s["y_out"], 16 * j + 1)
                    for a in range(4):
                        ins = act.activation(yo[0:PART, a, :], B[2 + a][0:PART, 0:D], ACT.Copy)
                    ins.then_inc(s["yo"], 1)

            @block.vector
            def _(dve):
                both = lambda ps: ps[:, 0:CHUNK].unsqueeze(1).to_broadcast([P, 2, CHUNK])
                dve.memset(b["state"][:, :, :], 0.0)
                dve.memset(b["raw"][:, :, CHUNK:CHUNK + 3], 0.0)
                dve.wait_ge(s["neg"], 1)
                dve.tensor_scalar(A2(b["neg"][:, :, :]), A2(b["neg"][:, :, :]), -1.0, None, ALU.mult).then_inc(s["neg"], 1)
                with dve.Fori(0, CHUNKS) as j:
                    dve.drain()
                    for i in range(2):
                        ins = dve.tensor_copy(b["raw"][:, i, 0:3], b["raw"][:, i, CHUNK:CHUNK + 3])
                    ins.then_inc(s["halo"], 1)
                    wait(net, dve, s["raw"], j + 1)
                    for i in range(2):
                        u = tmp[0][:, i * CHUNK:(i + 1) * CHUNK]
                        for k in range(4):
                            tap, x = b["cols"][:, i, k:k + 1], b["raw"][:, i, k:k + CHUNK]
                            if k == 0:
                                ins = dve.tensor_scalar(u, x, tap, None, ALU.mult)
                            else:
                                dve.drain()
                                ins = dve.scalar_tensor_tensor(u, x, tap, u, ALU.mult, ALU.add)
                    ins.then_inc(s["conv"], 1)
                    wait(net, dve, s["dt_mm"], j + 1)
                    for i in range(2):
                        v, bias = B[2 + i][:, 0:CHUNK], b["cols"][:, i, 5:6]
                        dve.tensor_scalar(b["dt"][:, i, :], v, bias, 0.0, ALU.add, ALU.max)
                        dve.drain()
                        ins = dve.scalar_tensor_tensor(tmp[1][:, i * CHUNK:(i + 1) * CHUNK], b["dt"][:, i, :], -2.0, v, ALU.mult, ALU.add)
                    ins.then_inc(s["sp_in"], 1)
                    wait(net, dve, s["sp_e"], j + 1)
                    e, den, q, s2 = tmp[2], tmp[3], tmp[4], tmp[1]
                    dve.tensor_scalar(den, e, 2.0, None, ALU.add)
                    dve.drain()
                    dve.reciprocal(den, den)
                    dve.drain()
                    dve.tensor_tensor(e, e, den, ALU.mult)
                    dve.drain()
                    dve.tensor_tensor(s2, e, e, ALU.mult)
                    dve.drain()
                    dve.tensor_scalar(q, s2, LOG1P[-1], None, ALU.mult)
                    dve.drain()
                    for coeff in LOG1P[-2:0:-1]:
                        dve.scalar_tensor_tensor(q, q, coeff, s2, ALU.add, ALU.mult)
                        dve.drain()
                    dve.scalar_tensor_tensor(q, q, LOG1P[0], e, ALU.add, ALU.mult)
                    dve.drain()
                    dve.tensor_tensor(A2(b["dt"][:, :, :]), A2(b["dt"][:, :, :]), q, ALU.add).then_inc(s["dt_ready"], 1)
                    dve.drain()
                    wait(net, dve, s["silu"], j + 1)
                    dve.tensor_tensor(A2(b["dtx"][:, :, :]), A2(b["dt"][:, :, :]), A2(b["xc"][:, :, :]), ALU.mult)
                    dve.drain()
                    for k in range(STATES):
                        g = j * STATES + k + 1
                        wait(net, dve, s["bc"], g)
                        dve.tensor_tensor(b["dB"][:, :, :], b["dtx"][:, :, :], both(B[6 - 2 * (k % 2)]), ALU.mult)
                        dve.drain()
                        wait(net, dve, s["dA"], g)
                        for i in range(2):
                            ins = dve.tensor_tensor_scan(b["h"][:, k % 2, i, :], b["dA"][:, k % 2, i, :], b["dB"][:, i, :], b["state"][:, i, k:k + 1], ALU.mult, ALU.add)
                        ins.then_inc(s["h_ready"], 1)
                        dve.drain()
                        dve.tensor_copy(b["state"][:, :, k], b["h"][:, k % 2, :, CHUNK - 1])
                        if k >= 2:
                            wait(net, dve, s["y_mm"], g - 2)
                        dve.tensor_tensor(hc[:, k % 2, :, :], b["h"][:, k % 2, :, :], both(B[7 - 2 * (k % 2)]), ALU.mult).then_inc(s["hc"], 1)
                    wait(net, dve, s["y_mm"], (j + 1) * STATES)
                    wait(net, dve, s["z_ready"], j + 1)
                    for i in range(2):
                        dve.scalar_tensor_tensor(b["dtx"][:, i, :], b["xc"][:, i, :], b["cols"][:, i, 6:7], B[i][:, 0:CHUNK], ALU.mult, ALU.add)
                    dve.drain()
                    dve.tensor_tensor(A2(b["dtx"][:, :, :]), A2(b["dtx"][:, :, :]), A2(b["z"][:, :, :]), ALU.mult).then_inc(s["yz"], 1)

            @block.tensor
            def _(pe):
                pe.wait_ge(s["w"], 80)

                def add_state(g, k):
                    wait(net, pe, s["hc"], g)
                    for i in range(2):
                        ins = pe.matmul(B[i][:, 0:CHUNK], net.const("ident"), hc[:, k % 2, i, :], start=(k == 0), stop=(k == STATES - 1))
                    ins.then_inc(s["y_mm"], 1)

                with pe.Fori(0, CHUNKS) as j:
                    wait(net, pe, s["xs_in"], 16 * j + 16)
                    for a in range(4):
                        for i in range(2):
                            ins = pe.transpose(B[i][:, a * PART:(a + 1) * PART], b["xs"][0:PART, a, i * P:(i + 1) * P], net.const("ident")[0:PART, 0:PART])
                    ins.then_inc(s["tr"], 1)
                    wait(net, pe, s["xsT"], j + 1)
                    for m in range(4):
                        ins = products(pe, B[2 + m][:, 0:CHUNK], [(b["w_in"][:, k, m * P:(m + 1) * P], b["xsT"][:, k, :]) for k in range(2)])
                    ins.then_inc(s["in_mm"], 1)
                    wait(net, pe, s["silu"], j + 1)
                    products(pe, B[6][0:48, 0:CHUNK], [(b["w_x"][:, k, :], b["xc"][:, k, :]) for k in range(2)]).then_inc(s["x_mm"], 1)
                    wait(net, pe, s["dbc"], j + 1)
                    for i in range(2):
                        ins = products(pe, B[2 + i][:, 0:CHUNK], [(b["w_dt"][0:16, i * P:(i + 1) * P], b["dbc"][0:16, :])])
                    ins.then_inc(s["dt_mm"], 1)
                    for k in range(STATES):
                        g = j * STATES + k + 1
                        if k >= 2:
                            wait(net, pe, s["hc"], g - 2)
                        for row, bank in ((16 + k, B[6 - 2 * (k % 2)]), (32 + k, B[7 - 2 * (k % 2)])):
                            ins = pe.matmul(bank[:, 0:CHUNK], net.const("ident")[0:48, row:row + 1].to_broadcast([48, P]), b["dbc"][0:48, :], start=True, stop=True)
                        ins.then_inc(s["bc"], 1)
                        if k:
                            add_state(g - 1, k - 1)
                    add_state((j + 1) * STATES, STATES - 1)
                    wait(net, pe, s["yz"], j + 1)
                    for a in range(4):
                        ins = products(pe, B[2 + a][0:PART, 0:D], [(b["dtx"][:, k, a * PART:(a + 1) * PART], b["w_out"][:, k, :]) for k in range(2)])
                    ins.then_inc(s["out_mm"], 1)


def guard_stage(nc, net):
    m, g = (a[:, :, :].rearrange("p a b -> p (a b)") for a in (net.node_max, net.guard))
    with ExitStack() as c:
        b = buffers(nc, c, "guard", has=[TILES], far=[TILES], masked=[TILES, H], top=[1], turn=[P], all=[1])
        with stage(nc, "guard", ["top", "row", "all", "ps", "diff", "exp"]) as (block, s):
            @block.vector
            def _(dve):
                dve.tensor_scalar(b["has"][:, :], net.degree[:, :], 0.0, None, ALU.is_gt)
                dve.drain()
                dve.tensor_scalar(b["far"][:, :], b["has"][:, :], BIG, BIG, ALU.mult, ALU.subtract)
                dve.drain()
                dve.tensor_tensor(b["masked"][:, :, :], net.node_max[:, :, :], b["far"][:, :].unsqueeze(2).to_broadcast([P, TILES, H]), ALU.add)
                dve.drain()
                dve.tensor_reduce(b["top"][:, :], b["masked"][:, :, :], AX.XY, ALU.max)
                dve.drain()
                dve.tensor_scalar(b["turn"][:, :], net.const("ident"), b["top"][:, :], None, ALU.mult).then_inc(s["top"], 1)
                dve.wait_ge(s["row"], 1)
                dve.tensor_reduce(b["all"][:, :], net.PS[0][:, 0:P], AX.X, ALU.max)
                dve.drain()
                dve.tensor_scalar(g, m, b["all"][:, :], -1.0, ALU.subtract, ALU.mult)
                dve.drain()
                dve.tensor_scalar(g, g, 87.0, None, ALU.min).then_inc(s["diff"], 1)
                dve.wait_ge(s["exp"], 1)
                dve.tensor_scalar(g, g, 1e-16, None, ALU.mult)

            @block.tensor
            def _(pe):
                pe.wait_ge(s["top"], 1)
                pe.matmul(net.PS[0][:, 0:P], net.const("ones"), b["turn"][:, :], start=True, stop=True).then_inc(s["row"], 1)

            @block.scalar
            def _(act):
                act.wait_ge(s["diff"], 1)
                act.activation(g, g, ACT.Exp).then_inc(s["exp"], 1)


def final_stage(nc, net):
    with ExitStack() as c:
        b = buffers(nc, c, "fin", rows=[8, D], gates=[4, D], ff1=[2, 512], ff1b=[4], ff2=[4, D], wq=[2, D], cols=[2, 3], idx_i=[2])
        bw = pair_buffers(nc, c, "fin_t", net.edge, xn=[D], xnT=[2, P], den=[H], v=[D], ex=[D], pair=[2, D], pT=[4, P], g=[D], h=[D],
                          hT=[2, P], fT=[4, P], qT=[2, P], y=[D], **SMALL)
        TURN, MIX, GATE, FF = ([net.PS[4 * w + i] for w in range(2)] for i in range(4))
        names = ["w_in", "loaded", "xn", "tr", "xnT", "q", "qT", "mix", "mix_used", "e_in", "e_out", "idx", "y_used", "pair", "tr_p", "pT", "gate",
                 "g_in", "g_out", "h", "tr_h", "hT", "f1", "f1r", "f2", "var_ready", "rstd_ready", "gp_y0", "gp_y1"]
        with stage(nc, "fin", names) as (block, s):
            GAT_B, LOC_G, LOC_B, GLO_G, GLO_B, LN2_G, LN2_B, FF2_B = range(8)
            y_in = (s["gp_y0"], s["gp_y1"])

            @block.sync
            def _(sp):
                i = net.inp
                loads = [(rows(b["rows"][:, :, :]), i["g1_rows"].to_broadcast([P, 8 * D])), (b["gates"][:, :, :], weight(i["g1_gates"])),
                         (b["ff1"][:, :, :], weight(i["g1_ff1"])), (b["ff1b"][:, :], i["g1_ff1b"]), (b["ff2"][:, :, :], weight(i["g1_ff2"])),
                         (b["wq"][:, :, :], weight(i["m1_wq"])), (rows(b["cols"][:, :, :]), i["m1_cols"])]
                for dst, src in loads:
                    sp.dma_start(dst, src).then_inc(s["w_in"], 16)
                sp.wait_ge(s["w_in"], 16 * len(loads))
                sp.sem_inc(s["loaded"], 1)

            @block.gpsimd
            def _(pool):
                def tiles(it, ws):
                    for w in ws:
                        wait(net, pool, s["y_used"], 2 * it + w + 1)
                        pool.tensor_copy(b["idx_i"][:, w:w + 1], net.rank[:, bass.ds(2 * it + w, 1)]).then_inc(s["idx"], 1)
                        wait_apart(net, pool, s["idx"], 2 * it + w + 1)
                        pool.indirect_dma_start(bw[w]["y"][:, :], None, net.mamba_y,
                                                bass.IndirectOffsetOnAxis(ap=b["idx_i"][:, w:w + 1], axis=0)).then_inc(y_in[w], 16)
                    for k in range(3):
                        for w in ws:
                            norm_power(net, pool, s, bw[w], norm_value(it, ws, w, k))

                with pool.Fori(0, TILES // 2) as it:
                    tiles(it, (0, 1))
                tiles(TILES // 2, (0,))

            @block.tensor
            def _(pe):
                def tiles(it, ws):
                    n = lambda w: 2 * it + w + 1
                    for w in ws:
                        wait(net, pe, s["xn"], n(w))
                        turned(pe, net, TURN[w], bw[w]["xn"], 2).then_inc(s["tr"], 1)
                    for w in ws:
                        wait(net, pe, s["xnT"], n(w))
                        for i in range(2):
                            ins = products(pe, GATE[w][:, i * P:(i + 1) * P], [(b["wq"][:, k, i * P:(i + 1) * P], bw[w]["xnT"][:, k, :]) for k in range(2)])
                        ins.then_inc(s["q"], 1)
                    for w in ws:
                        wait(net, pe, s["qT"], n(w))
                        products(pe, MIX[w][:, 0:D], [(bw[w]["qT"][:, k, :], net.lam[:, k, :]) for k in range(2)]).then_inc(s["mix"], 1)
                    for w in ws:
                        wait(net, pe, s["pair"], n(w))
                        turned(pe, net, TURN[w], rows(bw[w]["pair"][:, :, :]), 4).then_inc(s["tr_p"], 1)
                    for w in ws:
                        wait(net, pe, s["pT"], n(w))
                        products(pe, GATE[w][:, 0:D], [(bw[w]["pT"][:, k, :], b["gates"][:, k, :]) for k in range(4)]).then_inc(s["gate"], 1)
                    for w in ws:
                        wait(net, pe, s["h"], n(w))
                        turned(pe, net, TURN[w], bw[w]["h"], 2).then_inc(s["tr_h"], 1)
                    for w in ws:
                        wait(net, pe, s["hT"], n(w))
                        for i in range(4):
                            ins = products(pe, FF[w][:, i * P:(i + 1) * P], [(b["ff1"][:, k, i * P:(i + 1) * P], bw[w]["hT"][:, k, :]) for k in range(2)])
                        ins.then_inc(s["f1"], 1)
                    for w in ws:
                        wait(net, pe, s["f1r"], n(w))
                        wait(net, pe, s["mix_used"], n(w))
                        products(pe, MIX[w][:, 0:D], [(bw[w]["fT"][:, k, :], b["ff2"][:, k, :]) for k in range(4)]).then_inc(s["f2"], 1)

                pe.wait_ge(s["loaded"], 1)
                with pe.Fori(0, TILES // 2) as it:
                    tiles(it, (0, 1))
                tiles(TILES // 2, (0,))

            @block.scalar
            def _(act):
                copy = lambda dst, src: act.activation(rows(dst), src, ACT.Copy)

                def tiles(it, ws):
                    n = lambda w: 2 * it + w + 1
                    for w in ws:
                        wait(net, act, s["tr"], n(w))
                        copy(bw[w]["xnT"][:, :, :], TURN[w][:, 0:D]).then_inc(s["xnT"], 1)
                    for w in ws:
                        wait(net, act, s["q"], n(w))
                        for i in range(2):
                            ins = act.activation(bw[w]["qT"][:, i, :], GATE[w][:, i * P:(i + 1) * P], ACT.Identity, bias=b["cols"][:, i, 0:1])
                        ins.then_inc(s["qT"], 1)
                    for w in ws:
                        wait(net, act, s["e_in"], n(w))
                        act.activation(bw[w]["ex"][:, :], bw[w]["ex"][:, :], ACT.Exp).then_inc(s["e_out"], 1)
                    for w in ws:
                        wait(net, act, s["tr_p"], n(w))
                        copy(bw[w]["pT"][:, :, :], TURN[w][:, :]).then_inc(s["pT"], 1)
                    for w in ws:
                        wait(net, act, s["g_in"], n(w))
                        act.activation(bw[w]["g"][:, :], bw[w]["g"][:, :], ACT.Exp, scale=-1.0).then_inc(s["g_out"], 1)
                    for w in ws:
                        wait(net, act, s["tr_h"], n(w))
                        copy(bw[w]["hT"][:, :, :], TURN[w][:, 0:D]).then_inc(s["hT"], 1)
                    for w in ws:
                        wait(net, act, s["f1"], n(w))
                        for i in range(4):
                            ins = act.activation(bw[w]["fT"][:, i, :], FF[w][:, i * P:(i + 1) * P], ACT.Relu, bias=b["ff1b"][:, i:i + 1])
                        ins.then_inc(s["f1r"], 1)

                act.wait_ge(s["loaded"], 1)
                with act.Fori(0, TILES // 2) as it:
                    tiles(it, (0, 1))
                tiles(TILES // 2, (0,))

            @block.vector
            def _(dve):
                heads = lambda a: a.rearrange("p (h d) -> p h d", h=H)
                row = lambda k: b["rows"][:, k, :]
                full = lambda w, k: bw[w][k][:, :]

                def each(ws, step):
                    for w in ws:
                        step(w)
                    dve.drain()

                def tiles(it, ws):
                    n = lambda w: 2 * it + w + 1
                    x = [rows(net.X[:, bass.ds(2 * it + w, 1), :]) for w in ws]
                    agg = [rows(net.agg[:, bass.ds(2 * it + w, 1), :]) for w in ws]
                    local, globe = ([bw[w]["pair"][:, i, :] for w in ws] for i in range(2))
                    for w in ws:
                        dve.tensor_scalar(full(w, "xn"), x[w], net.rstd[:, bass.ds(2 * it + w, 1)], net.shift[:, bass.ds(2 * it + w, 1)],
                                          ALU.mult, ALU.add).then_inc(s["xn"], 1)
                    each(ws, lambda w: dve.tensor_tensor(full(w, "den"), agg[w][:, D:D + H], rows(net.guard[:, bass.ds(2 * it + w, 1), :]), ALU.add))
                    each(ws, lambda w: dve.reciprocal(full(w, "den"), full(w, "den")))
                    each(ws, lambda w: dve.tensor_tensor(heads(full(w, "v")), heads(agg[w][:, 0:D]),
                                                         full(w, "den").unsqueeze(2).to_broadcast([P, H, 64]), ALU.mult))
                    each(ws, lambda w: dve.tensor_tensor(full(w, "v"), full(w, "v"), full(w, "xn"), ALU.add))
                    each(ws, lambda w: dve.tensor_tensor(full(w, "v"), full(w, "v"), row(GAT_B), ALU.add))
                    for w in ws:
                        dve.tensor_scalar(full(w, "ex"), full(w, "v"), 0.0, None, ALU.min).then_inc(s["e_in"], 1)
                    for w in ws:
                        wait(net, dve, y_in[w], 16 * it + 16)
                        dve.tensor_tensor(full(w, "h"), full(w, "y"), full(w, "xn"), ALU.add).then_inc(s["y_used"], 1)
                    for w in ws:
                        wait(net, dve, s["e_out"], n(w))
                        dve.tensor_scalar(full(w, "ex"), full(w, "ex"), 1.0, None, ALU.subtract)
                    dve.drain()
                    each(ws, lambda w: dve.scalar_tensor_tensor(full(w, "v"), full(w, "v"), 0.0, full(w, "ex"), ALU.max, ALU.add))
                    for w in ws:
                        norm_stats(dve, s, bw[w], full(w, "v"))
                    for w in ws:
                        norm_apply(net, dve, s, bw[w], full(w, "v"), local[w], norm_value(it, ws, w, 0), row(LOC_G), row(LOC_B))
                        norm_stats(dve, s, bw[w], full(w, "h"))
                    for w in ws:
                        norm_apply(net, dve, s, bw[w], full(w, "h"), globe[w], norm_value(it, ws, w, 1), row(GLO_G), row(GLO_B)).then_inc(s["pair"], 1)
                    for w in ws:
                        wait(net, dve, s["mix"], n(w))
                        dve.tensor_tensor(x[w], x[w], MIX[w][:, 0:D], ALU.add).then_inc(s["mix_used"], 1)
                    dve.drain()
                    for w in ws:
                        dve.tensor_tensor(full(w, "v"), local[w], globe[w], ALU.subtract)
                    for w in ws:
                        wait(net, dve, s["gate"], n(w))
                        dve.tensor_scalar(full(w, "g"), GATE[w][:, 0:D], -87.0, None, ALU.max).then_inc(s["g_in"], 1)
                    for w in ws:
                        wait(net, dve, s["g_out"], n(w))
                        dve.tensor_scalar(full(w, "g"), full(w, "g"), 1.0, None, ALU.add)
                        dve.drain()
                        dve.reciprocal(full(w, "g"), full(w, "g"))
                        dve.drain()
                        dve.tensor_tensor(full(w, "v"), full(w, "v"), full(w, "g"), ALU.mult)
                        dve.drain()
                        dve.tensor_tensor(full(w, "h"), full(w, "v"), globe[w], ALU.add).then_inc(s["h"], 1)
                    dve.drain()
                    each(ws, lambda w: dve.tensor_tensor(full(w, "v"), full(w, "h"), row(FF2_B), ALU.add))
                    for w in ws:
                        wait(net, dve, s["f2"], n(w))
                        dve.tensor_tensor(full(w, "v"), full(w, "v"), MIX[w][:, 0:D], ALU.add)
                        dve.drain()
                        norm_stats(dve, s, bw[w], full(w, "v"))
                    for w in ws:
                        norm_apply(net, dve, s, bw[w], full(w, "v"), full(w, "g"), norm_value(it, ws, w, 2), row(LN2_G), row(LN2_B))
                    dve.drain()
                    each(ws, lambda w: dve.tensor_tensor(x[w], x[w], full(w, "g"), ALU.add))

                dve.wait_ge(s["loaded"], 1)
                dve.sem_inc(s["y_used"], 2)
                with dve.Fori(0, TILES // 2) as it:
                    tiles(it, (0, 1))
                tiles(TILES // 2, (0,))


EXPERTS = 8


def expert_stage(nc, net):
    with ExitStack() as c:
        w1 = net.agg[:, :, :].rearrange("p a b -> p (a b)")[:, 0:EXPERTS * 1024].rearrange("p (e k n) -> p e k n", e=EXPERTS, k=2)
        b = buffers(nc, c, "exp", gw=[2, EXPERTS], gb=[EXPERTS], b1=[32], b2=[EXPERTS, D], w2=[EXPERTS, 4, D],
                    xn=[D], xnT=[2, P], hT=[2, 4, P], gt=[64], eq=[64], before=[64], sel=[EXPERTS], g=[EXPERTS], o=[D])
        B = net.PS
        names = ["w_in", "loaded", "xn", "tr", "xnT", "gl", "h", "gelu", "y", "y_used", "acc", "stored"]
        with stage(nc, "exp", names) as (block, s):
            @block.sync
            def _(sp):
                i = net.inp
                loads = [(w1.rearrange("p e k n -> p (e k) n"), i["e_w1"].rearrange("(a p) n -> p a n", p=P)),
                         (b["w2"][:, :, :, :].rearrange("p e k n -> p (e k) n"), i["e_w2"].rearrange("(a p) n -> p a n", p=P)),
                         (b["gw"][:, :, :], weight(i["e_gw"])), (b["gb"][0:1, :], i["e_gb"]), (b["b1"][:, :], i["e_b1"]),
                         (b["b2"][0:1, :, :].rearrange("p a b -> p (a b)"), i["e_b2"].rearrange("e n -> (e n)").unsqueeze(0))]
                for dst, src in loads:
                    sp.dma_start(dst, src).then_inc(s["w_in"], 16)
                sp.wait_ge(s["w_in"], 16 * len(loads))
                sp.sem_inc(s["loaded"], 1)
                with sp.Fori(0, TILES - 1) as t:
                    wait(net, sp, s["acc"], t + 1)
                    sp.dma_start(net.out[bass.ds(t * P, P), :], rows(net.X[:, bass.ds(t, 1), :])).then_inc(s["stored"], 16)
                sp.wait_ge(s["acc"], TILES)
                sp.dma_start(net.out[(TILES - 1) * P:N, :], net.X[0:LAST, TILES - 1, :]).then_inc(s["stored"], 16)
                sp.wait_ge(s["stored"], 16 * TILES)

            @block.tensor
            def _(pe):
                pe.wait_ge(s["loaded"], 1)
                ones = net.const("ones")[0:1, :]
                with pe.Fori(0, TILES) as t:
                    wait(net, pe, s["xn"], t + 1)
                    turned(pe, net, B[0], b["xn"], 2).then_inc(s["tr"], 1)
                    wait(net, pe, s["xnT"], t + 1)
                    products(pe, B[1][:, 0:EXPERTS], [(b["xnT"][:, k, :], b["gw"][:, k, :]) for k in range(2)] + [(ones, b["gb"][0:1, :])]).then_inc(s["gl"], 1)

                    def up(e):
                        wait(net, pe, s["gelu"], t * EXPERTS + e + 1)
                        for i in range(4):
                            ins = products(pe, B[2 + e % 2][:, i * P:(i + 1) * P], [(w1[:, e, k, i * P:(i + 1) * P], b["xnT"][:, k, :]) for k in range(2)])
                        ins.then_inc(s["h"], 1)

                    def down(e):
                        wait(net, pe, s["gelu"], t * EXPERTS + e + 3)
                        wait(net, pe, s["y_used"], t * EXPERTS + e + 1)
                        products(pe, B[4 + e % 2][:, 0:D], [(b["hT"][:, e % 2, k, :], b["w2"][:, e, k, :]) for k in range(4)] +
                                 [(ones, b["b2"][0:1, e, :])]).then_inc(s["y"], 1)

                    up(0)
                    for e in range(1, EXPERTS):
                        up(e)
                        down(e - 1)
                    down(EXPERTS - 1)

            @block.scalar
            def _(act):
                act.wait_ge(s["loaded"], 1)
                act.sem_inc(s["gelu"], 2)
                with act.Fori(0, TILES) as t:
                    wait(net, act, s["tr"], t + 1)
                    act.activation(b["xnT"][:, :, :].rearrange("p a b -> p (a b)"), B[0][:, 0:D], ACT.Copy).then_inc(s["xnT"], 1)
                    for e in range(EXPERTS):
                        wait(net, act, s["h"], t * EXPERTS + e + 1)
                        wait(net, act, s["y"], t * EXPERTS + e + 1)
                        for i in range(4):
                            ins = act.activation(b["hT"][:, e % 2, i, :], B[2 + e % 2][:, i * P:(i + 1) * P], ACT.Gelu, bias=b["b1"][:, e * 4 + i:e * 4 + i + 1])
                        ins.then_inc(s["gelu"], 1)

            @block.vector
            def _(dve):
                make_before(dve, EXPERTS, b)
                dve.wait_ge(s["loaded"], 1)
                dve.sem_inc(s["y_used"], 2)
                dve.sem_inc(s["y"], 2)
                with dve.Fori(0, TILES) as t:
                    x = rows(net.X[:, bass.ds(t, 1), :])
                    dve.tensor_scalar(b["xn"][:, :], x, net.rstd[:, bass.ds(t, 1)], net.shift[:, bass.ds(t, 1)], ALU.mult, ALU.add).then_inc(s["xn"], 1)
                    wait(net, dve, s["gl"], t + 1)
                    dve.tensor_copy(b["g"][:, :], B[1][:, 0:EXPERTS])
                    dve.drain()
                    top_two(dve, net, EXPERTS, b["g"][:, :], b)
                    for e in range(EXPERTS):
                        wait(net, dve, s["y"], t * EXPERTS + e + 3)
                        ins = dve.scalar_tensor_tensor(x, B[4 + e % 2][:, 0:D], b["sel"][:, e:e + 1], x, ALU.mult, ALU.add).then_inc(s["y_used"], 1)
                        dve.drain()
                    dve.sem_inc(s["acc"], 1)


def build(nc, ins, out):
    net = Net()
    pool_sems[0] = POOL_SEM
    net.inp, net.out = ins, out
    dram = lambda name, shape, dt=F32: nc.dram_tensor(name, shape, dt, kind="Internal").ap()
    net.table = dram("table", (NPAD, D))
    net.src_tab = dram("src_tab", (NPAD, H))
    net.node_rec = dram("node_rec", (NPAD, 2 * H))
    net.src_pad = dram("src_pad", (ETILES, P), I32)
    net.dst_pad = dram("dst_pad", (ETILES, P), I32)
    net.run_max = dram("run_max", (EPAD, H))
    net.start_rec = dram("start_rec", (EPAD, 2 * H))
    net.weights = dram("weights", (ETILES, P * H))
    net.tile_row = dram("tile_row", (1, SPAD), I32)
    net.keys = dram("keys", (1, NPAD))
    net.sorted_x = dram("sorted_x", (NPAD, D))
    net.mamba_y = dram("mamba_y", (NPAD, D))
    with ExitStack() as c:
        net.tick = c.enter_context(nc.semaphore("tick"))
        sb = lambda name, shape, dt=F32: c.enter_context(nc.sbuf_tensor(name, shape, dt))
        net.PS = [c.enter_context(nc.psum_tensor(f"bank{i}", [P, 512], F32)) for i in range(8)]
        net.C = sb("consts", [P, CONST_N])
        net.const = lambda k: net.C[:, slice(*CONST_COLS[k])]
        net.X = sb("X", [P, TILES, D])
        net.zeros = sb("zeros", [P, 512])
        net.stat = sb("stat", [P, 8])
        net.rstd, net.shift = sb("rstd", [P, TILES]), sb("shift", [P, TILES])
        net.node_src, net.node_dst = sb("node_src", [P, TILES, H]), sb("node_dst", [P, TILES, H])
        net.node_max = sb("node_max", [P, TILES, H])
        net.kv, net.ksum = sb("kv", [P, 2, P]), sb("ksum", [P, 2, 4])
        net.starts, net.ends, net.degree = sb("starts", [P, TILES], I32), sb("ends", [P, TILES], I32), sb("degree", [P, TILES])
        net.src_degree = sb("src_degree", [P, TILES])
        net.agg = sb("agg", [P, TILES, D + H])
        net.step_src = sb("step_src", [P, SPAD], I32)
        net.step_et = sb("step_et", [P, SBLK], I32)
        net.step_dst = sb("step_dst", [P, SPAD])
        net.edge = sb("edge", [P, SPAD * H])
        net.key_top, net.lam, net.guard = sb("key_top", [P, D]), sb("lam", [P, 2, D]), sb("guard", [P, TILES, H])
        net.rank = sb("rank", [P, TILES], I32)
        stages = [load_stage,
                  lambda nc, net: norm_stage(nc, net, "norm0"),
                  project_stage, pad_edges_stage,
                  lambda nc, net: gather_stage(nc, net, "gather0", [degree_work, rank_work]), index_stage,
                  lambda nc, net: weight_stage(nc, net, "weight0", 0.01),
                  lambda nc, net: aggregate_stage(nc, net, "agg0"), combine_stage,
                  lambda nc, net: norm_stage(nc, net, "norm1"), project1_stage, lambda_stage,
                  sort_stage, mamba_stage,
                  lambda nc, net: weight_stage(nc, net, "weight1", 0.2), guard_stage,
                  lambda nc, net: aggregate_stage(nc, net, "agg1"), final_stage,
                  lambda nc, net: norm_stage(nc, net, "norm2"), expert_stage]
        for run in stages:
            run(nc, net)


def layout(i):
    f = {}
    a = lambda x: np.ascontiguousarray(np.asarray(x))

    def diagonal(src, dst):
        out = np.zeros((D, 8), np.float32)
        for h in range(H):
            out[h * 64:(h + 1) * 64, h] = np.asarray(src[h]).reshape(64)
            out[h * 64:(h + 1) * 64, 4 + h] = np.asarray(dst[h]).reshape(64)
        return out

    f["consts"] = constants()
    f["x"], f["src"], f["dst"] = a(i["x"]), a(i["src"]).reshape(1, E), a(i["dst"]).reshape(1, E)
    f["noise"] = a(i["node_vec"]).reshape(1, N)
    heads = lambda w: np.asarray(w).transpose(1, 0, 2).reshape(D, D)
    f["g0_w"] = a(heads(i["L0_gnn_W_fc"]))
    f["g0_wT"] = a(f["g0_w"].T)
    f["g0_al"] = diagonal(i["L0_gnn_W_ar"], i["L0_gnn_W_al"])
    f["g0_res"] = a(heads(i["L0_gnn_W_res"]))
    f["m0_wkv"] = a(np.concatenate([i["L0_mix_Wk"], i["L0_mix_Wv"]], 1))
    f["m0_wq"], f["m0_wm"], f["m0_w1"], f["m0_w2"] = (a(i["L0_mix_" + k]) for k in ("Wq", "Wm", "W1", "W2"))
    row = lambda *v: a(np.stack([np.asarray(x).reshape(-1) for x in v]).reshape(1, -1))
    f["m0_norms"] = row(i["L0_mix_g1"], i["L0_mix_b1"], i["L0_mix_g2"], i["L0_mix_b2"])
    experts = lambda w: np.asarray(w).transpose(1, 0, 2).reshape(w.shape[1], -1)
    f["f0_w1"] = a(np.concatenate([i["L0_ffn_sW1"], experts(i["L0_ffn_eW1"])], 1))
    f["f0_b1"] = a(np.concatenate([np.asarray(i["L0_ffn_sb1"]), np.asarray(i["L0_ffn_eb1"]).reshape(-1)]).reshape(6, P).T)
    f["f0_w2"], f["f0_e2"] = a(i["L0_ffn_sW2"]), a(experts(i["L0_ffn_eW2"]))
    f["f0_b2"] = a(np.asarray(i["L0_ffn_sb2"]).reshape(P, 1))
    f["f0_eb2"] = a(np.asarray(i["L0_ffn_eb2"]).T)
    f["f0_w3"], f["f0_e3"] = a(i["L0_ffn_sW3"]), a(np.asarray(i["L0_ffn_eW3"]).transpose(1, 0, 2).reshape(64, -1))
    f["f0_b3"] = a(np.asarray(i["L0_ffn_sb3"]).reshape(1, D))
    f["f0_eb3"] = a(np.asarray(i["L0_ffn_eb3"]).reshape(1, -1))
    f["f0_gw"], f["f0_gb"] = a(i["L0_ffn_gW"]), a(np.asarray(i["L0_ffn_gb"]).reshape(1, -1))
    g = {k[7:]: np.asarray(v) for k, v in i.items() if k.startswith("L1_gnn_")}
    f["g1_w"], f["g1_wT"] = a(g["gat_w"].T), a(g["gat_w"])
    f["g1_al"] = diagonal(g["gat_a_src"], g["gat_a_tgt"])
    f["g1_rows"] = row(g["gat_b"], g["ln_local_g"], g["ln_local_b"], g["ln_global_g"], g["ln_global_b"], g["ln2_g"],
                       g["ln2_b"], g["ff2_b"])
    f["s_in"], f["s_x"], f["s_dt"], f["s_out"] = (a(g[k].T) for k in ("in_proj_w", "x_proj_w", "dt_proj_w", "out_proj_w"))
    cols = lambda v: np.asarray(v).reshape(2, P, -1).transpose(1, 0, 2)
    f["s_cols"] = a(np.concatenate([cols(g[k]) for k in ("conv_w", "conv_b", "dt_proj_b", "D_param", "A_log")], 2).reshape(P, -1))
    f["g1_gates"] = a(np.concatenate([g["wl"].T, g["wg"].T], 0))
    f["g1_ff1"], f["g1_ff2"] = a(g["ff1_w"].T), a(g["ff2_w"].T)
    f["g1_ff1b"] = a(g["ff1_b"].reshape(4, P).T)
    m = {k[7:]: np.asarray(v) for k, v in i.items() if k.startswith("L1_mix_")}
    f["m1_wq"] = a(m["W_qk"][0])
    f["m1_wkv"] = a(np.concatenate([m["W_qk"][1], m["W_v"]], 1))
    f["m1_bkv"] = a(np.concatenate([m["b_qk"][1], m["b_v"]]).reshape(1, -1))
    f["m1_cols"] = a(np.stack([m["b_qk"][0], m["gamma"], m["beta"]], 1).reshape(2, P, 3).transpose(1, 0, 2).reshape(P, 6))
    f["e_gw"], f["e_gb"] = a(i["L1_ffn_Wg"]), a(np.asarray(i["L1_ffn_bg"]).reshape(1, -1))
    f["e_w1"] = a(i["L1_ffn_W1"]).reshape(8 * D, 512)
    f["e_b1"] = a(np.asarray(i["L1_ffn_b1"]).reshape(8 * 4, P).T)
    f["e_w2"] = a(i["L1_ffn_W2"]).reshape(8 * 512, D)
    f["e_b2"] = a(i["L1_ffn_b2"])
    return f


def kernel(**inputs):
    import concourse.bacc as _bacc
    from concourse.bass_utils import run_bass_kernel_spmd as _run

    nc = _bacc.Bacc("TRN2", target_bir_lowering=False, num_devices=1)
    arrays = layout(inputs)
    ins = {k: nc.dram_tensor(f"in_{k}", v.shape, mybir.dt.from_np(v.dtype), kind="ExternalInput").ap() for k, v in arrays.items()}
    out = nc.dram_tensor("out_x", (N, D), F32, kind="ExternalOutput").ap()
    build(nc, ins, out)
    got = _run(nc, [{f"in_{k}": v for k, v in arrays.items()}], core_ids=[0])
    return got.results[0]["out_x"]
```

```python
from contextlib import ExitStack, contextmanager

import numpy as np

import concourse.bass as bass
from concourse import mybir

F32 = mybir.dt.float32
I32 = mybir.dt.int32
ALU = mybir.AluOpType
ACT = mybir.ActivationFunctionType
AX = mybir.AxisListType

P = 128
N = 6250
E = 200000
D = 256
H = 4
TILES = (N + P - 1) // P
NPAD = TILES * P
LAST = N - (TILES - 1) * P
GROUP = 16
ETILES = -(-E // (P * GROUP)) * GROUP
EPAD = ETILES * P
EROW = EPAD // P
STEPS = -(-2 * (-(-E // (2 * P)) + TILES - 1) // (2 * GROUP)) * 2 * GROUP
SBLK = (STEPS + P - 1) // P
SPAD = SBLK * P
FIRST_SEM = 100
POOL_SEM = 220
pool_sems = [POOL_SEM]
BIG = 1.0e30
FAR = 1 << 20
LN_EPS = 1e-5

CONST_COLS = dict(ident=(0, 128), iota=(128, 256), upper=(256, 384), ones=(384, 512), block32=(512, 640),
                  valid=(640, 640 + TILES), step=(700, 700 + SBLK), bound=(720, 720 + TILES - 1),
                  head32=(780, 784), pid=(784, 785), eps=(785, 786), mhalf=(786, 787), zero=(787, 788),
                  one=(788, 789), lower=(800, 928), half=(928, 928 + SBLK))
CONST_N = 928 + SBLK


def constants():
    c = np.zeros((P, CONST_N), np.float32)
    p = np.arange(P)

    def put(k, v):
        lo, hi = CONST_COLS[k]
        c[:, lo:hi] = v

    put("ident", np.eye(P))
    put("iota", np.broadcast_to(p, (P, P)))
    put("upper", p[:, None] < p[None, :])
    put("lower", p[:, None] > p[None, :])
    put("ones", 1.0)
    put("block32", p[:, None] // 32 == p[None, :] // 32)
    put("valid", p[:, None] + P * np.arange(TILES)[None, :] < N)
    steps = p[:, None] + P * np.arange(SBLK)[None, :]
    put("step", steps // 2)
    put("half", steps % 2)
    put("bound", np.arange(1, TILES)[None, :])
    put("head32", p[:, None] // 32 == np.arange(4)[None, :])
    put("pid", p[:, None])
    put("eps", LN_EPS)
    put("mhalf", -0.5)
    put("one", 1.0)
    return c


class Net:
    pass


def rows(ap):
    return ap.rearrange("p a b -> p (a b)")


def wait(net, eng, sem, value):
    eng.wait_ge(sem, value)


def wait_apart(net, eng, sem, value):
    eng.wait_ge(sem, value)
    eng.sem_inc(net.tick, 1)


@contextmanager
def stage(nc, name, sems):
    pool = [x for x in sems if x.startswith("gp_")]
    rest = [x for x in sems if not x.startswith("gp_")]
    with ExitStack() as c:
        ns = {x: c.enter_context(nc.semaphore(f"{name}_{x}", num=first + i))
              for first, group in ((FIRST_SEM, rest), (pool_sems[0], pool)) for i, x in enumerate(group)}
        pool_sems[0] += len(pool)
        with nc.Block() as block:
            yield block, ns
        nc.all_engine_barrier(sems_to_clear=range(FIRST_SEM, FIRST_SEM + len(rest)))


def buffers(nc, c, name, **shapes):
    return {k: c.enter_context(nc.sbuf_tensor(f"{name}_{k}", [P] + list(v), I32 if k.endswith("_i") else F32))
            for k, v in shapes.items()}


def weight(dram):
    return dram.rearrange("(a p) n -> p a n", p=P)


def load_stage(nc, net):
    with stage(nc, "load", ["zeroed", "x_in", "c_in"]) as (block, s):
        @block.vector
        def _(dve):
            dve.memset(net.X[:, TILES - 1, :], 0.0).then_inc(s["zeroed"], 1)
            dve.memset(net.zeros[:, :], 0.0)
            dve.memset(net.stat[:, 0:1], 0.0)

        @block.sync
        def _(sp):
            sp.dma_start(net.C[:, :], net.inp["consts"]).then_inc(s["c_in"], 16)
            sp.dma_start(net.X[:, 0:TILES - 1, :],
                         net.inp["x"][0:(TILES - 1) * P, :].rearrange("(t p) d -> p t d", p=P)).then_inc(s["x_in"], 16)
            sp.wait_ge(s["zeroed"], 1)
            sp.dma_start(net.X[0:LAST, TILES - 1, :], net.inp["x"][(TILES - 1) * P:N, :]).then_inc(s["x_in"], 16)
            sp.wait_ge(s["x_in"], 32)
            sp.wait_ge(s["c_in"], 16)


def norm_stage(nc, net, name):
    with ExitStack() as c:
        b = buffers(nc, c, name, six=[TILES, 6], mean=[TILES], gap=[TILES], var=[TILES])
        with stage(nc, name, ["stats", "rstd"]) as (block, s):
            @block.vector
            def _(dve):
                with dve.Fori(0, TILES // 7) as it:
                    for k in range(7):
                        t = it * 7 + k
                        dve.bn_stats(rows(b["six"][:, bass.ds(t, 1), :]), rows(net.X[:, bass.ds(t, 1), :]))
                dve.drain()
                even, odd = b["six"][:, :, 0:3], b["six"][:, :, 3:6]
                dve.tensor_tensor(b["mean"][:, :], even[:, :, 1], odd[:, :, 1], ALU.add)
                dve.tensor_tensor(b["gap"][:, :], even[:, :, 1], odd[:, :, 1], ALU.subtract)
                dve.tensor_tensor(b["var"][:, :], even[:, :, 2], odd[:, :, 2], ALU.add)
                dve.drain()
                dve.tensor_tensor(b["gap"][:, :], b["gap"][:, :], b["gap"][:, :], ALU.mult)
                dve.drain()
                dve.scalar_tensor_tensor(b["var"][:, :], b["gap"][:, :], D / 4.0, b["var"][:, :], ALU.mult, ALU.add)
                dve.drain()
                dve.tensor_scalar(b["var"][:, :], b["var"][:, :], 1.0 / D, LN_EPS, ALU.mult, ALU.add).then_inc(s["stats"], 1)
                dve.wait_ge(s["rstd"], 1)
                dve.scalar_tensor_tensor(net.shift[:, :], b["mean"][:, :], -0.5, net.rstd[:, :], ALU.mult, ALU.mult)

            @block.gpsimd
            def _(pool):
                pool.wait_ge(s["stats"], 1)
                pool.tensor_tensor(net.rstd[:, :], b["var"][:, :], net.const("mhalf").to_broadcast([P, TILES]),
                                   ALU.pow).then_inc(s["rstd"], 1)


def project_stage(nc, net):
    with ExitStack() as c:
        b = buffers(nc, c, "proj", w=[2, 264], wT=[2, D], al=[2, 8], wkv=[2, 512], kvacc=[2, 132])
        bw = pair_buffers(nc, c, "proj_t", net.edge, xn=[D], xnT=[2, P], tab=[D], kx=[D], ke=[D], vv=[2, 132])
        TR, TAB, KV, SUM = ([net.PS[4 * w + i] for w in range(2)] for i in range(4))
        names = ["w_in", "folded", "fold_ps", "xn", "tr", "xnT", "mm", "tab_sb", "tab_out0", "tab_out1", "src_out", "kmin", "kexp",
                 "kv_ready", "kv_mm", "end"]
        with stage(nc, "proj", names) as (block, s):
            tab_out = (s["tab_out0"], s["tab_out1"])

            @block.sync
            def _(sp):
                sp.dma_start(b["w"][:, :, 0:D], weight(net.inp["g0_w"])).then_inc(s["w_in"], 16)
                sp.dma_start(b["wT"][:, :, :], weight(net.inp["g0_wT"])).then_inc(s["w_in"], 16)
                sp.dma_start(b["al"][:, :, :], weight(net.inp["g0_al"])).then_inc(s["w_in"], 16)
                sp.dma_start(b["wkv"][:, :, :], weight(net.inp["m0_wkv"])).then_inc(s["w_in"], 16)
                store_table(net, sp, s, bw, tab_out)

            @block.vector
            def _(dve):
                dve.memset(b["kvacc"][:, :, :], 0.0)
                dve.wait_ge(s["fold_ps"], 1)
                for i in range(2):
                    ins = dve.tensor_copy(b["w"][:, i, D:D + 8], TAB[0][:, 8 * i:8 * i + 8])
                ins.then_inc(s["folded"], 1)

                def tiles(it, ws):
                    n = lambda w: 2 * it + w + 1
                    for w in ws:
                        dve.tensor_scalar(bw[w]["xn"][:, :], rows(net.X[:, bass.ds(2 * it + w, 1), :]), net.rstd[:, bass.ds(2 * it + w, 1)],
                                          net.shift[:, bass.ds(2 * it + w, 1)], ALU.mult, ALU.add).then_inc(s["xn"], 1)
                    for w in ws:
                        wait(net, dve, s["mm"], n(w))
                        dve.tensor_scalar(bw[w]["kx"][:, :], KV[w][:, 0:D], 0.0, None, ALU.min).then_inc(s["kmin"], 1)
                    for w in ws:
                        dve.tensor_copy(bw[w]["vv"][:, :, 0:P], KV[w][:, D:2 * D].rearrange("p (a b) -> p a b", a=2))
                        for i in range(2):
                            dve.tensor_scalar(bw[w]["vv"][:, i, P:P + 1], net.const("valid")[:, bass.ds(2 * it + w, 1)], 1.0, None, ALU.mult)
                    for w in ws:
                        wait(net, dve, s["kexp"], n(w))
                        dve.scalar_tensor_tensor(bw[w]["ke"][:, :], KV[w][:, 0:D], 0.0, bw[w]["kx"][:, :], ALU.max, ALU.add).then_inc(s["kv_ready"], 1)
                    for w in ws:
                        wait(net, dve, s["kv_mm"], n(w))
                        dve.tensor_tensor(b["kvacc"][:, :, 0:P + 1], b["kvacc"][:, :, 0:P + 1],
                                          SUM[w][:, 0:264].rearrange("p (a b) -> p a b", a=2)[:, :, 0:P + 1], ALU.add)
                        dve.drain()

                with dve.Fori(0, TILES // 2) as it:
                    tiles(it, (0, 1))
                tiles(TILES // 2, (0,))
                for i in range(2):
                    dve.tensor_tensor(net.kv[:, i, :], b["kvacc"][:, i, 0:P], net.const("block32"), ALU.mult)
                    dve.tensor_scalar(net.ksum[:, i, :], net.const("head32"), b["kvacc"][:, i, P:P + 1], None, ALU.mult)

            @block.scalar
            def _(act):
                def tiles(it, ws):
                    n = lambda w: 2 * it + w + 1
                    for w in ws:
                        wait(net, act, s["tr"], n(w))
                        act.activation(rows(bw[w]["xnT"][:, :, :]), TR[w][:, 0:D], ACT.Copy).then_inc(s["xnT"], 1)
                    for w in ws:
                        wait(net, act, s["kmin"], n(w))
                        act.activation(bw[w]["kx"][:, :], bw[w]["kx"][:, :], ACT.Exp).then_inc(s["kexp"], 1)
                    for w in ws:
                        take_table(net, act, s, bw[w], TAB[w], tab_out[w], it, w)

                for w in range(2):
                    act.sem_inc(tab_out[w], 1)
                with act.Fori(0, TILES // 2) as it:
                    tiles(it, (0, 1))
                tiles(TILES // 2, (0,))
                act.sem_inc(s["end"], 1)

            @block.tensor
            def _(pe):
                pe.wait_ge(s["w_in"], 64)
                for i in range(2):
                    for k in range(2):
                        ins = pe.matmul(TAB[0][:, 8 * i:8 * i + 8], b["wT"][:, k, i * P:(i + 1) * P], b["al"][:, k, :],
                                        start=(k == 0), stop=(k == 1))
                ins.then_inc(s["fold_ps"], 1)
                pe.wait_ge(s["folded"], 1)

                def tiles(it, ws):
                    n = lambda w: 2 * it + w + 1
                    for w in ws:
                        wait(net, pe, s["xn"], n(w))
                        turned(pe, net, TR[w], bw[w]["xn"], 2).then_inc(s["tr"], 1)
                    for w in ws:
                        xnT = bw[w]["xnT"]
                        wait(net, pe, s["xnT"], n(w))
                        wait(net, pe, s["tab_sb"], n(w))
                        products(pe, TAB[w][:, 0:264], [(xnT[:, k, :], b["w"][:, k, :]) for k in range(2)])
                        products(pe, KV[w][:, :], [(xnT[:, k, :], b["wkv"][:, k, :]) for k in range(2)]).then_inc(s["mm"], 1)
                    for w in ws:
                        wait(net, pe, s["kv_ready"], n(w))
                        for i in range(2):
                            ins = pe.matmul(SUM[w][:, i * 132:i * 132 + P + 1], bw[w]["ke"][:, i * P:(i + 1) * P], bw[w]["vv"][:, i, 0:P + 1],
                                            start=True, stop=True)
                        ins.then_inc(s["kv_mm"], 1)

                pe.sem_inc(s["tab_sb"], 2)
                with pe.Fori(0, TILES // 2) as it:
                    tiles(it, (0, 1))
                tiles(TILES // 2, (0,))


def take_table(net, act, s, t, bank, tab_out, it, w):
    wait(net, act, s["mm"], 2 * it + w + 1)
    act.activation(rows(net.node_src[:, bass.ds(2 * it + w, 1), :]), bank[:, D:D + 4], ACT.Copy)
    act.activation(rows(net.node_dst[:, bass.ds(2 * it + w, 1), :]), bank[:, D + 4:D + 8], ACT.Copy)
    wait(net, act, tab_out, 16 * it + 1)
    act.activation(t["tab"][:, 0:D], bank[:, 0:D], ACT.Copy).then_inc(s["tab_sb"], 1)


def store_table(net, sp, s, bw, tab_out):
    def tiles(it, ws):
        for w in ws:
            wait(net, sp, s["tab_sb"], 2 * it + w + 3)
            sp.dma_start(net.table[bass.ds((2 * it + w) * P, P), :], bw[w]["tab"][:, 0:D]).then_inc(tab_out[w], 16)

    with sp.Fori(0, TILES // 2) as it:
        tiles(it, (0, 1))
    tiles(TILES // 2, (0,))
    sp.wait_ge(s["end"], 1)
    sp.dma_start(net.src_tab.rearrange("(t p) c -> p t c", p=P), net.node_src[:, :, :]).then_inc(s["src_out"], 16)
    sp.wait_ge(s["src_out"], 16)
    sp.wait_ge(tab_out[0], 16 * (TILES - TILES // 2) + 1)
    sp.wait_ge(tab_out[1], 16 * (TILES // 2) + 1)



def pad_edges_stage(nc, net):
    with ExitStack() as c:
        b = buffers(nc, c, "pad", minus_i=[64])
        with stage(nc, "pad", ["ready", "moved"]) as (block, s):
            @block.vector
            def _(dve):
                dve.memset(b["minus_i"][:, :], -1).then_inc(s["ready"], 1)

            @block.sync
            def _(sp):
                pads = EPAD - E
                for src, dst in ((net.inp["src"], net.src_pad), (net.inp["dst"], net.dst_pad)):
                    flat = dst.rearrange("t e -> (t e)")
                    sp.dma_start(flat[0:E].rearrange("(a b) -> a b", a=125),
                                 src.rearrange("o (a b) -> (o a) b", a=125)).then_inc(s["moved"], 16)
                sp.wait_ge(s["ready"], 1)
                for dst in (net.src_pad, net.dst_pad):
                    sp.dma_start(dst.rearrange("t e -> (t e)")[E:EPAD].rearrange("(a b) -> a b", b=64),
                                 b["minus_i"][0:pads // 64, :]).then_inc(s["moved"], 16)
                sp.dma_start(net.start_rec.rearrange("(p a b) c -> p a (b c)", p=P, a=28), net.zeros[:, 0:448].unsqueeze(1).to_broadcast([P, 28, 448])).then_inc(s["moved"], 16)
                sp.wait_ge(s["moved"], 80)


def degree_work(nc, net, c, block, s, b):
    G = 8
    oh = dict(
        lo=c.enter_context(nc.sbuf_tensor("deg_hot_lo", [P, 2, G, P], mybir.dt.bfloat16)),
        hi=c.enter_context(nc.sbuf_tensor("deg_hot_hi", [P, 2, G, TILES], mybir.dt.bfloat16)))
    d = buffers(nc, c, "deg", raw_i=[EROW], lo_i=[EROW])
    digits = net.agg[:, :, :].rearrange("p a b -> p (a b)")[:, 0:4 * EROW].rearrange("p (a q g) -> p a q g", a=2, q=2)
    d["lo"], d["hi"] = digits[:, 0, :, :], digits[:, 1, :, :]
    ps = net.PS[0:2]
    iota = net.PS[7][:, 0:P]
    acc = [net.degree, net.src_degree]

    @block.vector
    def _(dve):
        dve.sem_inc(s["deg_add"], 2)
        dve.tensor_copy(iota, net.const("iota"))
        for q in range(2):
            dve.memset(acc[q][:, :], 0.0)
        for q, raw in enumerate((b["dst_i"], b["src_i"])):
            dve.wait_ge(s["edges_in"], 32)
            dve.tensor_scalar(d["raw_i"][:, :], raw[:, :], 7, None, ALU.arith_shift_right)
            dve.tensor_scalar(d["lo_i"][:, :], raw[:, :], P - 1, None, ALU.bitwise_and)
            dve.drain()
            dve.tensor_copy(d["hi"][:, q, :], d["raw_i"][:, :])
            dve.tensor_copy(d["lo"][:, q, :], d["lo_i"][:, :])
            dve.drain()
        with dve.Fori(0, EROW // G) as it:
            for q in range(2):
                for wide, num, out in ((P, d["lo"], oh["lo"]), (TILES, d["hi"], oh["hi"])):
                    ins = dve.tensor_tensor(out[:, q, :, :], iota[:, 0:wide].unsqueeze(1).to_broadcast([P, G, wide]),
                                            num[:, q, bass.ds(it * G, G)].unsqueeze(2).to_broadcast([P, G, wide]), ALU.is_equal)
                ins.then_inc(s["deg_hot"], 1)
            for q in range(2):
                wait(net, dve, s["deg_mm"], it * 2 + q + 1)
                dve.tensor_tensor(acc[q][:, :], acc[q][:, :], ps[q][:, 0:TILES], ALU.add).then_inc(s["deg_add"], 1)
            dve.drain()

    @block.tensor
    def _(pe):
        with pe.Fori(0, EROW // G) as it:
            for q in range(2):
                wait(net, pe, s["deg_hot"], it * 2 + q + 1)
                wait(net, pe, s["deg_add"], 2 * it + q + 1)
                for g in range(G):
                    ins = pe.matmul(ps[q][:, 0:TILES], oh["lo"][:, q, g, :], oh["hi"][:, q, g, :],
                                    start=(g == 0), stop=(g == G - 1))
                ins.then_inc(s["deg_mm"], 1)


def gather_stage(nc, net, name, works):
    SET = 16
    with ExitStack() as c:
        b = buffers(nc, c, name, src_i=[EROW], dst_i=[EROW], idx_src_i=[EROW], idx_i=[2, SET], land=[2, SET, H])
        names = ["edges_in", "clipped", "idx_ready", "gp_landed0", "gp_landed1", "taken0", "taken1",
                 "deg_hot", "deg_mm", "deg_add", "noise_clear", "noise_in", "keys_ready", "keys_out", "keys_in"]
        with stage(nc, name, names) as (block, s):
            landed, taken = (s["gp_landed0"], s["gp_landed1"]), (s["taken0"], s["taken1"])

            @block.sync
            def _(sp):
                sp.dma_start(b["src_i"][:, :], net.src_pad.rearrange("(p a) e -> p (a e)", p=P) if EROW % P == 0 else
                             net.src_pad.rearrange("t e -> (t e)").rearrange("(p g) -> p g", p=P)).then_inc(s["edges_in"], 16)
                sp.dma_start(b["dst_i"][:, :], net.dst_pad.rearrange("t e -> (t e)").rearrange("(p g) -> p g", p=P)).then_inc(s["edges_in"], 16)
                sp.wait_ge(s["edges_in"], 32)

            @block.gpsimd
            def _(pool):
                pool.wait_ge(s["edges_in"], 32)
                pool.tensor_scalar(b["idx_src_i"][:, :], b["src_i"][:, :], 0, None, ALU.max).then_inc(s["clipped"], 1)
                pool.wait_ge(s["clipped"], 1)
                with pool.Fori(0, EROW // (2 * SET)) as it:
                    for q in range(2):
                        wait(net, pool, taken[q], it + 1)
                        pool.tensor_copy(b["idx_i"][:, q, :], b["idx_src_i"][:, bass.ds((it * 2 + q) * SET, SET)]).then_inc(s["idx_ready"], 1)
                        wait_apart(net, pool, s["idx_ready"], it * 2 + q + 1)
                        for r in range(SET):
                            pool.indirect_dma_start(b["land"][:, q, r, :], None, net.src_tab,
                                                    bass.IndirectOffsetOnAxis(ap=b["idx_i"][:, q, r:r + 1], axis=0)).then_inc(landed[q], 16)

            @block.scalar
            def _(act):
                for q in range(2):
                    act.sem_inc(taken[q], 1)
                with act.Fori(0, EROW // (2 * SET)) as it:
                    for q in range(2):
                        wait(net, act, landed[q], (it + 1) * 16 * SET)
                        act.activation(net.edge[:, bass.ds((it * 2 + q) * SET * H, SET * H)], b["land"][:, q, :, :].rearrange("p a b -> p (a b)"),
                                       ACT.Copy).then_inc(taken[q], 1)

            for work in works:
                work(nc, net, c, block, s, b)


def index_stage(nc, net):
    with ExitStack() as c:
        b = buffers(nc, c, "index", within=[TILES], total=[TILES], run=[TILES], f=[TILES], thr_i=[TILES], thr=[TILES],
                    hit=[TILES], tile=[SBLK], tile128=[SBLK], tile_i=[SBLK], etile=[SBLK], 
                    rows_i=[SBLK, 2, P], rows=[SBLK, 2, P])
        pa, pb, pt = net.PS[0], net.PS[1], net.PS[2]
        with stage(nc, "index", ["sums", "etile", "gp_rows_in", "rows_f", "tr", "copied", "tile_out", "tile_rdy"]) as (block, s):
            @block.tensor
            def _(pe):
                pe.matmul(pa[:, 0:TILES], net.const("upper"), net.degree[:, :], start=True, stop=True)
                pe.matmul(pb[:, 0:TILES], net.const("ones"), net.degree[:, :], start=True, stop=True).then_inc(s["sums"], 1)
                for j in range(SBLK):
                    pe.wait_ge(s["rows_f"], j + 1)
                    if j:
                        pe.wait_ge(s["copied"], j)
                    for q in range(2):
                        ins = pe.transpose(pt[:, q * P:(q + 1) * P], b["rows"][:, j, q, :], net.const("ident"))
                    ins.then_inc(s["tr"], 1)

            @block.vector
            def _(dve):
                dve.wait_ge(s["sums"], 1)
                dve.tensor_copy(b["total"][:, :], pb[:, 0:TILES])
                dve.tensor_copy(b["within"][:, :], pa[:, 0:TILES])
                dve.drain()
                dve.tensor_tensor_scan(b["run"][:, :], net.const("ones")[:, 0:TILES], b["total"][:, :], 0.0, ALU.mult, ALU.add)
                dve.drain()
                dve.tensor_tensor(b["run"][:, :], b["run"][:, :], b["total"][:, :], ALU.subtract)
                dve.drain()
                dve.tensor_tensor(b["f"][:, :], b["run"][:, :], b["within"][:, :], ALU.add)
                dve.drain()
                dve.tensor_scalar(b["hit"][:, :], net.degree[:, :], 0.0, float(FAR), ALU.is_equal, ALU.mult)
                dve.drain()
                dve.tensor_tensor(net.starts[:, :], b["f"][:, :], b["hit"][:, :], ALU.add)
                dve.tensor_tensor(b["f"][:, :], b["f"][:, :], net.degree[:, :], ALU.add)
                dve.drain()
                dve.tensor_scalar(net.ends[:, :], b["f"][:, :], 1.0, 0.0, ALU.subtract, ALU.max)
                dve.tensor_copy(b["thr_i"][:, :], b["run"][:, :])
                dve.drain()
                dve.tensor_scalar(b["thr_i"][:, :], b["thr_i"][:, :], 8, None, ALU.arith_shift_right)
                dve.drain()
                dve.tensor_copy(b["thr"][:, :], b["thr_i"][:, :])
                dve.drain()
                dve.tensor_tensor(b["thr"][:, 1:TILES], b["thr"][:, 1:TILES], net.const("bound"), ALU.add)
                dve.drain()
                for j in range(SBLK):
                    dve.tensor_scalar(b["hit"][:, 1:TILES], b["thr"][:, 1:TILES], net.const("step")[:, j:j + 1], None, ALU.is_le,
                                      ALU.add, accum_out=b["tile"][:, j:j + 1])
                    dve.drain()
                dve.tensor_tensor(b["etile"][:, :], net.const("step"), b["tile"][:, :], ALU.subtract)
                dve.tensor_scalar(b["tile128"][:, :], b["tile"][:, :], float(P), None, ALU.mult)
                dve.tensor_scalar(b["tile_i"][:, :], b["tile"][:, :], float(D + H), None, ALU.mult).then_inc(s["tile_rdy"], 1)
                dve.drain()
                dve.scalar_tensor_tensor(b["etile"][:, :], b["etile"][:, :], 2.0, net.const("half"), ALU.mult, ALU.add)
                dve.drain()
                dve.tensor_scalar(net.step_et[:, :], b["etile"][:, :], float(ETILES - 1), None, ALU.min).then_inc(s["etile"], 1)
                for j in range(SBLK):
                    dve.wait_ge(s["gp_rows_in"], 32 * SBLK)
                    dve.tensor_scalar(b["rows"][:, j, 0, :], b["rows_i"][:, j, 0, :], 0.0, None, ALU.max)
                    dve.tensor_scalar(b["rows"][:, j, 1, :], b["rows_i"][:, j, 1, :], b["tile128"][:, j:j + 1], None, ALU.subtract).then_inc(s["rows_f"], 1)
                    dve.wait_ge(s["tr"], j + 1)
                    dve.tensor_copy(net.step_src[:, j * P:(j + 1) * P], pt[:, 0:P])
                    dve.tensor_copy(net.step_dst[:, j * P:(j + 1) * P], pt[:, P:2 * P]).then_inc(s["copied"], 1)

            @block.gpsimd
            def _(pool):
                pool.wait_ge(s["etile"], 1)
                for j in range(SBLK):
                    for q, tab in enumerate((net.src_pad, net.dst_pad)):
                        pool.indirect_dma_start(b["rows_i"][:, j, q, :], None, tab,
                                                bass.IndirectOffsetOnAxis(ap=net.step_et[:, j:j + 1], axis=0)).then_inc(s["gp_rows_in"], 16)

            @block.sync
            def _(sp):
                sp.wait_ge(s["tile_rdy"], 1)
                with nc.allow_non_contiguous_dma("13 x 128 step numbers"):
                    sp.dma_start(net.tile_row.rearrange("o (j p) -> p (o j)", p=P), b["tile_i"][:, :]).then_inc(s["tile_out"], 16)
                sp.wait_ge(s["tile_out"], 16)


def weight_stage(nc, net, name, slope):
    rec = net.agg[:, :, :].rearrange("p a b -> p (a b)")[:, 0:EROW * 8].rearrange("p (g c) -> p g c", c=8)
    edge = net.edge[:, 0:EROW * H].rearrange("p (g c) -> p g c", c=H)
    w_rows = net.agg[:, :, :].rearrange("p a b -> p (a b)")[:, 0:SBLK * 512].rearrange("p (j c) -> p j c", c=512)
    with ExitStack() as c:
        b = buffers(nc, c, name, dst=[EROW], pen=[EROW], keep=[EROW], run=[EROW, H],
                    match=[P], diag=[H, P], spread=[H, P], carry=[H], node=[TILES, 8], z=[TILES, H],
                    first_i=[1], first=[8], hit=[TILES])
        dst_i = net.agg[:, :, :].rearrange("p a b -> p (a b)")[:, 0:EROW].bitcast(I32)
        p_last, p_row, p_t = net.PS[0], net.PS[1], net.PS[2:6]
        names = ["dst_in", "last_ps", "diag", "spread", "carried", "run_out", "gp_node_in", "node_done", "node_out", "first_idx",
                 "gp_first_in", "gp_scatter", "rec_in", "rec_ready", "exp_in", "exp_out", "w_out", "gp_rows_in", "tr", "copied", "dcopy", "etile", "sums"]
        with stage(nc, name, names) as (block, s):
            edges_of = lambda a: a.rearrange("(p g) c -> p g c", p=P)

            @block.sync
            def _(sp):
                sp.dma_start(dst_i, net.dst_pad.rearrange("t e -> (t e)").rearrange("(p g) -> p g", p=P)).then_inc(s["dst_in"], 16)
                sp.wait_ge(s["carried"], 1)
                sp.dma_start(edges_of(net.run_max), b["run"][:, :, :]).then_inc(s["run_out"], 16)
                sp.wait_ge(s["node_done"], 1)
                sp.dma_start(net.node_rec.rearrange("(t p) c -> p t c", p=P), b["node"][:, :, :]).then_inc(s["node_out"], 16)
                sp.wait_ge(s["gp_scatter"], 16 * TILES)
                sp.dma_start(rec, edges_of(net.start_rec)).then_inc(s["rec_in"], 16)
                sp.wait_ge(s["exp_out"], 1)
                sp.dma_start(net.weights.rearrange("t c -> (t c)").rearrange("(p g) -> p g", p=P), net.edge[:, 0:EROW * H]).then_inc(s["w_out"], 16)
                sp.wait_ge(s["w_out"], 16)

            @block.gpsimd
            def _(pool):
                pool.wait_ge(s["run_out"], 16)
                for t in range(TILES):
                    pool.indirect_dma_start(net.node_max[:, t, :], None, net.run_max,
                                            bass.IndirectOffsetOnAxis(ap=net.ends[:, t:t + 1], axis=0)).then_inc(s["gp_node_in"], 16)
                pool.wait_ge(s["node_done"], 1)
                for t in range(TILES):
                    pool.indirect_dma_start(net.start_rec, bass.IndirectOffsetOnAxis(ap=net.starts[:, t:t + 1], axis=0),
                                            b["node"][:, t, :], None, bounds_check=EPAD - 1, oob_is_err=False).then_inc(s["gp_scatter"], 16)
                pool.wait_ge(s["node_out"], 16)
                pool.wait_ge(s["first_idx"], 1)
                pool.indirect_dma_start(b["first"][:, :], None, net.node_rec,
                                        bass.IndirectOffsetOnAxis(ap=b["first_i"][:, 0:1], axis=0)).then_inc(s["gp_first_in"], 16)
                pool.wait_ge(s["w_out"], 16)
                for j in range(SBLK):
                    pool.indirect_dma_start(w_rows[:, j, :], None, net.weights,
                                            bass.IndirectOffsetOnAxis(ap=net.step_et[:, j:j + 1], axis=0)).then_inc(s["gp_rows_in"], 16)

            @block.tensor
            def _(pe):
                pe.wait_ge(s["diag"], 1)
                pe.matmul(p_last[:, 0:P], net.const("ones"), b["diag"][:, 0, :], start=True, stop=True).then_inc(s["last_ps"], 1)
                pe.wait_ge(s["diag"], 2)
                pe.matmul(p_row[:, :], net.const("ones"), b["diag"][:, :, :].rearrange("p a b -> p (a b)"), start=True, stop=True).then_inc(s["spread"], 1)
                for j in range(SBLK):
                    pe.wait_ge(s["gp_rows_in"], 16 * SBLK)
                    if j >= 4:
                        pe.wait_ge(s["copied"], j - 3)
                    for h in range(H):
                        ins = pe.transpose(p_t[j % 4][:, h * P:(h + 1) * P],
                                           w_rows[:, j, :].rearrange("p (e h) -> p e h", h=H)[:, :, h], net.const("ident"))
                    ins.then_inc(s["tr"], 1)

            @block.scalar
            def _(act):
                act.wait_ge(s["exp_in"], 1)
                act.activation(net.edge[:, 0:EROW * H], net.edge[:, 0:EROW * H], ACT.Exp).then_inc(s["exp_out"], 1)
                for j in range(SBLK):
                    act.wait_ge(s["tr"], j + 1)
                    act.wait_ge(s["w_out"], 16)
                    act.activation(net.edge[:, j * P * H:(j + 1) * P * H].rearrange("p (s h) -> p h s", h=H),
                                   p_t[j % 4][:, :].rearrange("p (h s) -> p h s", h=H), ACT.Copy).then_inc(s["copied"], 1)

            @block.vector
            def _(dve):
                flat = lambda a: a.rearrange("p a b -> p (a b)")
                dve.wait_ge(s["dst_in"], 16)
                dve.tensor_copy(b["dst"][:, :], dst_i)
                dve.drain()
                dve.tensor_scalar(b["first_i"][:, :], b["dst"][:, 0:1], 0.0, None, ALU.max).then_inc(s["first_idx"], 1)
                dve.tensor_scalar(b["diag"][:, 0, :], net.const("ident"), b["dst"][:, EROW - 1:EROW], None, ALU.mult).then_inc(s["diag"], 1)
                dve.tensor_tensor(b["keep"][:, 1:EROW], b["dst"][:, 1:EROW], b["dst"][:, 0:EROW - 1], ALU.is_equal)
                dve.memset(b["keep"][:, 0:1], 0.0)
                dve.drain()
                dve.tensor_scalar(b["pen"][:, :], b["keep"][:, :], BIG, BIG, ALU.mult, ALU.subtract)
                dve.drain()
                dve.memset(b["pen"][:, 0:1], 0.0)
                dve.wait_ge(s["last_ps"], 1)
                dve.tensor_scalar(b["match"][:, :], p_last[:, 0:P], b["dst"][:, 0:1], None, ALU.is_equal)
                dve.drain()
                dve.tensor_tensor(b["match"][:, :], b["match"][:, :], net.const("lower"), ALU.mult)
                dve.drain()
                dve.tensor_scalar(b["match"][:, :], b["match"][:, :], BIG, BIG, ALU.mult, ALU.subtract)
                for h in range(H):
                    dve.tensor_tensor_scan(b["run"][:, :, h], b["pen"][:, :], edge[:, :, h], -BIG, ALU.add, ALU.max)
                dve.drain()
                for h in range(H):
                    ins = dve.tensor_scalar(b["diag"][:, h, :], net.const("ident"), b["run"][:, EROW - 1, h:h + 1], None, ALU.mult)
                ins.then_inc(s["diag"], 1)
                dve.wait_ge(s["spread"], 1)
                for h in range(H):
                    dve.tensor_tensor(b["spread"][:, h, :], b["match"][:, :], p_row[:, h * P:(h + 1) * P], ALU.add)
                dve.drain()
                dve.tensor_reduce(b["carry"][:, :], b["spread"][:, :, :], AX.X, ALU.max)
                dve.drain()
                for h in range(H):
                    ins = dve.tensor_tensor_scan(b["run"][:, :, h], b["pen"][:, :], edge[:, :, h], b["carry"][:, h:h + 1], ALU.add, ALU.max)
                ins.then_inc(s["carried"], 1)
                dve.wait_ge(s["gp_node_in"], 16 * TILES)
                dve.tensor_tensor(flat(b["z"][:, :, :]), flat(net.node_dst[:, :, :]), flat(net.node_max[:, :, :]), ALU.add)
                dve.tensor_copy(b["node"][:, :, 0:H], net.node_dst[:, :, :])
                dve.drain()
                dve.scalar_tensor_tensor(flat(net.node_max[:, :, :]), flat(b["z"][:, :, :]), slope, flat(b["z"][:, :, :]), ALU.mult, ALU.max)
                dve.drain()
                dve.tensor_scalar(b["hit"][:, :], net.degree[:, :], 0.0, None, ALU.is_gt)
                dve.drain()
                for h in range(H):
                    dve.tensor_tensor(net.node_max[:, :, h], net.node_max[:, :, h], b["hit"][:, :], ALU.mult)
                dve.drain()
                dve.tensor_copy(b["node"][:, :, H:2 * H], net.node_max[:, :, :]).then_inc(s["node_done"], 1)
                dve.wait_ge(s["rec_in"], 16)
                dve.wait_ge(s["gp_first_in"], 16)
                dve.tensor_copy(rec[:, 0, :], b["first"][:, :])
                dve.drain()
                for k in range(8):
                    dve.tensor_tensor_scan(rec[:, :, k], b["keep"][:, :], rec[:, :, k], 0.0, ALU.mult, ALU.add)
                dve.drain()
                dve.tensor_tensor(edge, edge, rec[:, :, 0:H], ALU.add)
                dve.drain()
                dve.scalar_tensor_tensor(flat(edge), flat(edge), slope, flat(edge), ALU.mult, ALU.max)
                dve.drain()
                dve.tensor_tensor(edge, edge, rec[:, :, H:2 * H], ALU.subtract)
                dve.drain()
                dve.tensor_scalar(flat(edge), flat(edge), 0.0, None, ALU.min).then_inc(s["exp_in"], 1)


def aggregate_stage(nc, net, name):
    SETS, SET, RING = 4, 8, 4
    U = SETS * SET
    PAIRS = U // 2
    A_HEADS = 3
    AHEAD = RING - 1
    aggf = net.agg[:, :, :].rearrange("p a b -> p (a b)")
    with ExitStack() as c:
        b = buffers(nc, c, name, idx_i=[SETS, SET], got=[U, D], hot=[RING, 2, P], wx=[RING, 2, D])
        where = c.enter_context(nc.sbuf_tensor(f"{name}_where", [1, SPAD], I32))
        names = ["where_in", "idx_ready"] + [f"gp_landed{i}" for i in range(SETS)] + \
                ["weighed", "hot", "mm"]
        with stage(nc, name, names) as (block, s):
            landed = (s["gp_landed0"], s["gp_landed1"], s["gp_landed2"], s["gp_landed3"])

            @block.sync
            def _(sp):
                sp.dma_start(where[:, :], net.tile_row).then_inc(s["where_in"], 16)
                sp.wait_ge(s["where_in"], 16)

            @block.gpsimd
            def _(pool):
                with pool.Fori(0, STEPS // U) as it:
                    for q in range(SETS):
                        wait_apart(net, pool, s["weighed"], it * U + (q + 1) * SET)
                        wait(net, pool, s["hot"], it * U + (q + 1) * SET)
                        pool.tensor_copy(b["idx_i"][:, q, :], net.step_src[:, bass.ds((it * SETS + q) * SET, SET)]).then_inc(s["idx_ready"], 1)
                        wait_apart(net, pool, s["idx_ready"], it * SETS + q + 1)
                        for r in range(SET):
                            pool.indirect_dma_start(b["got"][:, q * SET + r, :], None, net.table,
                                                    bass.IndirectOffsetOnAxis(ap=b["idx_i"][:, q, r:r + 1], axis=0)).then_inc(landed[q], 16)

            @block.scalar
            def _(act):
                act.sem_inc(s["weighed"], U)
                with act.Fori(0, STEPS // U) as it:
                    for u in range(U):
                        if u % SET == 0:
                            wait(net, act, landed[u // SET], (it + 1) * 16 * SET)
                        if u % 2 == 0:
                            wait(net, act, s["mm"], it * PAIRS + u // 2 + 1)
                        for h in range(A_HEADS):
                            ins = act.activation(b["wx"][:, u // 2 % RING, u % 2, h * 64:(h + 1) * 64], b["got"][:, u, h * 64:(h + 1) * 64], ACT.Copy,
                                                 scale=net.edge[:, bass.ds((it * U + u) * H + h, 1)])
                        ins.then_inc(s["weighed"], 1)

            @block.tensor
            def _(pe):
                pe.sem_inc(s["mm"], RING)
                with pe.Fori(0, STEPS // U) as it:
                    for k in range(PAIRS):
                        r = k % RING
                        wait(net, pe, s["hot"], it * U + 2 * (k + 1) + U)
                        wait(net, pe, s["weighed"], it * U + 2 * (k + 1) + U)
                        for i in range(2):
                            pe.matmul(net.PS[r][:, 0:D], b["hot"][:, r, i, :], b["wx"][:, r, i, :], start=(i == 0), stop=(i == 1))
                        for i in range(2):
                            ins = pe.matmul(net.PS[r][:, D:D + H], b["hot"][:, r, i, :], net.edge[:, bass.ds((it * U + 2 * k + i) * H, H)],
                                            start=(i == 0), stop=(i == 1))
                        ins.then_inc(s["mm"], 1)

            @block.vector
            def _(dve):
                dve.sem_inc(s["hot"], U)
                dve.memset(aggf, 0.0)
                dve.wait_ge(s["where_in"], 16)

                def one_hot(it, k):
                    wait(net, dve, s["mm"], it * PAIRS + k + 1)
                    for i in range(2):
                        step = it * U + 2 * k + i
                        dve.tensor_scalar(b["hot"][:, k % RING, i, :], net.const("iota"), net.step_dst[:, bass.ds(step, 1)], None, ALU.is_equal)
                        if i == 0 and 2 * k % SET == 0:
                            wait(net, dve, landed[2 * k // SET], (it + 1) * 16 * SET)
                        for h in range(A_HEADS, H):
                            ins = dve.tensor_scalar(b["wx"][:, k % RING, i, h * 64:(h + 1) * 64], b["got"][:, 2 * k + i, h * 64:(h + 1) * 64],
                                                    net.edge[:, bass.ds(step * H + h, 1)], None, ALU.mult)
                        ins.then_inc(s["hot"], 1)

                def round_of(it, last):
                    for k in range(PAIRS):
                        at = dve.value_load(where[0:1, bass.ds(it * U + 2 * k, 1)], min_val=0, max_val=(TILES - 1) * (D + H))
                        wait(net, dve, s["mm"], it * PAIRS + k + 1 + RING)
                        dve.tensor_tensor(aggf[:, bass.ds(at, D + H)], aggf[:, bass.ds(at, D + H)], net.PS[k % RING][:, 0:D + H], ALU.add)
                        dve.drain()
                        if k + AHEAD < PAIRS:
                            one_hot(it, k + AHEAD)
                        elif not last:
                            one_hot(it + 1, k + AHEAD - PAIRS)

                for k in range(AHEAD):
                    one_hot(0, k)
                with dve.Fori(0, STEPS // U - 1) as it:
                    round_of(it, False)
                round_of(STEPS // U - 1, True)


SMALL = dict(six=[6], mv=[2], var=[1], rs=[1])


def pair_buffers(nc, c, name, spare, **shapes):
    first, second, at = buffers(nc, c, name, **shapes), {}, 0
    for k, v in shapes.items():
        size = int(np.prod(v))
        part = spare[:, at:at + size]
        if len(v) == 2:
            part = part.rearrange("p (a b) -> p a b", a=v[0])
        second[k] = part
        at += size
    return first, second


def norm_value(it, ws, w, k):
    return it * 6 + k * len(ws) + w + 1


def norm_stats(dve, s, b, x, out=None, gain=None):
    dve.bn_stats(b["six"][:, :], x)
    dve.drain()
    dve.bn_aggr(b["mv"][:, :], b["six"][:, :])
    dve.drain()
    dve.tensor_scalar(b["var"][:, :], b["mv"][:, 1:2], LN_EPS, None, ALU.add).then_inc(s["var_ready"], 1)
    if gain is not None:
        dve.scalar_tensor_tensor(out, x, b["mv"][:, 0:1], gain, ALU.subtract, ALU.mult)


def norm_apply(net, dve, s, b, centred, out, value, shift):
    dve.drain()
    wait(net, dve, s["rstd_ready"], value)
    return dve.scalar_tensor_tensor(out, centred, b["rs"][:, :], shift, ALU.mult, ALU.add)


def norm_power(net, pool, s, b, value):
    wait(net, pool, s["var_ready"], value)
    pool.tensor_tensor(b["rs"][:, :], b["var"][:, :], net.const("mhalf"), ALU.pow).then_inc(s["rstd_ready"], 1)


def top_two(dve, net, n, g, b):
    pair = lambda t: t[:, 0:n * n].rearrange("p (e j) -> p e j", e=n)
    mine = g.unsqueeze(2).to_broadcast([P, n, n])
    theirs = g.unsqueeze(1).to_broadcast([P, n, n])
    dve.tensor_tensor(pair(b["gt"]), theirs, mine, ALU.is_gt)
    dve.tensor_tensor(pair(b["eq"]), theirs, mine, ALU.is_equal)
    dve.drain()
    dve.tensor_tensor(pair(b["eq"]), pair(b["eq"]), pair(b["before"]), ALU.mult)
    dve.drain()
    dve.tensor_tensor(pair(b["gt"]), pair(b["gt"]), pair(b["eq"]), ALU.add)
    dve.drain()
    dve.tensor_reduce(b["sel"][:, 0:n], pair(b["gt"]), AX.X, ALU.add)
    dve.drain()
    dve.tensor_scalar(b["sel"][:, 0:n], b["sel"][:, 0:n], 2.0, None, ALU.is_lt)
    dve.drain()


def make_before(dve, n, b):
    dve.memset(b["before"][:, :], 0.0)
    dve.drain()
    for e in range(1, n):
        dve.memset(b["before"][:, e * n:e * n + e], 1.0)


def combine_stage(nc, net):
    with ExitStack() as c:
        b = buffers(nc, c, "comb", wq=[2, D], wres=[2, D], wm=[2, D], w1=[4, 512], w2=[4, D], norms=[4, D],
                    f1=[2, 768], f1b=[6], f2=[2, P], f2b=[1], e2=[4, 64], eb2=[4], f3=[D], b3=[D], e3=[4, D], gw=[2, 4], gb=[4],
                    before=[16])
        bw = pair_buffers(nc, c, "comb_t", net.edge,
                          xn=[D], cat=[4, P], qx=[D], qe=[D], den=[8], msg=[D], hT=[4, P], sum=[D], rden=[4], nb=[D],
                          yT=[2, P], h1=[6, P], h2=[P], h2e=[4, P],
                          gt=[16], eq=[16], sel=[4], g=[4], gmax=[1], gsum=[1], x1=[D], y=[D], **SMALL)
        for t in bw:
            t["before"] = b["before"]
        TURN, MAIN, SIDE, KEEP = ([net.PS[4 * w + i] for w in range(2)] for i in range(4))
        names = ["w_in", "xn", "tr_x", "xT", "q", "qmin", "qexp", "qe", "msg", "msgn", "tr_m", "mT", "wm", "m1", "tr_1", "oT",
                 "h", "hr", "w2", "x1y", "tr_y", "yT", "f1", "f1r", "f2", "f2r", "f3", "gl", "gexp_in", "gexp", "g2_in", "g2",
                 "var_ready", "rstd_ready", "done"]
        with stage(nc, "comb", names) as (block, s):
            @block.sync
            def _(sp):
                i = net.inp
                loads = [(b["wq"][:, :, :], weight(i["m0_wq"])), (b["wres"][:, :, :], weight(i["g0_res"])), (b["wm"][:, :, :], weight(i["m0_wm"])),
                         (b["w1"][:, :, :], weight(i["m0_w1"])), (b["w2"][:, :, :], weight(i["m0_w2"])),
                         (rows(b["norms"][:, :, :]), i["m0_norms"].to_broadcast([P, 4 * D])),
                         (b["f1"][:, :, :], weight(i["f0_w1"])), (b["f1b"][:, :], i["f0_b1"]), (b["f2"][:, :, :], weight(i["f0_w2"])),
                         (b["f2b"][:, :], i["f0_b2"]), (rows(b["e2"][:, :, :]), i["f0_e2"]), (b["eb2"][0:64, :], i["f0_eb2"]),
                         (b["f3"][:, :], i["f0_w3"]), (b["b3"][0:1, :], i["f0_b3"]), (rows(b["e3"][0:64, :, :]), i["f0_e3"]),
                         (rows(b["e3"][64:65, :, :]), i["f0_eb3"]), (b["gw"][:, :, :], weight(i["f0_gw"])), (b["gb"][0:1, :], i["f0_gb"])]
                for dst, src in loads:
                    sp.dma_start(dst, src).then_inc(s["w_in"], 16)
                sp.wait_ge(s["w_in"], 16 * len(loads))
                sp.sem_inc(s["done"], 1)

            def walk(eng, body):
                body(0, 0, False, True, True)
                with eng.Fori(0, TILES // 2 - 1) as it:
                    body(2 * it + 1, 1, True, True, True)
                    body(2 * it + 2, 0, True, True, True)
                body(TILES - 2, 1, True, True, True)
                body(TILES - 1, 0, True, True, False)
                body(TILES, 1, True, False, False)

            @block.gpsimd
            def _(pool):
                def body(t, w, before, now, after):
                    for k in range(3):
                        if now:
                            norm_power(net, pool, s, bw[w], 3 * t + k + 1)

                walk(pool, body)

            @block.tensor
            def _(pe):
                ones = net.const("ones")

                def start(t, w):
                    cat = bw[w]["cat"]
                    wait(net, pe, s["xn"], t + 1)
                    turned(pe, net, TURN[w], bw[w]["xn"], 2).then_inc(s["tr_x"], 1)
                    wait(net, pe, s["xT"], t + 1)
                    for i in range(2):
                        ins = products(pe, MAIN[w][:, i * P:(i + 1) * P], [(b["wq"][:, k, i * P:(i + 1) * P], cat[:, k, :]) for k in range(2)])
                    ins.then_inc(s["q"], 1)
                    products(pe, KEEP[w][:, 0:D], [(cat[:, k, :], b["wres"][:, k, :]) for k in range(2)])

                def body(t, w, before, now, after):
                    v = 1 - w
                    if before:
                        yT, h1 = bw[v]["yT"], bw[v]["h1"]
                        wait(net, pe, s["x1y"], t)
                        turned(pe, net, TURN[v], bw[v]["y"], 2).then_inc(s["tr_y"], 1)
                        wait(net, pe, s["yT"], t)
                        products(pe, KEEP[v][:, 0:4], [(yT[:, k, :], b["gw"][:, k, :]) for k in range(2)] + [(ones[0:1, :], b["gb"][0:1, :])]).then_inc(s["gl"], 1)
                        for i in range(6):
                            out = MAIN[v][:, i * P:(i + 1) * P] if i < 4 else SIDE[v][:, (i - 4) * P:(i - 3) * P]
                            ins = products(pe, out, [(b["f1"][:, k, i * P:(i + 1) * P], yT[:, k, :]) for k in range(2)])
                        ins.then_inc(s["f1"], 1)
                    if now:
                        qe = bw[w]["qe"]
                        wait(net, pe, s["qe"], t + 1)
                        for i in range(2):
                            products(pe, SIDE[w][:, i * P:(i + 1) * P], [(qe[:, i * P:(i + 1) * P], net.kv[:, i, :])])
                            ins = products(pe, SIDE[w][:, D + 4 * i:D + 4 * i + 4], [(qe[:, i * P:(i + 1) * P], net.ksum[:, i, :])])
                        ins.then_inc(s["msg"], 1)
                        wait(net, pe, s["msgn"], t + 1)
                        turned(pe, net, TURN[w], bw[w]["msg"], 2).then_inc(s["tr_m"], 1)
                    if before:
                        wait(net, pe, s["f1r"], t)
                        products(pe, SIDE[v][:, 0:P], [(b["f2"][:, k, :], h1[:, k, :]) for k in range(2)])
                        for e in range(4):
                            ins = products(pe, TURN[v][0:64, e * P:(e + 1) * P], [(b["e2"][:, e, :], h1[:, 2 + e, :])])
                        ins.then_inc(s["f2"], 1)
                    if now:
                        wait(net, pe, s["mT"], t + 1)
                        products(pe, MAIN[w][:, 0:D], [(bw[w]["cat"][:, 2 + k, :], b["wm"][:, k, :]) for k in range(2)]).then_inc(s["wm"], 1)
                    if before:
                        wait(net, pe, s["f2r"], t)
                        products(pe, TURN[v][:, 0:D], [(bw[v]["h2"][:, :], b["f3"][:, :]), (ones[0:1, :], b["b3"][0:1, :])])
                        for e in range(4):
                            ins = products(pe, (MAIN, SIDE)[e // 2][v][:, (e % 2) * D:(e % 2 + 1) * D], [(bw[v]["h2e"][0:65, e, :], b["e3"][0:65, e, :])])
                        ins.then_inc(s["f3"], 1)
                    if now:
                        wait(net, pe, s["m1"], t + 1)
                        turned(pe, net, TURN[w], bw[w]["msg"], 2).then_inc(s["tr_1"], 1)
                        wait(net, pe, s["oT"], t + 1)
                        for i in range(4):
                            ins = products(pe, SIDE[w][:, i * P:(i + 1) * P], [(b["w1"][:, k, i * P:(i + 1) * P], bw[w]["cat"][:, k, :]) for k in range(4)])
                        ins.then_inc(s["h"], 1)
                        wait(net, pe, s["hr"], t + 1)
                        products(pe, MAIN[w][:, 0:D], [(bw[w]["hT"][:, k, :], b["w2"][:, k, :]) for k in range(4)]).then_inc(s["w2"], 1)
                    if after:
                        start(t + 1, v)

                pe.wait_ge(s["done"], 1)
                start(0, 0)
                walk(pe, body)

            @block.scalar
            def _(act):
                def start(t, w):
                    wait(net, act, s["tr_x"], t + 1)
                    act.activation(rows(bw[w]["cat"][:, 0:2, :]), TURN[w][:, 0:D], ACT.Copy).then_inc(s["xT"], 1)

                def body(t, w, before, now, after):
                    v = 1 - w
                    if before:
                        wait(net, act, s["tr_y"], t)
                        act.activation(rows(bw[v]["yT"][:, :, :]), TURN[v][:, 0:D], ACT.Copy).then_inc(s["yT"], 1)
                    if now:
                        wait(net, act, s["qmin"], t + 1)
                        act.activation(bw[w]["qx"][:, :], bw[w]["qx"][:, :], ACT.Exp).then_inc(s["qexp"], 1)
                    if before:
                        wait(net, act, s["gexp_in"], t)
                        act.activation(bw[v]["g"][:, :], bw[v]["g"][:, :], ACT.Exp).then_inc(s["gexp"], 1)
                        wait(net, act, s["f1"], t)
                        for i in range(6):
                            src = MAIN[v][:, i * P:(i + 1) * P] if i < 4 else SIDE[v][:, (i - 4) * P:(i - 3) * P]
                            ins = act.activation(bw[v]["h1"][:, i, :], src, ACT.Relu, bias=b["f1b"][:, i:i + 1])
                        ins.then_inc(s["f1r"], 1)
                        wait(net, act, s["g2_in"], t)
                        act.activation(bw[v]["g"][:, :], bw[v]["g"][:, :], ACT.Exp).then_inc(s["g2"], 1)
                    if now:
                        wait(net, act, s["tr_m"], t + 1)
                        act.activation(rows(bw[w]["cat"][:, 2:4, :]), TURN[w][:, 0:D], ACT.Copy).then_inc(s["mT"], 1)
                    if before:
                        wait(net, act, s["f2"], t)
                        act.activation(bw[v]["h2"][:, :], SIDE[v][:, 0:P], ACT.Relu, bias=b["f2b"][:, :])
                        for e in range(4):
                            ins = act.activation(bw[v]["h2e"][0:64, e, :], TURN[v][0:64, e * P:(e + 1) * P], ACT.Relu, bias=b["eb2"][0:64, e:e + 1])
                        ins.then_inc(s["f2r"], 1)
                    if now:
                        wait(net, act, s["tr_1"], t + 1)
                        act.activation(rows(bw[w]["cat"][:, 2:4, :]), TURN[w][:, 0:D], ACT.Copy).then_inc(s["oT"], 1)
                        wait(net, act, s["h"], t + 1)
                        act.activation(rows(bw[w]["hT"][:, :, :]), SIDE[w][:, :], ACT.Relu).then_inc(s["hr"], 1)
                    if after:
                        start(t + 1, v)

                act.wait_ge(s["done"], 1)
                start(0, 0)
                walk(act, body)

            @block.vector
            def _(dve):
                heads = lambda a, n: a.rearrange("p (h d) -> p h d", h=n)
                spread = lambda a, n, d: a.unsqueeze(2).to_broadcast([P, n, d])
                norm = lambda k: b["norms"][:, k, :]
                full = lambda w, k: bw[w][k][:, :]

                def start(t, w):
                    agg, rden = rows(net.agg[:, bass.ds(t, 1), :]), full(w, "rden")
                    dve.tensor_scalar(full(w, "xn"), rows(net.X[:, bass.ds(t, 1), :]), net.rstd[:, bass.ds(t, 1)], net.shift[:, bass.ds(t, 1)],
                                      ALU.mult, ALU.add).then_inc(s["xn"], 1)
                    dve.tensor_scalar(rden, agg[:, D:D + H], 1e-9, None, ALU.max)
                    dve.drain()
                    dve.reciprocal(rden, rden)
                    dve.drain()
                    dve.tensor_tensor(heads(full(w, "sum"), H), heads(agg[:, 0:D], H), spread(rden, H, 64), ALU.mult)

                def body(t, w, before, now, after):
                    v = 1 - w
                    if now:
                        x = rows(net.X[:, bass.ds(t, 1), :])
                        wait(net, dve, s["q"], t + 1)
                        dve.tensor_scalar(full(w, "qx"), MAIN[w][:, 0:D], 0.0, None, ALU.min).then_inc(s["qmin"], 1)
                    if before:
                        g, top, total, sel = full(v, "g"), full(v, "gmax"), full(v, "gsum"), full(v, "sel")
                        wait(net, dve, s["gl"], t)
                        dve.tensor_reduce(top, KEEP[v][:, 0:4], AX.X, ALU.max)
                        dve.drain()
                        dve.tensor_scalar(g, KEEP[v][:, 0:4], top, None, ALU.subtract).then_inc(s["gexp_in"], 1)
                    if now:
                        wait(net, dve, s["qexp"], t + 1)
                        dve.scalar_tensor_tensor(full(w, "qe"), MAIN[w][:, 0:D], 0.0, full(w, "qx"), ALU.max, ALU.add).then_inc(s["qe"], 1)
                    if before:
                        wait(net, dve, s["gexp"], t)
                        dve.tensor_reduce(total, g, AX.X, ALU.add)
                        dve.drain()
                        dve.reciprocal(total, total)
                        dve.drain()
                        dve.tensor_scalar(g, g, total, None, ALU.mult)
                        dve.drain()
                        top_two(dve, net, 4, g, bw[v])
                        dve.tensor_reduce(top, g, AX.X, ALU.max)
                        dve.drain()
                        dve.tensor_scalar(g, g, top, None, ALU.subtract).then_inc(s["g2_in"], 1)
                    if now:
                        den = full(w, "den")
                        wait(net, dve, s["msg"], t + 1)
                        dve.tensor_scalar(den, SIDE[w][:, D:D + 8], 1e-6, None, ALU.add)
                        dve.drain()
                        dve.reciprocal(den, den)
                        dve.drain()
                        dve.tensor_tensor(heads(full(w, "msg"), 8), heads(SIDE[w][:, 0:D], 8), spread(den, 8, 32), ALU.mult).then_inc(s["msgn"], 1)
                        dve.tensor_tensor(full(w, "sum"), full(w, "sum"), KEEP[w][:, 0:D], ALU.add)
                        dve.drain()
                        dve.scalar_tensor_tensor(full(w, "sum"), full(w, "sum"), 0.0, x, ALU.max, ALU.add)
                        dve.drain()
                        dve.tensor_tensor(full(w, "sum"), full(w, "sum"), full(w, "xn"), ALU.add)
                        dve.drain()
                        dve.tensor_tensor(full(w, "sum"), full(w, "sum"), norm(3), ALU.add)
                    if before:
                        wait(net, dve, s["g2"], t)
                        dve.tensor_tensor(sel, sel, g, ALU.mult)
                        dve.drain()
                        dve.tensor_reduce(total, sel, AX.X, ALU.add)
                        dve.drain()
                        dve.reciprocal(total, total)
                        dve.drain()
                        dve.tensor_scalar(sel, sel, total, None, ALU.mult)
                    if now:
                        wait(net, dve, s["wm"], t + 1)
                        norm_stats(dve, s, bw[w], MAIN[w][:, 0:D], full(w, "msg"), norm(0))
                        norm_apply(net, dve, s, bw[w], full(w, "msg"), full(w, "msg"), 3 * t + 1, norm(1)).then_inc(s["m1"], 1)
                    if before:
                        x1, last_x = full(v, "x1"), rows(net.X[:, bass.ds(t - 1, 1), :])
                        wait(net, dve, s["f3"], t)
                        dve.tensor_tensor(x1, x1, TURN[v][:, 0:D], ALU.add)
                        for e in range(4):
                            dve.drain()
                            dve.scalar_tensor_tensor(x1 if e < 3 else last_x, (MAIN, SIDE)[e // 2][v][:, (e % 2) * D:(e % 2 + 1) * D],
                                                     sel[:, e:e + 1], x1, ALU.mult, ALU.add)
                    if after:
                        start(t + 1, v)
                    if now:
                        wait(net, dve, s["w2"], t + 1)
                        norm_stats(dve, s, bw[w], MAIN[w][:, 0:D], full(w, "nb"), norm(2))
                        norm_apply(net, dve, s, bw[w], full(w, "nb"), full(w, "x1"), 3 * t + 2, full(w, "sum"))
                        dve.drain()
                        norm_stats(dve, s, bw[w], full(w, "x1"))
                        wait(net, dve, s["rstd_ready"], 3 * t + 3)
                        dve.tensor_scalar(full(w, "y"), full(w, "x1"), bw[w]["mv"][:, 0:1], bw[w]["rs"][:, :], ALU.subtract, ALU.mult).then_inc(s["x1y"], 1)

                make_before(dve, 4, b)
                for w in range(2):
                    dve.memset(bw[w]["h2e"][64:65, :, :], 1.0)
                dve.wait_ge(s["done"], 1)
                start(0, 0)
                walk(dve, body)


def products(pe, out, parts):
    for k, (left, right) in enumerate(parts):
        ins = pe.matmul(out, left, right, start=(k == 0), stop=(k == len(parts) - 1))
    return ins


def turned(pe, net, out, src, n):
    for k in range(n):
        ins = pe.transpose(out[:, k * P:(k + 1) * P], src[:, k * P:(k + 1) * P], net.const("ident"))
    return ins


def project1_stage(nc, net):
    with ExitStack() as c:
        b = buffers(nc, c, "proj1", w=[2, 264], wT=[2, D], al=[2, 8], wkv=[2, 512], bkv=[512],
                    top=[D], pen=[TILES], col=[2], diag=[2, P])
        bw = pair_buffers(nc, c, "proj1_t", net.edge, xn=[D], xnT=[2, P], tab=[D])
        TR, TAB, KEYS = ([net.PS[4 * w + i] for w in range(2)] for i in range(3))
        p_top = net.PS[3]
        names = ["w_in", "folded", "fold_ps", "xn", "tr", "xnT", "mm", "k_used", "tab_sb", "tab_out0", "tab_out1", "src_out", "end", "top", "top_tr", "diag", "top_row"]
        with stage(nc, "proj1", names) as (block, s):
            tab_out = (s["tab_out0"], s["tab_out1"])

            @block.sync
            def _(sp):
                for dst, src in ((b["w"][:, :, 0:D], weight(net.inp["g1_w"])), (b["wT"][:, :, :], weight(net.inp["g1_wT"])),
                                 (b["al"][:, :, :], weight(net.inp["g1_al"])), (b["wkv"][:, :, :], weight(net.inp["m1_wkv"])),
                                 (b["bkv"][0:1, :], net.inp["m1_bkv"])):
                    sp.dma_start(dst, src).then_inc(s["w_in"], 16)
                store_table(net, sp, s, bw, tab_out)

            @block.vector
            def _(dve):
                dve.memset(b["top"][:, :], -BIG)
                dve.tensor_scalar(b["pen"][:, :], net.const("valid"), BIG, BIG, ALU.mult, ALU.subtract)
                dve.wait_ge(s["fold_ps"], 1)
                for i in range(2):
                    ins = dve.tensor_copy(b["w"][:, i, D:D + 8], TAB[0][:, 8 * i:8 * i + 8])
                ins.then_inc(s["folded"], 1)

                def tiles(it, ws):
                    for w in ws:
                        dve.tensor_scalar(bw[w]["xn"][:, :], rows(net.X[:, bass.ds(2 * it + w, 1), :]), net.rstd[:, bass.ds(2 * it + w, 1)],
                                          net.shift[:, bass.ds(2 * it + w, 1)], ALU.mult, ALU.add).then_inc(s["xn"], 1)
                    for w in ws:
                        wait(net, dve, s["mm"], 2 * it + w + 1)
                        dve.scalar_tensor_tensor(b["top"][:, :], KEYS[w][:, 0:D], b["pen"][:, bass.ds(2 * it + w, 1)], b["top"][:, :],
                                                 ALU.add, ALU.max).then_inc(s["k_used"], 1)
                        dve.drain()

                with dve.Fori(0, TILES // 2) as it:
                    tiles(it, (0, 1))
                tiles(TILES // 2, (0,))
                dve.sem_inc(s["top"], 1)
                dve.wait_ge(s["top_tr"], 1)
                dve.tensor_reduce(b["col"][:, :], p_top[:, 0:D].rearrange("p (a b) -> p a b", a=2), AX.X, ALU.max)
                dve.drain()
                for i in range(2):
                    ins = dve.tensor_scalar(b["diag"][:, i, :], net.const("ident"), b["col"][:, i:i + 1], None, ALU.mult)
                ins.then_inc(s["diag"], 1)
                dve.wait_ge(s["top_row"], 1)
                dve.tensor_copy(net.key_top[:, :], TR[0][:, 0:D])

            @block.scalar
            def _(act):
                def tiles(it, ws):
                    for w in ws:
                        wait(net, act, s["tr"], 2 * it + w + 1)
                        act.activation(rows(bw[w]["xnT"][:, :, :]), TR[w][:, 0:D], ACT.Copy).then_inc(s["xnT"], 1)
                    for w in ws:
                        take_table(net, act, s, bw[w], TAB[w], tab_out[w], it, w)

                for w in range(2):
                    act.sem_inc(tab_out[w], 1)
                with act.Fori(0, TILES // 2) as it:
                    tiles(it, (0, 1))
                tiles(TILES // 2, (0,))
                act.sem_inc(s["end"], 1)

            @block.tensor
            def _(pe):
                pe.wait_ge(s["w_in"], 80)
                for i in range(2):
                    ins = products(pe, TAB[0][:, 8 * i:8 * i + 8], [(b["wT"][:, k, i * P:(i + 1) * P], b["al"][:, k, :]) for k in range(2)])
                ins.then_inc(s["fold_ps"], 1)
                pe.wait_ge(s["folded"], 1)

                def tiles(it, ws):
                    n = lambda w: 2 * it + w + 1
                    for w in ws:
                        wait(net, pe, s["xn"], n(w))
                        turned(pe, net, TR[w], bw[w]["xn"], 2).then_inc(s["tr"], 1)
                    for w in ws:
                        xnT = bw[w]["xnT"]
                        wait(net, pe, s["xnT"], n(w))
                        wait(net, pe, s["tab_sb"], n(w))
                        products(pe, TAB[w][:, 0:264], [(xnT[:, k, :], b["w"][:, k, :]) for k in range(2)])
                        wait(net, pe, s["k_used"], n(w))
                        products(pe, KEYS[w][:, 0:D], [(xnT[:, k, :], b["wkv"][:, k, 0:D]) for k in range(2)] +
                                 [(net.const("ones")[0:1, :], b["bkv"][0:1, 0:D])]).then_inc(s["mm"], 1)

                pe.sem_inc(s["tab_sb"], 2)
                pe.sem_inc(s["k_used"], 2)
                with pe.Fori(0, TILES // 2) as it:
                    tiles(it, (0, 1))
                tiles(TILES // 2, (0,))
                pe.wait_ge(s["top"], 1)
                turned(pe, net, p_top, b["top"], 2).then_inc(s["top_tr"], 1)
                pe.wait_ge(s["diag"], 1)
                pe.matmul(TR[0][:, 0:D], net.const("ones"), rows(b["diag"][:, :, :]), start=True, stop=True).then_inc(s["top_row"], 1)


def lambda_stage(nc, net):
    with ExitStack() as c:
        b = buffers(nc, c, "lam", wkv=[2, 512], bkv=[512], cols=[2, 3], acc=[2, D + 4],
                    sum=[2], six=[2, 6], mv=[2, 2], var=[2], rs=[2])
        bw = pair_buffers(nc, c, "lam_t", net.edge, xn=[D], xnT=[2, P], kx=[D], v=[D + 4])
        TR, KV, SUM0, SUM1 = ([net.PS[4 * w + i] for w in range(2)] for i in range(4))
        names = ["w_in", "xn", "tr", "xnT", "mm", "kx", "kexp", "kv_ready", "lam_mm", "var_ready", "rstd_ready"]
        with stage(nc, "lam", names) as (block, s):
            @block.sync
            def _(sp):
                for dst, src in ((b["wkv"][:, :, :], weight(net.inp["m1_wkv"])), (b["bkv"][0:1, :], net.inp["m1_bkv"]),
                                 (rows(b["cols"][:, :, :]), net.inp["m1_cols"])):
                    sp.dma_start(dst, src).then_inc(s["w_in"], 16)

            @block.vector
            def _(dve):
                dve.memset(b["acc"][:, :, :], 0.0)
                for w in range(2):
                    dve.memset(bw[w]["v"][:, D:D + 1], 1.0)
                dve.wait_ge(s["w_in"], 48)

                def tiles(it, ws):
                    n = lambda w: 2 * it + w + 1
                    for w in ws:
                        dve.tensor_scalar(bw[w]["xn"][:, :], rows(net.X[:, bass.ds(2 * it + w, 1), :]), net.rstd[:, bass.ds(2 * it + w, 1)],
                                          net.shift[:, bass.ds(2 * it + w, 1)], ALU.mult, ALU.add).then_inc(s["xn"], 1)
                    for w in ws:
                        wait(net, dve, s["mm"], n(w))
                        dve.tensor_tensor(bw[w]["kx"][:, :], KV[w][:, 0:D], net.key_top[:, :], ALU.subtract).then_inc(s["kx"], 1)
                    for w in ws:
                        dve.tensor_copy(bw[w]["v"][:, 0:D], KV[w][:, D:2 * D])
                    for w in ws:
                        wait(net, dve, s["kexp"], n(w))
                        dve.tensor_scalar(bw[w]["kx"][:, :], bw[w]["kx"][:, :], net.const("valid")[:, bass.ds(2 * it + w, 1)], None, ALU.mult).then_inc(s["kv_ready"], 1)
                    for w in ws:
                        wait(net, dve, s["lam_mm"], n(w))
                        for i, ps in enumerate((SUM0[w], SUM1[w])):
                            dve.tensor_tensor(b["acc"][:, i, 0:D + 1], b["acc"][:, i, 0:D + 1], ps[:, 0:D + 1], ALU.add)
                        dve.drain()

                with dve.Fori(0, TILES // 2) as it:
                    tiles(it, (0, 1))
                tiles(TILES // 2, (0,))
                for i in range(2):
                    dve.reciprocal(b["sum"][:, i:i + 1], b["acc"][:, i, D:D + 1])
                    dve.drain()
                    dve.tensor_scalar(b["acc"][:, i, 0:D], b["acc"][:, i, 0:D], b["sum"][:, i:i + 1], None, ALU.mult)
                    dve.drain()
                    dve.bn_stats(b["six"][:, i, :], b["acc"][:, i, 0:D])
                    dve.drain()
                    dve.bn_aggr(b["mv"][:, i, :], b["six"][:, i, :])
                    dve.drain()
                dve.tensor_scalar(b["var"][:, :], b["mv"][:, :, 1], 1e-5, None, ALU.add).then_inc(s["var_ready"], 1)
                dve.wait_ge(s["rstd_ready"], 1)
                dve.tensor_tensor(b["rs"][:, :], b["rs"][:, :], b["cols"][:, :, 1], ALU.mult)
                dve.drain()
                for i in range(2):
                    dve.tensor_scalar(net.lam[:, i, :], b["acc"][:, i, 0:D], b["mv"][:, i, 0:1], b["rs"][:, i:i + 1], ALU.subtract, ALU.mult)
                dve.drain()
                for i in range(2):
                    dve.tensor_scalar(net.lam[:, i, :], net.lam[:, i, :], b["cols"][:, i, 2:3], None, ALU.add)

            @block.gpsimd
            def _(pool):
                pool.wait_ge(s["var_ready"], 1)
                pool.tensor_tensor(b["rs"][:, :], b["var"][:, :], net.const("mhalf").to_broadcast([P, 2]), ALU.pow).then_inc(s["rstd_ready"], 1)

            @block.scalar
            def _(act):
                def tiles(it, ws):
                    n = lambda w: 2 * it + w + 1
                    for w in ws:
                        wait(net, act, s["tr"], n(w))
                        act.activation(rows(bw[w]["xnT"][:, :, :]), TR[w][:, 0:D], ACT.Copy).then_inc(s["xnT"], 1)
                    for w in ws:
                        wait(net, act, s["kx"], n(w))
                        act.activation(bw[w]["kx"][:, :], bw[w]["kx"][:, :], ACT.Exp).then_inc(s["kexp"], 1)

                with act.Fori(0, TILES // 2) as it:
                    tiles(it, (0, 1))
                tiles(TILES // 2, (0,))

            @block.tensor
            def _(pe):
                def tiles(it, ws):
                    n = lambda w: 2 * it + w + 1
                    for w in ws:
                        wait(net, pe, s["xn"], n(w))
                        turned(pe, net, TR[w], bw[w]["xn"], 2).then_inc(s["tr"], 1)
                    for w in ws:
                        wait(net, pe, s["xnT"], n(w))
                        products(pe, KV[w][:, :], [(bw[w]["xnT"][:, k, :], b["wkv"][:, k, :]) for k in range(2)] +
                                 [(net.const("ones")[0:1, :], b["bkv"][0:1, :])]).then_inc(s["mm"], 1)
                    for w in ws:
                        wait(net, pe, s["kv_ready"], n(w))
                        for i, ps in enumerate((SUM0[w], SUM1[w])):
                            ins = pe.matmul(ps[:, 0:D + 1], bw[w]["kx"][:, i * P:(i + 1) * P], bw[w]["v"][:, 0:D + 1], start=True, stop=True)
                        ins.then_inc(s["lam_mm"], 1)

                pe.wait_ge(s["w_in"], 48)
                with pe.Fori(0, TILES // 2) as it:
                    tiles(it, (0, 1))
                tiles(TILES // 2, (0,))


def rank_work(nc, net, c, block, s, b):
    flat = net.agg[:, :, :].rearrange("p a b -> p (a b)")
    row, sink = flat[:, 0:NPAD], flat[:, NPAD:NPAD + NPAD // 2]
    d = buffers(nc, c, "rank", key=[TILES], noise=[TILES], part=[4, TILES], far=[TILES])

    @block.sync
    def _(sp):
        sp.wait_ge(s["noise_clear"], 1)
        with nc.allow_non_contiguous_dma("one number a node"):
            sp.dma_start(d["noise"][:, 0:TILES - 1], net.inp["noise"][:, 0:(TILES - 1) * P].rearrange("o (t p) -> p (o t)", p=P)).then_inc(s["noise_in"], 16)
            sp.dma_start(d["noise"][0:LAST, TILES - 1:TILES], net.inp["noise"][:, (TILES - 1) * P:N].rearrange("o (t p) -> p (o t)", p=LAST)).then_inc(s["noise_in"], 16)
            sp.wait_ge(s["keys_ready"], 1)
            sp.dma_start(net.keys.rearrange("o (t p) -> p (o t)", p=P), d["key"][:, :]).then_inc(s["keys_out"], 16)
        sp.wait_ge(s["keys_out"], 16)
        sp.dma_start(row, net.keys.to_broadcast([P, NPAD])).then_inc(s["keys_in"], 16)

    @block.vector
    def _(dve):
        dve.memset(d["noise"][:, :], 0.0).then_inc(s["noise_clear"], 1)
        dve.memset(d["part"][:, :, :], 0.0)
        dve.wait_ge(s["noise_in"], 32)
        dve.tensor_tensor(d["key"][:, :], net.src_degree[:, :], d["noise"][:, :], ALU.add)
        dve.drain()
        dve.tensor_tensor(d["key"][:, :], d["key"][:, :], net.const("valid"), ALU.mult)
        dve.tensor_scalar(d["far"][:, :], net.const("valid"), -BIG, BIG, ALU.mult, ALU.add)
        dve.drain()
        dve.tensor_tensor(d["key"][:, :], d["key"][:, :], d["far"][:, :], ALU.add).then_inc(s["keys_ready"], 1)
        dve.wait_ge(s["keys_in"], 16)
        half = NPAD // 2

        def count(t, k, lo, hi, op):
            for a in range(lo, hi, half):
                z = min(hi, a + half)
                kk = k + (a > lo)
                dve.tensor_scalar(sink[:, 0:z - a], row[:, a:z], d["key"][:, t:t + 1], None, op, ALU.add, accum_out=d["part"][:, kk, t:t + 1])
                dve.drain()

        for t in range(TILES):
            lo, hi = t * P, (t + 1) * P
            count(t, 0, 0, lo, ALU.is_le)
            for k, (first, last) in enumerate(((lo, NPAD),)):
                for a in range(first, last, half):
                    z = min(last, a + half)
                    dve.tensor_scalar(sink[:, 0:z - a], row[:, a:z], d["key"][:, t:t + 1], None, ALU.is_lt, ALU.add,
                                      accum_out=d["far"][:, t:t + 1])
                    dve.drain()
                    dve.tensor_tensor(d["part"][:, 2, t:t + 1], d["part"][:, 2, t:t + 1], d["far"][:, t:t + 1], ALU.add)
                    dve.drain()
            dve.scalar_tensor_tensor(sink[:, 0:P], row[:, lo:hi], d["key"][:, t:t + 1], net.const("lower"), ALU.is_equal, ALU.mult,
                                     accum_out=d["part"][:, 3, t:t + 1])
            dve.drain()
        for k in range(1, 4):
            dve.tensor_tensor(d["part"][:, 0, :], d["part"][:, 0, :], d["part"][:, k, :], ALU.add)
            dve.drain()
        dve.tensor_copy(net.rank[:, :], d["part"][:, 0, :])


def sort_stage(nc, net):
    R = 4
    with ExitStack() as c:
        b = buffers(nc, c, "sort", xn=[R, D])
        with stage(nc, "sort", ["xn", "gp_out0", "gp_out1", "gp_out2", "gp_out3"]) as (block, s):
            out = (s["gp_out0"], s["gp_out1"], s["gp_out2"], s["gp_out3"])

            @block.vector
            def _(dve):
                for t in range(TILES):
                    if t >= R:
                        dve.wait_ge(out[t % R], 16 * (t // R))
                    dve.tensor_scalar(b["xn"][:, t % R, :], net.X[:, t, :], net.rstd[:, t:t + 1], net.shift[:, t:t + 1],
                                      ALU.mult, ALU.add).then_inc(s["xn"], 1)

            @block.gpsimd
            def _(pool):
                for t in range(TILES):
                    pool.wait_ge(s["xn"], t + 1)
                    pool.indirect_dma_start(net.sorted_x, bass.IndirectOffsetOnAxis(ap=net.rank[:, t:t + 1], axis=0),
                                            b["xn"][:, t % R, :], None).then_inc(out[t % R], 16)
                for r in range(R):
                    pool.wait_ge(out[r], 16 * len(range(r, TILES, R)))


CHUNK = 448
PART = 112
CHUNKS = NPAD // CHUNK
STATES = 16
LOG1P = [2.0000000078777487, 0.6666631593508171, 0.4002485372345264, 0.2796141883488086, 0.28174657263251685]


def mamba_stage(nc, net):
    SET, SLOTS = 16, 2
    spare = rows(net.agg[:, :, :])
    with ExitStack() as c:
        b = buffers(nc, c, "mamba", w_in=[2, 512], w_x=[2, 48], w_dt=[D], w_out=[2, D], cols=[2, 23], neg=[2, STATES],
                    xsT=[2, CHUNK], raw=[2, CHUNK + 4], xc=[2, CHUNK], dbc=[CHUNK], dt=[2, CHUNK],
                    dtx=[2, CHUNK], dA=[2, 2, CHUNK], dB=[2, CHUNK], h=[2, 2, CHUNK], state=[2, STATES],
                    idx_src_i=[EROW], idx_i=[SLOTS, SET], land=[SLOTS, SET, H])
        A2 = rows
        tmp = [spare[:, i * 2 * CHUNK:(i + 1) * 2 * CHUNK] for i in range(5)]
        hc = spare[:, 10 * CHUNK:14 * CHUNK].rearrange("p (q i c) -> p q i c", q=2, i=2)
        at = 14 * CHUNK
        yo = spare[:, at:at + 4 * D].rearrange("p (a d) -> p a d", a=4)
        b["xs"] = spare[:, at + 4 * D:at + 8 * D].rearrange("p (a d) -> p a d", a=4)
        at += 8 * D
        b["z"] = spare[:, at:at + 2 * CHUNK].rearrange("p (a d) -> p a d", a=2)
        src_i = spare[:, at + 2 * CHUNK:at + 2 * CHUNK + EROW].bitcast(I32)
        B = net.PS
        names = ["w", "xs_in", "tr", "xsT", "in_mm", "raw", "conv", "silu", "x_mm", "dbc", "dt_mm", "sp_in", "sp_e", "dt_ready",
                 "bc", "dA", "dB", "h_ready", "hc", "y_mm", "yz", "out_mm", "yo", "y_out", "z_ready", "neg", "halo", "edges_in", "clipped", "copied"] + \
                [f"gp_landed{q}" for q in range(SLOTS)]
        with stage(nc, "mamba", names) as (block, s):
            landed = (s["gp_landed0"], s["gp_landed1"])

            @block.sync
            def _(sp):
                i = net.inp
                sp.dma_start(src_i, net.src_pad.rearrange("t e -> (t e)").rearrange("(p g) -> p g", p=P)).then_inc(s["edges_in"], 16)
                for dst, src in ((b["w_in"][:, :, :], weight(i["s_in"])), (b["w_x"][:, :, :], weight(i["s_x"])), (b["w_dt"][0:16, :], i["s_dt"]),
                                 (b["w_out"][:, :, :], weight(i["s_out"])), (A2(b["cols"][:, :, :]), i["s_cols"])):
                    sp.dma_start(dst, src).then_inc(s["w"], 16)
                sp.sem_inc(s["tr"], 1)
                with sp.Fori(0, CHUNKS) as j:
                    wait(net, sp, s["tr"], j + 1)
                    sp.dma_start(b["xs"][0:PART, :, :], net.sorted_x[bass.ds(j * CHUNK, CHUNK), :].rearrange("(a p) d -> p a d", p=PART)).then_inc(s["xs_in"], 16)
                    wait(net, sp, s["yo"], j + 1)
                    sp.dma_start(net.mamba_y[bass.ds(j * CHUNK, CHUNK), :].rearrange("(a p) d -> p a d", p=PART), yo[0:PART, :, :]).then_inc(s["y_out"], 16)
                sp.wait_ge(s["y_out"], 16 * CHUNKS + 1)

            @block.gpsimd
            def _(pool):
                pool.wait_ge(s["edges_in"], 16)
                pool.tensor_scalar(b["idx_src_i"][:, :], src_i, 0, None, ALU.max).then_inc(s["clipped"], 1)
                pool.wait_ge(s["clipped"], 1)
                def indices(it, q):
                    pool.tensor_copy(b["idx_i"][:, q, :], b["idx_src_i"][:, bass.ds((it * SLOTS + q) * SET, SET)]).then_inc(s["copied"], 1)

                def fetch(q):
                    for r in range(SET):
                        pool.indirect_dma_start(b["land"][:, q, r, :], None, net.src_tab,
                                                bass.IndirectOffsetOnAxis(ap=b["idx_i"][:, q, r:r + 1], axis=0)).then_inc(landed[q], 16)

                def empty(it, q):
                    wait_apart(net, pool, landed[q], (it + 1) * 16 * SET)
                    pool.tensor_copy(net.edge[:, bass.ds((it * SLOTS + q) * SET * H, SET * H)], rows(b["land"][:, q, :, :])).then_inc(s["copied"], 1)

                rounds = EROW // (SLOTS * SET)
                for q in range(SLOTS):
                    indices(0, q)
                    wait_apart(net, pool, s["copied"], q + 1)
                    fetch(q)
                with pool.Fori(0, rounds - 1) as it:
                    for q in range(SLOTS):
                        empty(it, q)
                        indices(it + 1, q)
                        wait_apart(net, pool, s["copied"], SLOTS + 2 * (it * SLOTS + q + 1))
                        fetch(q)
                for q in range(SLOTS):
                    empty(rounds - 1, q)

            @block.scalar
            def _(act):
                act.wait_ge(s["w"], 80)
                for i in range(2):
                    ins = act.activation(b["neg"][:, i, :], b["cols"][:, i, 7:23], ACT.Exp)
                ins.then_inc(s["neg"], 1)
                act.wait_ge(s["neg"], 2)
                act.sem_inc(s["y_out"], 1)
                with act.Fori(0, CHUNKS) as j:
                    wait(net, act, s["tr"], j + 2)
                    for i in range(2):
                        ins = act.activation(b["xsT"][:, i, :], B[i][:, 0:CHUNK], ACT.Copy)
                    ins.then_inc(s["xsT"], 1)
                    wait(net, act, s["in_mm"], j + 1)
                    wait(net, act, s["halo"], j + 1)
                    for i in range(2):
                        ins = act.activation(b["raw"][:, i, 3:3 + CHUNK], B[2 + i][:, 0:CHUNK], ACT.Copy)
                    ins.then_inc(s["raw"], 1)
                    for i in range(2):
                        ins = act.activation(b["z"][:, i, :], B[4 + i][:, 0:CHUNK], ACT.Silu)
                    ins.then_inc(s["z_ready"], 1)
                    wait(net, act, s["conv"], j + 1)
                    for i in range(2):
                        ins = act.activation(b["xc"][:, i, :], tmp[0][:, i * CHUNK:(i + 1) * CHUNK], ACT.Silu, bias=b["cols"][:, i, 4:5])
                    ins.then_inc(s["silu"], 1)
                    wait(net, act, s["x_mm"], j + 1)
                    act.activation(b["dbc"][0:48, :], B[6][0:48, 0:CHUNK], ACT.Copy).then_inc(s["dbc"], 1)
                    wait(net, act, s["sp_in"], j + 1)
                    for i in range(2):
                        ins = act.activation(tmp[2][:, i * CHUNK:(i + 1) * CHUNK], tmp[1][:, i * CHUNK:(i + 1) * CHUNK], ACT.Exp, bias=b["cols"][:, i, 5:6])
                    ins.then_inc(s["sp_e"], 1)
                    wait(net, act, s["dt_ready"], j + 1)
                    for k in range(STATES):
                        wait(net, act, s["h_ready"], j * STATES + k - 1) if k >= 2 else None
                        for i in range(2):
                            ins = act.activation(b["dA"][:, k % 2, i, :], b["dt"][:, i, :], ACT.Exp, scale=b["neg"][:, i, k:k + 1])
                        ins.then_inc(s["dA"], 1)
                    wait(net, act, s["out_mm"], j + 1)
                    wait(net, act, s["y_out"], 16 * j + 1)
                    for a in range(4):
                        ins = act.activation(yo[0:PART, a, :], B[2 + a][0:PART, 0:D], ACT.Copy)
                    ins.then_inc(s["yo"], 1)

            @block.vector
            def _(dve):
                both = lambda ps: ps[:, 0:CHUNK].unsqueeze(1).to_broadcast([P, 2, CHUNK])
                dve.memset(b["state"][:, :, :], 0.0)
                dve.memset(b["raw"][:, :, CHUNK:CHUNK + 3], 0.0)
                dve.wait_ge(s["neg"], 1)
                dve.tensor_scalar(A2(b["neg"][:, :, :]), A2(b["neg"][:, :, :]), -1.0, None, ALU.mult).then_inc(s["neg"], 1)
                with dve.Fori(0, CHUNKS) as j:
                    dve.drain()
                    for i in range(2):
                        ins = dve.tensor_copy(b["raw"][:, i, 0:3], b["raw"][:, i, CHUNK:CHUNK + 3])
                    ins.then_inc(s["halo"], 1)
                    wait(net, dve, s["raw"], j + 1)
                    for i in range(2):
                        u = tmp[0][:, i * CHUNK:(i + 1) * CHUNK]
                        for k in range(4):
                            tap, x = b["cols"][:, i, k:k + 1], b["raw"][:, i, k:k + CHUNK]
                            if k == 0:
                                ins = dve.tensor_scalar(u, x, tap, None, ALU.mult)
                            else:
                                dve.drain()
                                ins = dve.scalar_tensor_tensor(u, x, tap, u, ALU.mult, ALU.add)
                    ins.then_inc(s["conv"], 1)
                    wait(net, dve, s["dt_mm"], j + 1)
                    for i in range(2):
                        v, bias = B[2 + i][:, 0:CHUNK], b["cols"][:, i, 5:6]
                        dve.tensor_scalar(b["dt"][:, i, :], v, bias, 0.0, ALU.add, ALU.max)
                        dve.drain()
                        ins = dve.scalar_tensor_tensor(tmp[1][:, i * CHUNK:(i + 1) * CHUNK], b["dt"][:, i, :], -2.0, v, ALU.mult, ALU.add)
                    ins.then_inc(s["sp_in"], 1)
                    wait(net, dve, s["sp_e"], j + 1)
                    e, den, q, s2 = tmp[2], tmp[3], tmp[4], tmp[1]
                    dve.tensor_scalar(den, e, 2.0, None, ALU.add)
                    dve.drain()
                    dve.reciprocal(den, den)
                    dve.drain()
                    dve.tensor_tensor(e, e, den, ALU.mult)
                    dve.drain()
                    dve.tensor_tensor(s2, e, e, ALU.mult)
                    dve.drain()
                    dve.tensor_scalar(q, s2, LOG1P[-1], None, ALU.mult)
                    dve.drain()
                    for coeff in LOG1P[-2:0:-1]:
                        dve.scalar_tensor_tensor(q, q, coeff, s2, ALU.add, ALU.mult)
                        dve.drain()
                    dve.scalar_tensor_tensor(q, q, LOG1P[0], e, ALU.add, ALU.mult)
                    dve.drain()
                    dve.tensor_tensor(A2(b["dt"][:, :, :]), A2(b["dt"][:, :, :]), q, ALU.add).then_inc(s["dt_ready"], 1)
                    dve.drain()
                    wait(net, dve, s["silu"], j + 1)
                    dve.tensor_tensor(A2(b["dtx"][:, :, :]), A2(b["dt"][:, :, :]), A2(b["xc"][:, :, :]), ALU.mult)
                    dve.drain()
                    for k in range(STATES):
                        g = j * STATES + k + 1
                        wait(net, dve, s["bc"], g)
                        dve.tensor_tensor(b["dB"][:, :, :], b["dtx"][:, :, :], both(B[6 - 2 * (k % 2)]), ALU.mult)
                        dve.drain()
                        wait(net, dve, s["dA"], g)
                        for i in range(2):
                            ins = dve.tensor_tensor_scan(b["h"][:, k % 2, i, :], b["dA"][:, k % 2, i, :], b["dB"][:, i, :], b["state"][:, i, k:k + 1], ALU.mult, ALU.add)
                        ins.then_inc(s["h_ready"], 1)
                        dve.drain()
                        dve.tensor_copy(b["state"][:, :, k], b["h"][:, k % 2, :, CHUNK - 1])
                        if k >= 2:
                            wait(net, dve, s["y_mm"], g - 2)
                        dve.tensor_tensor(hc[:, k % 2, :, :], b["h"][:, k % 2, :, :], both(B[7 - 2 * (k % 2)]), ALU.mult).then_inc(s["hc"], 1)
                    wait(net, dve, s["y_mm"], (j + 1) * STATES)
                    wait(net, dve, s["z_ready"], j + 1)
                    for i in range(2):
                        dve.scalar_tensor_tensor(b["dtx"][:, i, :], b["xc"][:, i, :], b["cols"][:, i, 6:7], B[i][:, 0:CHUNK], ALU.mult, ALU.add)
                    dve.drain()
                    dve.tensor_tensor(A2(b["dtx"][:, :, :]), A2(b["dtx"][:, :, :]), A2(b["z"][:, :, :]), ALU.mult).then_inc(s["yz"], 1)

            @block.tensor
            def _(pe):
                pe.wait_ge(s["w"], 80)

                def add_state(g, k):
                    wait(net, pe, s["hc"], g)
                    for i in range(2):
                        ins = pe.matmul(B[i][:, 0:CHUNK], net.const("ident"), hc[:, k % 2, i, :], start=(k == 0), stop=(k == STATES - 1))
                    ins.then_inc(s["y_mm"], 1)

                with pe.Fori(0, CHUNKS) as j:
                    wait(net, pe, s["xs_in"], 16 * j + 16)
                    for a in range(4):
                        for i in range(2):
                            ins = pe.transpose(B[i][:, a * PART:(a + 1) * PART], b["xs"][0:PART, a, i * P:(i + 1) * P], net.const("ident")[0:PART, 0:PART])
                    ins.then_inc(s["tr"], 1)
                    wait(net, pe, s["xsT"], j + 1)
                    for m in range(4):
                        ins = products(pe, B[2 + m][:, 0:CHUNK], [(b["w_in"][:, k, m * P:(m + 1) * P], b["xsT"][:, k, :]) for k in range(2)])
                    ins.then_inc(s["in_mm"], 1)
                    wait(net, pe, s["silu"], j + 1)
                    products(pe, B[6][0:48, 0:CHUNK], [(b["w_x"][:, k, :], b["xc"][:, k, :]) for k in range(2)]).then_inc(s["x_mm"], 1)
                    wait(net, pe, s["dbc"], j + 1)
                    for i in range(2):
                        ins = products(pe, B[2 + i][:, 0:CHUNK], [(b["w_dt"][0:16, i * P:(i + 1) * P], b["dbc"][0:16, :])])
                    ins.then_inc(s["dt_mm"], 1)
                    for k in range(STATES):
                        g = j * STATES + k + 1
                        if k >= 2:
                            wait(net, pe, s["hc"], g - 2)
                        for row, bank in ((16 + k, B[6 - 2 * (k % 2)]), (32 + k, B[7 - 2 * (k % 2)])):
                            ins = pe.matmul(bank[:, 0:CHUNK], net.const("ident")[0:48, row:row + 1].to_broadcast([48, P]), b["dbc"][0:48, :], start=True, stop=True)
                        ins.then_inc(s["bc"], 1)
                        if k:
                            add_state(g - 1, k - 1)
                    add_state((j + 1) * STATES, STATES - 1)
                    wait(net, pe, s["yz"], j + 1)
                    for a in range(4):
                        ins = products(pe, B[2 + a][0:PART, 0:D], [(b["dtx"][:, k, a * PART:(a + 1) * PART], b["w_out"][:, k, :]) for k in range(2)])
                    ins.then_inc(s["out_mm"], 1)


def guard_stage(nc, net):
    m, g = (a[:, :, :].rearrange("p a b -> p (a b)") for a in (net.node_max, net.guard))
    with ExitStack() as c:
        b = buffers(nc, c, "guard", has=[TILES], far=[TILES], masked=[TILES, H], top=[1], turn=[P], all=[1])
        with stage(nc, "guard", ["top", "row", "all", "ps", "diff", "exp"]) as (block, s):
            @block.vector
            def _(dve):
                dve.tensor_scalar(b["has"][:, :], net.degree[:, :], 0.0, None, ALU.is_gt)
                dve.drain()
                dve.tensor_scalar(b["far"][:, :], b["has"][:, :], BIG, BIG, ALU.mult, ALU.subtract)
                dve.drain()
                dve.tensor_tensor(b["masked"][:, :, :], net.node_max[:, :, :], b["far"][:, :].unsqueeze(2).to_broadcast([P, TILES, H]), ALU.add)
                dve.drain()
                dve.tensor_reduce(b["top"][:, :], b["masked"][:, :, :], AX.XY, ALU.max)
                dve.drain()
                dve.tensor_scalar(b["turn"][:, :], net.const("ident"), b["top"][:, :], None, ALU.mult).then_inc(s["top"], 1)
                dve.wait_ge(s["row"], 1)
                dve.tensor_reduce(b["all"][:, :], net.PS[0][:, 0:P], AX.X, ALU.max)
                dve.drain()
                dve.tensor_scalar(g, m, b["all"][:, :], -1.0, ALU.subtract, ALU.mult)
                dve.drain()
                dve.tensor_scalar(g, g, 87.0, None, ALU.min).then_inc(s["diff"], 1)
                dve.wait_ge(s["exp"], 1)
                dve.tensor_scalar(g, g, 1e-16, None, ALU.mult)

            @block.tensor
            def _(pe):
                pe.wait_ge(s["top"], 1)
                pe.matmul(net.PS[0][:, 0:P], net.const("ones"), b["turn"][:, :], start=True, stop=True).then_inc(s["row"], 1)

            @block.scalar
            def _(act):
                act.wait_ge(s["diff"], 1)
                act.activation(g, g, ACT.Exp).then_inc(s["exp"], 1)


def final_stage(nc, net):
    with ExitStack() as c:
        b = buffers(nc, c, "fin", rows=[8, D], gates=[4, D], ff1=[2, 512], ff1b=[4], ff2=[4, D], wq=[2, D], cols=[2, 3], idx_i=[2])
        bw = pair_buffers(nc, c, "fin_t", net.edge, xn=[D], xnT=[2, P], den=[H], v=[D], ex=[D], pair=[2, D], pT=[4, P], g=[D], h=[D],
                          hT=[2, P], fT=[4, P], qT=[2, P], y=[D], base=[D], ysum=[D], **SMALL)
        TURN, MIX, GATE, FF = ([net.PS[4 * w + i] for w in range(2)] for i in range(4))
        names = ["w_in", "loaded", "xn", "tr", "xnT", "q", "qT", "mix", "mix_used", "e_in", "e_out", "idx", "base", "y_sum", "pair", "tr_p", "pT", "gate",
                 "g_in", "g_out", "h", "tr_h", "hT", "f1", "f1r", "f2", "var_ready", "rstd_ready", "gp_y0", "gp_y1"]
        with stage(nc, "fin", names) as (block, s):
            GAT_B, LOC_G, LOC_B, GLO_G, GLO_B, LN2_G, LN2_B, FF2_B = range(8)
            y_in = (s["gp_y0"], s["gp_y1"])

            @block.sync
            def _(sp):
                i = net.inp
                loads = [(rows(b["rows"][:, :, :]), i["g1_rows"].to_broadcast([P, 8 * D])), (b["gates"][:, :, :], weight(i["g1_gates"])),
                         (b["ff1"][:, :, :], weight(i["g1_ff1"])), (b["ff1b"][:, :], i["g1_ff1b"]), (b["ff2"][:, :, :], weight(i["g1_ff2"])),
                         (b["wq"][:, :, :], weight(i["m1_wq"])), (rows(b["cols"][:, :, :]), i["m1_cols"])]
                for dst, src in loads:
                    sp.dma_start(dst, src).then_inc(s["w_in"], 16)
                sp.wait_ge(s["w_in"], 16 * len(loads))
                sp.sem_inc(s["loaded"], 1)

            @block.gpsimd
            def _(pool):
                pool.wait_ge(s["loaded"], 1)
                pool.sem_inc(s["y_sum"], 2)

                def tiles(it, ws):
                    for w in ws:
                        wait_apart(net, pool, s["xn"], 2 * it + w + 1)
                        pool.tensor_tensor(bw[w]["base"][:, :], bw[w]["xn"][:, :], b["rows"][:, GAT_B, :], ALU.add).then_inc(s["base"], 1)
                    for w in ws:
                        wait_apart(net, pool, s["y_sum"], 2 * it + w + 1)
                        pool.tensor_copy(b["idx_i"][:, w:w + 1], net.rank[:, bass.ds(2 * it + w, 1)]).then_inc(s["idx"], 1)
                        wait_apart(net, pool, s["idx"], 2 * it + w + 1)
                        pool.indirect_dma_start(bw[w]["y"][:, :], None, net.mamba_y,
                                                bass.IndirectOffsetOnAxis(ap=b["idx_i"][:, w:w + 1], axis=0)).then_inc(y_in[w], 16)
                    for w in ws:
                        wait_apart(net, pool, y_in[w], 16 * it + 16)
                        pool.tensor_tensor(bw[w]["ysum"][:, :], bw[w]["y"][:, :], bw[w]["xn"][:, :], ALU.add).then_inc(s["y_sum"], 1)
                    for k in range(3):
                        for w in ws:
                            norm_power(net, pool, s, bw[w], norm_value(it, ws, w, k))

                with pool.Fori(0, TILES // 2) as it:
                    tiles(it, (0, 1))
                tiles(TILES // 2, (0,))

            @block.tensor
            def _(pe):
                def tiles(it, ws):
                    n = lambda w: 2 * it + w + 1
                    for w in ws:
                        wait(net, pe, s["xn"], n(w))
                        turned(pe, net, TURN[w], bw[w]["xn"], 2).then_inc(s["tr"], 1)
                    for w in ws:
                        wait(net, pe, s["xnT"], n(w))
                        for i in range(2):
                            ins = products(pe, GATE[w][:, i * P:(i + 1) * P], [(b["wq"][:, k, i * P:(i + 1) * P], bw[w]["xnT"][:, k, :]) for k in range(2)])
                        ins.then_inc(s["q"], 1)
                    for w in ws:
                        wait(net, pe, s["qT"], n(w))
                        products(pe, MIX[w][:, 0:D], [(bw[w]["qT"][:, k, :], net.lam[:, k, :]) for k in range(2)]).then_inc(s["mix"], 1)
                    for w in ws:
                        wait(net, pe, s["pair"], n(w))
                        turned(pe, net, TURN[w], rows(bw[w]["pair"][:, :, :]), 4).then_inc(s["tr_p"], 1)
                    for w in ws:
                        wait(net, pe, s["pT"], n(w))
                        products(pe, GATE[w][:, 0:D], [(bw[w]["pT"][:, k, :], b["gates"][:, k, :]) for k in range(4)]).then_inc(s["gate"], 1)
                    for w in ws:
                        wait(net, pe, s["h"], n(w))
                        turned(pe, net, TURN[w], bw[w]["h"], 2).then_inc(s["tr_h"], 1)
                    for w in ws:
                        wait(net, pe, s["hT"], n(w))
                        for i in range(4):
                            ins = products(pe, FF[w][:, i * P:(i + 1) * P], [(b["ff1"][:, k, i * P:(i + 1) * P], bw[w]["hT"][:, k, :]) for k in range(2)])
                        ins.then_inc(s["f1"], 1)
                    for w in ws:
                        wait(net, pe, s["f1r"], n(w))
                        wait(net, pe, s["mix_used"], n(w))
                        products(pe, MIX[w][:, 0:D], [(bw[w]["fT"][:, k, :], b["ff2"][:, k, :]) for k in range(4)]).then_inc(s["f2"], 1)

                pe.wait_ge(s["loaded"], 1)
                with pe.Fori(0, TILES // 2) as it:
                    tiles(it, (0, 1))
                tiles(TILES // 2, (0,))

            @block.scalar
            def _(act):
                copy = lambda dst, src: act.activation(rows(dst), src, ACT.Copy)

                def tiles(it, ws):
                    n = lambda w: 2 * it + w + 1
                    for w in ws:
                        wait(net, act, s["tr"], n(w))
                        copy(bw[w]["xnT"][:, :, :], TURN[w][:, 0:D]).then_inc(s["xnT"], 1)
                    for w in ws:
                        wait(net, act, s["q"], n(w))
                        for i in range(2):
                            ins = act.activation(bw[w]["qT"][:, i, :], GATE[w][:, i * P:(i + 1) * P], ACT.Identity, bias=b["cols"][:, i, 0:1])
                        ins.then_inc(s["qT"], 1)
                    for w in ws:
                        wait(net, act, s["e_in"], n(w))
                        act.activation(bw[w]["ex"][:, :], bw[w]["ex"][:, :], ACT.Exp).then_inc(s["e_out"], 1)
                    for w in ws:
                        wait(net, act, s["tr_p"], n(w))
                        copy(bw[w]["pT"][:, :, :], TURN[w][:, :]).then_inc(s["pT"], 1)
                    for w in ws:
                        wait(net, act, s["g_in"], n(w))
                        act.activation(bw[w]["g"][:, :], bw[w]["g"][:, :], ACT.Exp, scale=-1.0).then_inc(s["g_out"], 1)
                    for w in ws:
                        wait(net, act, s["tr_h"], n(w))
                        copy(bw[w]["hT"][:, :, :], TURN[w][:, 0:D]).then_inc(s["hT"], 1)
                    for w in ws:
                        wait(net, act, s["f1"], n(w))
                        for i in range(4):
                            ins = act.activation(bw[w]["fT"][:, i, :], FF[w][:, i * P:(i + 1) * P], ACT.Relu, bias=b["ff1b"][:, i:i + 1])
                        ins.then_inc(s["f1r"], 1)

                act.wait_ge(s["loaded"], 1)
                with act.Fori(0, TILES // 2) as it:
                    tiles(it, (0, 1))
                tiles(TILES // 2, (0,))

            @block.vector
            def _(dve):
                heads = lambda a: a.rearrange("p (h d) -> p h d", h=H)
                row = lambda k: b["rows"][:, k, :]
                full = lambda w, k: bw[w][k][:, :]

                def each(ws, step):
                    for w in ws:
                        step(w)
                    dve.drain()

                def tiles(it, ws):
                    n = lambda w: 2 * it + w + 1
                    x = [rows(net.X[:, bass.ds(2 * it + w, 1), :]) for w in ws]
                    agg = [rows(net.agg[:, bass.ds(2 * it + w, 1), :]) for w in ws]
                    local, globe = ([bw[w]["pair"][:, i, :] for w in ws] for i in range(2))
                    for w in ws:
                        dve.tensor_scalar(full(w, "xn"), x[w], net.rstd[:, bass.ds(2 * it + w, 1)], net.shift[:, bass.ds(2 * it + w, 1)],
                                          ALU.mult, ALU.add).then_inc(s["xn"], 1)
                    each(ws, lambda w: dve.tensor_tensor(full(w, "den"), agg[w][:, D:D + H], rows(net.guard[:, bass.ds(2 * it + w, 1), :]), ALU.add))
                    each(ws, lambda w: dve.reciprocal(full(w, "den"), full(w, "den")))
                    each(ws, lambda w: dve.tensor_tensor(heads(full(w, "v")), heads(agg[w][:, 0:D]),
                                                         full(w, "den").unsqueeze(2).to_broadcast([P, H, 64]), ALU.mult))
                    for w in ws:
                        wait(net, dve, s["base"], n(w))
                        dve.tensor_tensor(full(w, "v"), full(w, "v"), full(w, "base"), ALU.add)
                    dve.drain()
                    for w in ws:
                        dve.tensor_scalar(full(w, "ex"), full(w, "v"), 0.0, None, ALU.min).then_inc(s["e_in"], 1)
                    for w in ws:
                        wait(net, dve, s["e_out"], n(w))
                        dve.tensor_scalar(full(w, "ex"), full(w, "ex"), 1.0, None, ALU.subtract)
                    dve.drain()
                    each(ws, lambda w: dve.scalar_tensor_tensor(full(w, "v"), full(w, "v"), 0.0, full(w, "ex"), ALU.max, ALU.add))
                    for w in ws:
                        norm_stats(dve, s, bw[w], full(w, "v"), local[w], row(LOC_G))
                    for w in ws:
                        norm_apply(net, dve, s, bw[w], local[w], local[w], norm_value(it, ws, w, 0), row(LOC_B))
                        wait(net, dve, s["y_sum"], n(w) + 2)
                        norm_stats(dve, s, bw[w], full(w, "ysum"), globe[w], row(GLO_G))
                    for w in ws:
                        norm_apply(net, dve, s, bw[w], globe[w], globe[w], norm_value(it, ws, w, 1), row(GLO_B)).then_inc(s["pair"], 1)
                    for w in ws:
                        wait(net, dve, s["mix"], n(w))
                        dve.tensor_tensor(x[w], x[w], MIX[w][:, 0:D], ALU.add).then_inc(s["mix_used"], 1)
                    dve.drain()
                    for w in ws:
                        dve.tensor_tensor(full(w, "v"), local[w], globe[w], ALU.subtract)
                    for w in ws:
                        wait(net, dve, s["gate"], n(w))
                        dve.tensor_scalar(full(w, "g"), GATE[w][:, 0:D], -87.0, None, ALU.max).then_inc(s["g_in"], 1)
                    for w in ws:
                        wait(net, dve, s["g_out"], n(w))
                        dve.tensor_scalar(full(w, "g"), full(w, "g"), 1.0, None, ALU.add)
                        dve.drain()
                        dve.reciprocal(full(w, "g"), full(w, "g"))
                        dve.drain()
                        dve.tensor_tensor(full(w, "v"), full(w, "v"), full(w, "g"), ALU.mult)
                        dve.drain()
                        dve.tensor_tensor(full(w, "h"), full(w, "v"), globe[w], ALU.add).then_inc(s["h"], 1)
                    dve.drain()
                    each(ws, lambda w: dve.tensor_tensor(full(w, "v"), full(w, "h"), row(FF2_B), ALU.add))
                    each(ws, lambda w: dve.tensor_tensor(x[w], x[w], row(LN2_B), ALU.add))
                    for w in ws:
                        wait(net, dve, s["f2"], n(w))
                        dve.tensor_tensor(full(w, "v"), full(w, "v"), MIX[w][:, 0:D], ALU.add)
                        dve.drain()
                        norm_stats(dve, s, bw[w], full(w, "v"), full(w, "g"), row(LN2_G))
                    for w in ws:
                        norm_apply(net, dve, s, bw[w], full(w, "g"), x[w], norm_value(it, ws, w, 2), x[w])
                    dve.drain()

                dve.wait_ge(s["loaded"], 1)
                with dve.Fori(0, TILES // 2) as it:
                    tiles(it, (0, 1))
                tiles(TILES // 2, (0,))


EXPERTS = 8


def expert_stage(nc, net):
    with ExitStack() as c:
        w1 = rows(net.agg[:, :, :])[:, 0:EXPERTS * 1024].rearrange("p (e k n) -> p e k n", e=EXPERTS, k=2)
        b = buffers(nc, c, "exp", gw=[2, EXPERTS], gb=[EXPERTS], b1=[32], b2=[D], w2=[EXPERTS, 4, D],
                    xn=[D], xnT=[2, D], hT=[2, 4, P], gt=[64], eq=[64], before=[64], sel=[EXPERTS], selT=[P], g=[EXPERTS])
        TURN, GATE, UP, DOWN, PICK, BIAS = net.PS[0], net.PS[1], net.PS[2:4], net.PS[4:6], net.PS[6], net.PS[7]
        names = ["w_in", "loaded", "xn", "tr", "xnT", "gl", "sel", "sel_tr", "selT", "bias", "h", "gelu", "y", "y_used", "acc", "stored"]
        with stage(nc, "exp", names) as (block, s):
            @block.sync
            def _(sp):
                i = net.inp
                loads = [(w1.rearrange("p e k n -> p (e k) n"), i["e_w1"].rearrange("(a p) n -> p a n", p=P)),
                         (b["w2"][:, :, :, :].rearrange("p e k n -> p (e k) n"), i["e_w2"].rearrange("(a p) n -> p a n", p=P)),
                         (b["gw"][:, :, :], weight(i["e_gw"])), (b["gb"][0:1, :], i["e_gb"]), (b["b1"][:, :], i["e_b1"]),
                         (b["b2"][0:EXPERTS, :], i["e_b2"])]
                for dst, src in loads:
                    sp.dma_start(dst, src).then_inc(s["w_in"], 16)
                sp.wait_ge(s["w_in"], 16 * len(loads))
                sp.sem_inc(s["loaded"], 1)
                with sp.Fori(0, TILES - 1) as t:
                    wait(net, sp, s["acc"], t + 1)
                    sp.dma_start(net.out[bass.ds(t * P, P), :], rows(net.X[:, bass.ds(t, 1), :])).then_inc(s["stored"], 16)
                sp.wait_ge(s["acc"], TILES)
                sp.dma_start(net.out[(TILES - 1) * P:N, :], net.X[0:LAST, TILES - 1, :]).then_inc(s["stored"], 16)
                sp.wait_ge(s["stored"], 16 * TILES)

            @block.tensor
            def _(pe):
                def turn(t):
                    wait(net, pe, s["xn"], t + 1)
                    turned(pe, net, TURN, b["xn"], 2).then_inc(s["tr"], 1)

                def tile(t, w, last):
                    xnT = lambda k: b["xnT"][:, w, k * P:(k + 1) * P]

                    def up(e):
                        wait(net, pe, s["gelu"], t * EXPERTS + e + 1)
                        for i in range(4):
                            ins = products(pe, UP[e % 2][:, i * P:(i + 1) * P], [(w1[:, e, k, i * P:(i + 1) * P], xnT(k)) for k in range(2)])
                        ins.then_inc(s["h"], 1)

                    def down(e):
                        wait(net, pe, s["gelu"], t * EXPERTS + e + 3)
                        wait(net, pe, s["y_used"], t * EXPERTS + e + 1)
                        products(pe, DOWN[e % 2][:, 0:D], [(b["hT"][:, e % 2, k, :], b["w2"][:, e, k, :]) for k in range(4)]).then_inc(s["y"], 1)

                    wait(net, pe, s["xnT"], t + 1)
                    products(pe, GATE[:, 0:EXPERTS], [(xnT(k), b["gw"][:, k, :]) for k in range(2)] +
                             [(net.const("ones")[0:1, :], b["gb"][0:1, :])]).then_inc(s["gl"], 1)
                    up(0)
                    for e in range(1, EXPERTS):
                        up(e)
                        down(e - 1)
                        if e == 3:
                            wait(net, pe, s["sel"], t + 1)
                            pe.transpose(PICK[0:EXPERTS, 0:P], b["sel"][:, :], net.const("ident")).then_inc(s["sel_tr"], 1)
                        if e == 5 and not last:
                            turn(t + 1)
                        if e == 6:
                            wait(net, pe, s["selT"], t + 1)
                            pe.matmul(BIAS[:, 0:D], b["selT"][0:EXPERTS, :], b["b2"][0:EXPERTS, :], start=True, stop=True).then_inc(s["bias"], 1)
                    down(EXPERTS - 1)

                pe.wait_ge(s["loaded"], 1)
                turn(0)
                with pe.Fori(0, TILES // 2) as it:
                    tile(2 * it, 0, False)
                    tile(2 * it + 1, 1, False)
                tile(TILES - 1, 0, True)

            @block.scalar
            def _(act):
                act.wait_ge(s["loaded"], 1)
                act.sem_inc(s["gelu"], 2)
                with act.Fori(0, TILES) as t:
                    for e in range(EXPERTS):
                        wait(net, act, s["h"], t * EXPERTS + e + 1)
                        wait(net, act, s["y"], t * EXPERTS + e + 1)
                        for i in range(4):
                            ins = act.activation(b["hT"][:, e % 2, i, :], UP[e % 2][:, i * P:(i + 1) * P], ACT.Gelu, bias=b["b1"][:, e * 4 + i:e * 4 + i + 1])
                        ins.then_inc(s["gelu"], 1)

            @block.vector
            def _(dve):
                def norm(t):
                    dve.tensor_scalar(b["xn"][:, :], rows(net.X[:, bass.ds(t, 1), :]), net.rstd[:, bass.ds(t, 1)], net.shift[:, bass.ds(t, 1)],
                                      ALU.mult, ALU.add).then_inc(s["xn"], 1)

                def take_turned(t, w):
                    wait(net, dve, s["tr"], t + 1)
                    dve.tensor_copy(b["xnT"][:, w, :], TURN[:, 0:D]).then_inc(s["xnT"], 1)

                def tile(t, w, last):
                    x = rows(net.X[:, bass.ds(t, 1), :])
                    wait(net, dve, s["gl"], t + 1)
                    dve.tensor_copy(b["g"][:, :], GATE[:, 0:EXPERTS])
                    dve.drain()
                    top_two(dve, net, EXPERTS, b["g"][:, :], b)
                    dve.sem_inc(s["sel"], 1)
                    for e in range(EXPERTS):
                        wait(net, dve, s["y"], t * EXPERTS + e + 3)
                        dve.scalar_tensor_tensor(x, DOWN[e % 2][:, 0:D], b["sel"][:, e:e + 1], x, ALU.mult, ALU.add).then_inc(s["y_used"], 1)
                        dve.drain()
                        if e == 3 and not last:
                            norm(t + 1)
                        if e == 4:
                            wait(net, dve, s["sel_tr"], t + 1)
                            dve.tensor_copy(b["selT"][0:EXPERTS, :], PICK[0:EXPERTS, 0:P]).then_inc(s["selT"], 1)
                        if e == 5 and not last:
                            take_turned(t + 1, 1 - w)
                    wait(net, dve, s["bias"], t + 1)
                    dve.tensor_tensor(x, x, BIAS[:, 0:D], ALU.add).then_inc(s["acc"], 1)

                make_before(dve, EXPERTS, b)
                dve.wait_ge(s["loaded"], 1)
                dve.sem_inc(s["y_used"], 2)
                dve.sem_inc(s["y"], 2)
                norm(0)
                take_turned(0, 0)
                with dve.Fori(0, TILES // 2) as it:
                    tile(2 * it, 0, False)
                    tile(2 * it + 1, 1, False)
                tile(TILES - 1, 0, True)


def build(nc, ins, out):
    net = Net()
    pool_sems[0] = POOL_SEM
    net.inp, net.out = ins, out
    dram = lambda name, shape, dt=F32: nc.dram_tensor(name, shape, dt, kind="Internal").ap()
    net.table = dram("table", (NPAD, D))
    net.src_tab = dram("src_tab", (NPAD, H))
    net.node_rec = dram("node_rec", (NPAD, 2 * H))
    net.src_pad = dram("src_pad", (ETILES, P), I32)
    net.dst_pad = dram("dst_pad", (ETILES, P), I32)
    net.run_max = dram("run_max", (EPAD, H))
    net.start_rec = dram("start_rec", (EPAD, 2 * H))
    net.weights = dram("weights", (ETILES, P * H))
    net.tile_row = dram("tile_row", (1, SPAD), I32)
    net.keys = dram("keys", (1, NPAD))
    net.sorted_x = dram("sorted_x", (NPAD, D))
    net.mamba_y = dram("mamba_y", (NPAD, D))
    with ExitStack() as c:
        net.tick = c.enter_context(nc.semaphore("tick"))
        sb = lambda name, shape, dt=F32: c.enter_context(nc.sbuf_tensor(name, shape, dt))
        net.PS = [c.enter_context(nc.psum_tensor(f"bank{i}", [P, 512], F32)) for i in range(8)]
        net.C = sb("consts", [P, CONST_N])
        net.const = lambda k: net.C[:, slice(*CONST_COLS[k])]
        net.X = sb("X", [P, TILES, D])
        net.zeros = sb("zeros", [P, 512])
        net.stat = sb("stat", [P, 8])
        net.rstd, net.shift = sb("rstd", [P, TILES]), sb("shift", [P, TILES])
        net.node_src, net.node_dst = sb("node_src", [P, TILES, H]), sb("node_dst", [P, TILES, H])
        net.node_max = sb("node_max", [P, TILES, H])
        net.kv, net.ksum = sb("kv", [P, 2, P]), sb("ksum", [P, 2, 4])
        net.starts, net.ends, net.degree = sb("starts", [P, TILES], I32), sb("ends", [P, TILES], I32), sb("degree", [P, TILES])
        net.src_degree = sb("src_degree", [P, TILES])
        net.agg = sb("agg", [P, TILES, D + H])
        net.step_src = sb("step_src", [P, SPAD], I32)
        net.step_et = sb("step_et", [P, SBLK], I32)
        net.step_dst = sb("step_dst", [P, SPAD])
        net.edge = sb("edge", [P, SPAD * H])
        net.key_top, net.lam, net.guard = sb("key_top", [P, D]), sb("lam", [P, 2, D]), sb("guard", [P, TILES, H])
        net.rank = sb("rank", [P, TILES], I32)
        stages = [load_stage,
                  lambda nc, net: norm_stage(nc, net, "norm0"),
                  project_stage, pad_edges_stage,
                  lambda nc, net: gather_stage(nc, net, "gather0", [degree_work, rank_work]), index_stage,
                  lambda nc, net: weight_stage(nc, net, "weight0", 0.01),
                  lambda nc, net: aggregate_stage(nc, net, "agg0"), combine_stage,
                  lambda nc, net: norm_stage(nc, net, "norm1"), project1_stage, lambda_stage,
                  sort_stage, mamba_stage,
                  lambda nc, net: weight_stage(nc, net, "weight1", 0.2), guard_stage,
                  lambda nc, net: aggregate_stage(nc, net, "agg1"), final_stage,
                  lambda nc, net: norm_stage(nc, net, "norm2"), expert_stage]
        for run in stages:
            run(nc, net)


def layout(i):
    f = {}
    a = lambda x: np.ascontiguousarray(np.asarray(x))

    def diagonal(src, dst):
        out = np.zeros((D, 8), np.float32)
        for h in range(H):
            out[h * 64:(h + 1) * 64, h] = np.asarray(src[h]).reshape(64)
            out[h * 64:(h + 1) * 64, 4 + h] = np.asarray(dst[h]).reshape(64)
        return out

    f["consts"] = constants()
    f["x"], f["src"], f["dst"] = a(i["x"]), a(i["src"]).reshape(1, E), a(i["dst"]).reshape(1, E)
    f["noise"] = a(i["node_vec"]).reshape(1, N)
    heads = lambda w: np.asarray(w).transpose(1, 0, 2).reshape(D, D)
    f["g0_w"] = a(heads(i["L0_gnn_W_fc"]))
    f["g0_wT"] = a(f["g0_w"].T)
    f["g0_al"] = diagonal(i["L0_gnn_W_ar"], i["L0_gnn_W_al"])
    f["g0_res"] = a(heads(i["L0_gnn_W_res"]))
    f["m0_wkv"] = a(np.concatenate([i["L0_mix_Wk"], i["L0_mix_Wv"]], 1))
    f["m0_wq"], f["m0_wm"], f["m0_w1"], f["m0_w2"] = (a(i["L0_mix_" + k]) for k in ("Wq", "Wm", "W1", "W2"))
    row = lambda *v: a(np.stack([np.asarray(x).reshape(-1) for x in v]).reshape(1, -1))
    f["m0_norms"] = row(i["L0_mix_g1"], i["L0_mix_b1"], i["L0_mix_g2"], i["L0_mix_b2"])
    experts = lambda w: np.asarray(w).transpose(1, 0, 2).reshape(w.shape[1], -1)
    f["f0_w1"] = a(np.concatenate([i["L0_ffn_sW1"], experts(i["L0_ffn_eW1"])], 1))
    f["f0_b1"] = a(np.concatenate([np.asarray(i["L0_ffn_sb1"]), np.asarray(i["L0_ffn_eb1"]).reshape(-1)]).reshape(6, P).T)
    f["f0_w2"], f["f0_e2"] = a(i["L0_ffn_sW2"]), a(experts(i["L0_ffn_eW2"]))
    f["f0_b2"] = a(np.asarray(i["L0_ffn_sb2"]).reshape(P, 1))
    f["f0_eb2"] = a(np.asarray(i["L0_ffn_eb2"]).T)
    f["f0_w3"], f["f0_e3"] = a(i["L0_ffn_sW3"]), a(np.asarray(i["L0_ffn_eW3"]).transpose(1, 0, 2).reshape(64, -1))
    f["f0_b3"] = a(np.asarray(i["L0_ffn_sb3"]).reshape(1, D))
    f["f0_eb3"] = a(np.asarray(i["L0_ffn_eb3"]).reshape(1, -1))
    f["f0_gw"], f["f0_gb"] = a(i["L0_ffn_gW"]), a(np.asarray(i["L0_ffn_gb"]).reshape(1, -1))
    g = {k[7:]: np.asarray(v) for k, v in i.items() if k.startswith("L1_gnn_")}
    f["g1_w"], f["g1_wT"] = a(g["gat_w"].T), a(g["gat_w"])
    f["g1_al"] = diagonal(g["gat_a_src"], g["gat_a_tgt"])
    f["g1_rows"] = row(g["gat_b"], g["ln_local_g"], g["ln_local_b"], g["ln_global_g"], g["ln_global_b"], g["ln2_g"],
                       g["ln2_b"], g["ff2_b"])
    f["s_in"], f["s_x"], f["s_dt"], f["s_out"] = (a(g[k].T) for k in ("in_proj_w", "x_proj_w", "dt_proj_w", "out_proj_w"))
    cols = lambda v: np.asarray(v).reshape(2, P, -1).transpose(1, 0, 2)
    f["s_cols"] = a(np.concatenate([cols(g[k]) for k in ("conv_w", "conv_b", "dt_proj_b", "D_param", "A_log")], 2).reshape(P, -1))
    f["g1_gates"] = a(np.concatenate([g["wl"].T, g["wg"].T], 0))
    f["g1_ff1"], f["g1_ff2"] = a(g["ff1_w"].T), a(g["ff2_w"].T)
    f["g1_ff1b"] = a(g["ff1_b"].reshape(4, P).T)
    m = {k[7:]: np.asarray(v) for k, v in i.items() if k.startswith("L1_mix_")}
    f["m1_wq"] = a(m["W_qk"][0])
    f["m1_wkv"] = a(np.concatenate([m["W_qk"][1], m["W_v"]], 1))
    f["m1_bkv"] = a(np.concatenate([m["b_qk"][1], m["b_v"]]).reshape(1, -1))
    f["m1_cols"] = a(np.stack([m["b_qk"][0], m["gamma"], m["beta"]], 1).reshape(2, P, 3).transpose(1, 0, 2).reshape(P, 6))
    f["e_gw"], f["e_gb"] = a(i["L1_ffn_Wg"]), a(np.asarray(i["L1_ffn_bg"]).reshape(1, -1))
    f["e_w1"] = a(i["L1_ffn_W1"]).reshape(8 * D, 512)
    f["e_b1"] = a(np.asarray(i["L1_ffn_b1"]).reshape(8 * 4, P).T)
    f["e_w2"] = a(i["L1_ffn_W2"]).reshape(8 * 512, D)
    f["e_b2"] = a(i["L1_ffn_b2"])
    return f


def kernel(**inputs):
    import concourse.bacc as _bacc
    from concourse.bass_utils import run_bass_kernel_spmd as _run

    nc = _bacc.Bacc("TRN2", target_bir_lowering=False, num_devices=1)
    arrays = layout(inputs)
    ins = {k: nc.dram_tensor(f"in_{k}", v.shape, mybir.dt.from_np(v.dtype), kind="ExternalInput").ap() for k, v in arrays.items()}
    out = nc.dram_tensor("out_x", (N, D), F32, kind="ExternalOutput").ap()
    build(nc, ins, out)
    got = _run(nc, [{f"in_{k}": v for k, v in arrays.items()}], core_ids=[0])
    return got.results[0]["out_x"]
```
